# Optimizing a Trainium2 kernel written in Bass

```python
import numpy as np
import jax
import jax.numpy as jnp

def _softmax(x, axis=-1):
    return jax.nn.softmax(x, axis=axis)

def _gelu(x):
    return jax.nn.gelu(x, approximate=True)

def _silu(x):
    return jax.nn.silu(x)

def _sigmoid(x):
    return jax.nn.sigmoid(x)

def _layernorm(x, axis=-1, eps=1e-05):
    m = jnp.mean(x, axis=axis, keepdims=True)
    v = jnp.var(x, axis=axis, keepdims=True)
    return (x - m) / jnp.sqrt(v + eps)

def _scatter_add(tgt, idx, src, axis=0):
    return tgt.at[idx].add(src)

def _segment_sum(src, seg, n):
    return jax.ops.segment_sum(src, seg, n)
kernel_name = 'mk_vit_tower_cls_d2_tok_img1024_r4_ed6dc7'

def setup_inputs(seed: int=0):
    np.random.seed(seed)
    _w = jnp.asarray

    def _rec_inputs():
        import jax
        import jax.numpy as jnp
        _rk = jax.random.key(seed)
        x = -0.00016672 + 0.999947 * jax.random.normal(jax.random.fold_in(_rk, 1), (64, 3, 96, 96), jnp.float32)
        cls_tok = 0.02 * jax.random.normal(jax.random.fold_in(_rk, 5), (1, 1, 256), jnp.float32)
        return (x, cls_tok)
    x, cls_tok = _rec_inputs()

    def _L0_tok_setup():
        import jax, jax.numpy as jnp
        import numpy as np
        B, C, H, W = (64, 3, 96, 96)
        P = 16
        NP = H // P * (W // P)
        PD = C * P * P
        ED = 256
        NCLS = 1

        def _layernorm(x, g, b, eps=1e-05):
            mu = jnp.mean(x, axis=-1, keepdims=True)
            var = jnp.mean(jnp.square(x - mu), axis=-1, keepdims=True)
            return (x - mu) * jax.lax.rsqrt(var + eps) * g + b
        key = jax.random.key(seed)
        ks = jax.random.split(key, 8)
        x = jax.random.normal(ks[0], (B, C, H, W), dtype=jnp.float32)
        ln1_g = jnp.ones((PD,), jnp.float32)
        ln1_b = jnp.zeros((PD,), jnp.float32)
        W_proj = jax.random.normal(ks[1], (PD, ED), jnp.float32) / np.sqrt(PD)
        b_proj = jnp.zeros((ED,), jnp.float32)
        ln2_g = jnp.ones((ED,), jnp.float32)
        ln2_b = jnp.zeros((ED,), jnp.float32)
        cls_token = jax.random.normal(ks[2], (1, NCLS, ED), jnp.float32)
        pos_emb = jax.random.normal(ks[3], (1, NP + NCLS, ED), jnp.float32)
        return {'x': x, 'ln1_g': ln1_g, 'ln1_b': ln1_b, 'W_proj': W_proj, 'b_proj': b_proj, 'ln2_g': ln2_g, 'ln2_b': ln2_b, 'cls_token': cls_token, 'pos_emb': pos_emb}
    _L0_tok_all = _L0_tok_setup()
    _L0_tok_in = {k: v for k, v in _L0_tok_all.items() if k in ('ln1_g', 'ln1_b', 'W_proj', 'b_proj', 'ln2_g', 'ln2_b', 'cls_token', 'pos_emb')}
    del _L0_tok_all

    def _L0_attn_setup():
        import jax, jax.numpy as jnp
        import numpy as np
        import math
        B, N, E, D = (4, 2048, 256, 64)
        key = jax.random.key(seed)
        kx, kq, kk, kv, ko = jax.random.split(key, 5)
        x = jax.random.normal(kx, (B, N, E), dtype=jnp.float32)
        wq = jnp.sign(jax.random.normal(kq, (D, E), dtype=jnp.float32)) / math.sqrt(E)
        wk = jnp.sign(jax.random.normal(kk, (D, E), dtype=jnp.float32)) / math.sqrt(E)
        wv = jnp.sign(jax.random.normal(kv, (D, E), dtype=jnp.float32)) / math.sqrt(E)
        wo = jnp.sign(jax.random.normal(ko, (E, D), dtype=jnp.float32)) / math.sqrt(D)
        return {'x': x, 'wq': wq, 'wk': wk, 'wv': wv, 'wo': wo}
    _L0_attn_all = _L0_attn_setup()
    _L0_attn_in = {k: v for k, v in _L0_attn_all.items() if k in ('wq', 'wk', 'wv', 'wo')}
    del _L0_attn_all

    def _L0_ffn_setup():
        import jax, jax.numpy as jnp
        import numpy as np
        B, P, D, D_MLP, E, K = (2, 512, 256, 1024, 8, 2)
        key = jax.random.key(seed)
        k_x, k_g, k_in, k_out = jax.random.split(key, 4)
        s_in = 1.0 / np.sqrt(D).astype(np.float32)
        s_out = 1.0 / np.sqrt(D_MLP).astype(np.float32)
        return {'x': jax.random.normal(k_x, (B, P, D), dtype=jnp.float32), 'W_gate': jax.random.normal(k_g, (D, E), dtype=jnp.float32) * s_in, 'W_in': jax.random.normal(k_in, (E, D, D_MLP), dtype=jnp.float32) * s_in, 'b_in': jnp.zeros((E, D_MLP), dtype=jnp.float32), 'W_out': jax.random.normal(k_out, (E, D_MLP, D), dtype=jnp.float32) * s_out, 'b_out': jnp.zeros((E, D), dtype=jnp.float32)}
    _L0_ffn_all = _L0_ffn_setup()
    _L0_ffn_in = {k: v for k, v in _L0_ffn_all.items() if k in ('W_gate', 'W_in', 'b_in', 'W_out', 'b_out')}
    del _L0_ffn_all

    def _L1_attn_setup():
        import jax, jax.numpy as jnp
        import numpy as np
        H, HEADDIM, HIDDEN, DSTATE, G, K, NL = (32, 64, 256, 128, 1, 4, 15)
        DIM = H * HEADDIM
        CONV_DIM = DIM + 2 * G * DSTATE
        PROJ = DIM + CONV_DIM + H * (NL + 1)
        EPS = 1e-05

        def fenwick_level_map(T, num_levels):
            t = np.arange(T)[:, None]
            s = np.arange(T)[None, :]
            lvl = np.zeros((T, T), np.int32)
            for k in range(num_levels - 1):
                lo = t >> k + 1 << k + 1
                hi = t >> k << k
                m = (t >> k & 1 == 1) & (s >= lo) & (s < hi)
                lvl = np.where(m, k + 1, lvl)
            return jnp.asarray(lvl)
        key = jax.random.key(seed)
        ks = jax.random.split(key, 6)
        B, T = (1, 256)
        return {'hidden_states': jax.random.normal(ks[0], (B, T, HIDDEN), jnp.float32), 'in_proj_w': jax.random.normal(ks[1], (PROJ, HIDDEN), jnp.float32) / np.sqrt(HIDDEN).astype(np.float32), 'in_proj_b': jax.random.normal(ks[2], (PROJ,), jnp.float32) * 0.02, 'conv_w': jax.random.normal(ks[3], (CONV_DIM, K), jnp.float32) / np.sqrt(K).astype(np.float32), 'dt_bias': jnp.ones((H,), jnp.float32), 'A_log': jnp.log(jnp.arange(1, H + 1, dtype=jnp.float32)), 'L': jnp.ones((H, NL), jnp.float32), 'D': jnp.ones((H,), jnp.float32), 'norm_w': jnp.ones((DIM,), jnp.float32), 'out_proj_w': jax.random.normal(ks[4], (HIDDEN, DIM), jnp.float32) / np.sqrt(DIM).astype(np.float32), 'out_proj_b': jnp.zeros((HIDDEN,), jnp.float32)}
    _L1_attn_all = _L1_attn_setup()
    _L1_attn_in = {k: v for k, v in _L1_attn_all.items() if k in ('in_proj_w', 'in_proj_b', 'conv_w', 'dt_bias', 'A_log', 'L', 'D', 'norm_w', 'out_proj_w', 'out_proj_b')}
    del _L1_attn_all

    def _L1_ffn_setup():
        import jax, jax.numpy as jnp
        import numpy as np
        HIDDEN = 256
        N_EXPERTS = 8
        TOP_K = 2
        INTER = 352
        N_SHARED = 2
        SCALE = 1.0
        key = jax.random.key(seed)
        ks = jax.random.split(key, 9)
        s_h = 1.0 / np.sqrt(HIDDEN)
        s_i = 1.0 / np.sqrt(INTER)
        x = jax.random.normal(ks[0], (2, 512, HIDDEN), dtype=jnp.float32)
        gate_w = jax.random.uniform(ks[1], (N_EXPERTS, HIDDEN), jnp.float32, -s_h, s_h)
        wg = jax.random.uniform(ks[2], (N_EXPERTS, HIDDEN, INTER), jnp.float32, -s_h, s_h)
        wu = jax.random.uniform(ks[3], (N_EXPERTS, HIDDEN, INTER), jnp.float32, -s_h, s_h)
        wd = jax.random.uniform(ks[4], (N_EXPERTS, INTER, HIDDEN), jnp.float32, -s_i, s_i)
        si = INTER * N_SHARED
        s_si = 1.0 / np.sqrt(si)
        swg = jax.random.uniform(ks[5], (HIDDEN, si), jnp.float32, -s_h, s_h)
        swu = jax.random.uniform(ks[6], (HIDDEN, si), jnp.float32, -s_h, s_h)
        swd = jax.random.uniform(ks[7], (si, HIDDEN), jnp.float32, -s_si, s_si)
        return {'x': x, 'gate_w': gate_w, 'wg': wg, 'wu': wu, 'wd': wd, 'swg': swg, 'swu': swu, 'swd': swd}
    _L1_ffn_all = _L1_ffn_setup()
    _L1_ffn_in = {k: v for k, v in _L1_ffn_all.items() if k in ('gate_w', 'wg', 'wu', 'wd', 'swg', 'swu', 'swd')}
    del _L1_ffn_all
    return {'x': x, 'cls_tok': cls_tok, 'L0_tok_ln1_g': _L0_tok_in['ln1_g'], 'L0_tok_ln1_b': _L0_tok_in['ln1_b'], 'L0_tok_W_proj': _L0_tok_in['W_proj'], 'L0_tok_b_proj': _L0_tok_in['b_proj'], 'L0_tok_ln2_g': _L0_tok_in['ln2_g'], 'L0_tok_ln2_b': _L0_tok_in['ln2_b'], 'L0_tok_cls_token': _L0_tok_in['cls_token'], 'L0_tok_pos_emb': _L0_tok_in['pos_emb'], 'L0_attn_wq': _L0_attn_in['wq'], 'L0_attn_wk': _L0_attn_in['wk'], 'L0_attn_wv': _L0_attn_in['wv'], 'L0_attn_wo': _L0_attn_in['wo'], 'L0_ffn_W_gate': _L0_ffn_in['W_gate'], 'L0_ffn_W_in': _L0_ffn_in['W_in'], 'L0_ffn_b_in': _L0_ffn_in['b_in'], 'L0_ffn_W_out': _L0_ffn_in['W_out'], 'L0_ffn_b_out': _L0_ffn_in['b_out'], 'L1_attn_in_proj_w': _L1_attn_in['in_proj_w'], 'L1_attn_in_proj_b': _L1_attn_in['in_proj_b'], 'L1_attn_conv_w': _L1_attn_in['conv_w'], 'L1_attn_dt_bias': _L1_attn_in['dt_bias'], 'L1_attn_A_log': _L1_attn_in['A_log'], 'L1_attn_L': _L1_attn_in['L'], 'L1_attn_D': _L1_attn_in['D'], 'L1_attn_norm_w': _L1_attn_in['norm_w'], 'L1_attn_out_proj_w': _L1_attn_in['out_proj_w'], 'L1_attn_out_proj_b': _L1_attn_in['out_proj_b'], 'L1_ffn_gate_w': _L1_ffn_in['gate_w'], 'L1_ffn_wg': _L1_ffn_in['wg'], 'L1_ffn_wu': _L1_ffn_in['wu'], 'L1_ffn_wd': _L1_ffn_in['wd'], 'L1_ffn_swg': _L1_ffn_in['swg'], 'L1_ffn_swu': _L1_ffn_in['swu'], 'L1_ffn_swd': _L1_ffn_in['swd']}

def reference(x, cls_tok, L0_tok_ln1_g, L0_tok_ln1_b, L0_tok_W_proj, L0_tok_b_proj, L0_tok_ln2_g, L0_tok_ln2_b, L0_tok_cls_token, L0_tok_pos_emb, L0_attn_wq, L0_attn_wk, L0_attn_wv, L0_attn_wo, L0_ffn_W_gate, L0_ffn_W_in, L0_ffn_b_in, L0_ffn_W_out, L0_ffn_b_out, L1_attn_in_proj_w, L1_attn_in_proj_b, L1_attn_conv_w, L1_attn_dt_bias, L1_attn_A_log, L1_attn_L, L1_attn_D, L1_attn_norm_w, L1_attn_out_proj_w, L1_attn_out_proj_b, L1_ffn_gate_w, L1_ffn_wg, L1_ffn_wu, L1_ffn_wd, L1_ffn_swg, L1_ffn_swu, L1_ffn_swd):
    import jax
    import jax.numpy as jnp

    def _L0_tok_ref(x, ln1_g, ln1_b, W_proj, b_proj, ln2_g, ln2_b, cls_token, pos_emb):
        import jax, jax.numpy as jnp
        import numpy as np
        B, C, H, W = (64, 3, 96, 96)
        P = 16
        NP = H // P * (W // P)
        PD = C * P * P
        ED = 256
        NCLS = 1

        def _layernorm(x, g, b, eps=1e-05):
            mu = jnp.mean(x, axis=-1, keepdims=True)
            var = jnp.mean(jnp.square(x - mu), axis=-1, keepdims=True)
            return (x - mu) * jax.lax.rsqrt(var + eps) * g + b
        b = x.shape[0]
        h, w = (H // P, W // P)
        patches = x.reshape(b, C, h, P, w, P)
        patches = patches.transpose(0, 2, 4, 3, 5, 1).reshape(b, h * w, P * P * C)
        z = _layernorm(patches, ln1_g, ln1_b)
        z = jnp.einsum('bnp,pe->bne', z, W_proj) + b_proj
        z = _layernorm(z, ln2_g, ln2_b)
        cls = jnp.broadcast_to(cls_token, (b, NCLS, ED))
        z = jnp.concatenate([cls, z], axis=1)
        z = z + pos_emb
        return z

    def _L0_attn_ref(x, wq, wk, wv, wo):
        import jax, jax.numpy as jnp
        import numpy as np
        import math
        B, N, E, D = (4, 2048, 256, 64)
        Q = jnp.einsum('bne,de->bnd', x, wq)
        K = jnp.einsum('bne,de->bnd', x, wk)
        V = jnp.einsum('bne,de->bnd', x, wv)
        energy = jnp.einsum('bnd,bne->bde', K, V)
        context = jnp.einsum('bnd,bde->bne', Q, energy)
        context = context * jnp.asarray(math.sqrt(3.0 / D), dtype=context.dtype)
        out = jnp.einsum('bnd,ed->bne', context, wo)
        return out

    def _L0_ffn_ref(x, W_gate, W_in, b_in, W_out, b_out):
        import jax, jax.numpy as jnp
        import numpy as np
        B, P, D, D_MLP, E, K = (2, 512, 256, 1024, 8, 2)
        gate_logits = jnp.einsum('bpd,de->bpe', x, W_gate)
        top_w, top_idx = jax.lax.top_k(gate_logits, K)
        top_w = jax.nn.softmax(top_w, axis=-1)
        combine = jnp.einsum('bpke,bpk->bpe', jax.nn.one_hot(top_idx, E, dtype=x.dtype), top_w)
        out = jnp.zeros_like(x)
        for e in range(E):
            h = jax.nn.gelu(jnp.einsum('bpd,dm->bpm', x, W_in[e]) + b_in[e], approximate=False)
            y = jnp.einsum('bpm,md->bpd', h, W_out[e]) + b_out[e]
            out = out + combine[..., e, None] * y
        return out

    def _L1_attn_ref(hidden_states, in_proj_w, in_proj_b, conv_w, dt_bias, A_log, L, D, norm_w, out_proj_w, out_proj_b):
        import jax, jax.numpy as jnp
        import numpy as np
        H, HEADDIM, HIDDEN, DSTATE, G, K, NL = (32, 64, 256, 128, 1, 4, 15)
        DIM = H * HEADDIM
        CONV_DIM = DIM + 2 * G * DSTATE
        PROJ = DIM + CONV_DIM + H * (NL + 1)
        EPS = 1e-05

        def fenwick_level_map(T, num_levels):
            t = np.arange(T)[:, None]
            s = np.arange(T)[None, :]
            lvl = np.zeros((T, T), np.int32)
            for k in range(num_levels - 1):
                lo = t >> k + 1 << k + 1
                hi = t >> k << k
                m = (t >> k & 1 == 1) & (s >= lo) & (s < hi)
                lvl = np.where(m, k + 1, lvl)
            return jnp.asarray(lvl)
        B, T, _ = hidden_states.shape
        zxbcdtdl = hidden_states @ in_proj_w.T + in_proj_b
        z = zxbcdtdl[..., :DIM]
        xBC = zxbcdtdl[..., DIM:DIM + CONV_DIM]
        dt = zxbcdtdl[..., DIM + CONV_DIM:DIM + CONV_DIM + H]
        dl = zxbcdtdl[..., DIM + CONV_DIM + H:].reshape(B, T, H, NL)
        xp = jnp.pad(xBC, ((0, 0), (K - 1, 0), (0, 0)))
        xBC = sum((xp[:, i:i + T, :] * conv_w[:, i] for i in range(K)))
        xBC = jax.nn.silu(xBC)
        x = xBC[..., :DIM].reshape(B, T, H, HEADDIM)
        Bm = xBC[..., DIM:DIM + G * DSTATE].reshape(B, T, G, DSTATE)
        Cm = xBC[..., DIM + G * DSTATE:].reshape(B, T, G, DSTATE)
        dt = jax.nn.softplus(dt + dt_bias)
        D_res = x * D[None, None, :, None]
        v = x * dt[..., None]
        g = -jnp.exp(A_log)[None, None, :] * dt
        lam = jax.nn.softplus(L[None, None] * dl)
        gc = jnp.cumsum(g, axis=1).transpose(0, 2, 1)
        causal = jnp.tril(jnp.ones((T, T), bool))
        diff = jnp.where(causal, gc[:, :, :, None] - gc[:, :, None, :], -jnp.inf)
        decay = jnp.exp(diff)
        lvl = fenwick_level_map(T, NL)
        lam_ts = jnp.take_along_axis(lam.transpose(0, 2, 1, 3), lvl[None, None], axis=3)
        qk = jnp.einsum('btgn,bsgn->bgts', Cm, Bm)
        qk = jnp.repeat(qk, H // G, axis=1)
        att = qk * decay * lam_ts
        y = jnp.einsum('bhts,bshp->bthp', att, v) + D_res
        y = y.reshape(B, T, DIM)
        yz = y * jax.nn.silu(z)
        y = yz * jax.lax.rsqrt(jnp.mean(yz * yz, axis=-1, keepdims=True) + EPS) * norm_w
        return y @ out_proj_w.T + out_proj_b

    def _L1_ffn_ref(x, gate_w, wg, wu, wd, swg, swu, swd):
        import jax, jax.numpy as jnp
        import numpy as np
        HIDDEN = 256
        N_EXPERTS = 8
        TOP_K = 2
        INTER = 352
        N_SHARED = 2
        SCALE = 1.0
        B, S, H = x.shape
        xf = x.reshape(-1, H)
        T = xf.shape[0]
        logits = xf.astype(jnp.float32) @ gate_w.astype(jnp.float32).T
        scores = jax.nn.softmax(logits, axis=-1)
        topw, topi = jax.lax.top_k(scores, TOP_K)
        denom = topw.sum(axis=-1, keepdims=True) + 1e-20
        topw = topw / denom * SCALE
        wdense = jnp.zeros((T, N_EXPERTS), jnp.float32).at[jnp.arange(T)[:, None], topi].set(topw)
        hg = jnp.einsum('th,ehi->eti', xf, wg)
        hu = jnp.einsum('th,ehi->eti', xf, wu)
        eo = jnp.einsum('eti,eih->eth', jax.nn.silu(hg) * hu, wd)
        y = jnp.einsum('te,eth->th', wdense, eo)
        shared = jax.nn.silu(xf @ swg) * (xf @ swu) @ swd
        return (y + shared).reshape(B, S, H)
    h = _L0_tok_ref(x, L0_tok_ln1_g, L0_tok_ln1_b, L0_tok_W_proj, L0_tok_b_proj, L0_tok_ln2_g, L0_tok_ln2_b, L0_tok_cls_token, L0_tok_pos_emb)
    h = jnp.concatenate([jnp.broadcast_to(cls_tok, (h.shape[0], 1, h.shape[2])), h], axis=1)
    h = h + _L0_attn_ref(_layernorm(h, axis=-1), L0_attn_wq, L0_attn_wk, L0_attn_wv, L0_attn_wo)
    h = h + _L0_ffn_ref(_layernorm(h, axis=-1), L0_ffn_W_gate, L0_ffn_W_in, L0_ffn_b_in, L0_ffn_W_out, L0_ffn_b_out)
    h = h + _L1_attn_ref(_layernorm(h, axis=-1), L1_attn_in_proj_w, L1_attn_in_proj_b, L1_attn_conv_w, L1_attn_dt_bias, L1_attn_A_log, L1_attn_L, L1_attn_D, L1_attn_norm_w, L1_attn_out_proj_w, L1_attn_out_proj_b)
    h = h + _L1_ffn_ref(_layernorm(h, axis=-1), L1_ffn_gate_w, L1_ffn_wg, L1_ffn_wu, L1_ffn_wd, L1_ffn_swg, L1_ffn_swu, L1_ffn_swd)
    return h

_drawn_inputs = setup_inputs


def setup_inputs(seed=0):
    import zlib

    import numpy as np

    out = dict(_drawn_inputs(seed))
    spreads = {'L0_tok_ln1_g': (1.0, 0.2),
     'L0_tok_ln1_b': (0.0, 0.1),
     'L0_tok_b_proj': (0.0, 0.1),
     'L0_tok_ln2_g': (1.0, 0.2),
     'L0_tok_ln2_b': (0.0, 0.1),
     'L0_ffn_b_in': (0.0, 0.8),
     'L0_ffn_b_out': (0.0, 0.8),
     'L1_attn_dt_bias': (1.0, 0.6),
     'L1_attn_L': (1.0, 0.6),
     'L1_attn_D': (1.0, 0.6),
     'L1_attn_norm_w': (1.0, 0.6),
     'L1_attn_out_proj_b': (0.0, 0.8)}
    factors = {'L1_attn_in_proj_b': 8.0,
     'L1_attn_A_log': 6.957,
     'L1_ffn_gate_w': 8.0,
     'L1_ffn_wg': 8.0,
     'L1_ffn_wu': 8.0,
     'L1_ffn_wd': 8.0,
     'L1_ffn_swg': 8.0,
     'L1_ffn_swu': 8.0,
     'L1_ffn_swd': 8.0}
    for name, (base, spread) in spreads.items():
        noise = np.random.default_rng([zlib.crc32(name.encode()), seed]).standard_normal(out[name].shape)
        drawn = base * np.exp(spread * noise) if base else spread * noise
        out[name] = jnp.asarray(drawn.astype(out[name].dtype))
    for name, factor in factors.items():
        out[name] = (out[name] * factor).astype(out[name].dtype)
    return out
```

```python
import concourse.bass as bass
from concourse import mybir
from contextlib import ExitStack, contextmanager

F32 = mybir.dt.float32
F32R = mybir.dt.float32r
U32 = mybir.dt.uint32
I32 = mybir.dt.int32
ALU = mybir.AluOpType
ACT = mybir.ActivationFunctionType
AX = mybir.AxisListType

BATCH = 64
PATCHES = 36
SEQ = PATCHES + 2
E = 256
KE = E // 128
PD = 3 * 16 * 16
KP = PD // 128
SPT = 3
R = SPT * SEQ
NT = -(-BATCH // SPT)
TOK = NT * R
PAIRS = NT // 2
G2 = 2 * R
LN_EPS = 1e-5
assert NT % 2 == 0 and R <= 128


class Chain:

    def __init__(self, eng, sem, spare=None):
        self.eng, self.sem, self.n, self.base = eng, sem, 0, 0
        self.spare = spare

    def __call__(self, ins, apart=False):
        self.n += 1
        ins.then_inc(self.sem, 1)
        self.eng.wait_ge(self.sem, self.base + self.n)
        if apart:
            self.eng.memset(self.spare[:, :], 0.0)

    def enter(self, turn, per_turn):
        self.start = self.n
        self.base = turn * per_turn

    def leave(self, turns, per_turn):
        assert self.n - self.start == per_turn, (self.n - self.start, per_turn)
        self.base = 0
        self.n = self.start + turns * per_turn


def moments(v, step, x, stats, mv):
    n = x.shape[-1]
    chunk = n // 2 if n > 512 else n
    for c in range(n // chunk):
        ins = v.bn_stats(stats[:, c, :], x[:, c * chunk:(c + 1) * chunk])
    step(ins, apart=True)
    return v.bn_aggr(mv, stats[:, 0:n // chunk, :].rearrange("p c s -> p (c s)"))


def normalize(v, out, x, mv, rstd):
    return v.tensor_scalar(out, x, mv[:, 0:1], rstd, ALU.subtract, ALU.mult)


class Space:

    def __init__(self, nc):
        self.nc, self.sems = nc, []

    @contextmanager
    def part(self):
        yield
        self.nc.clear_and_free_semaphores(self.sems)
        self.nc.all_engine_barrier()
        self.sems = []

    def sb(self, stack, name, shape, dt=F32):
        return stack.enter_context(self.nc.sbuf_tensor(name, shape, dt))

    def ps(self, stack, name, shape):
        return stack.enter_context(self.nc.psum_tensor(name, shape, F32))

    def sem(self, name):
        self.sems.append(self.nc.alloc_semaphore(name=name))
        return self.sems[-1]


def tokenize(nc, space, io, hidden, to_clear, ident, ones_row, eps, spare):
    with ExitStack() as stack:
        def sb(name, shape, dt=F32):
            return space.sb(stack, name, shape, dt)

        patches = sb("tk_patches", [R, 2, PD])
        normed = sb("tk_normed", [R, 2, PD])
        normedT = sb("tk_normedT", [128, 2, KP, R])
        proj = sb("tk_proj", [128, KP, E])
        proj_bias = sb("tk_proj_bias", [1, E])
        ln1_g = sb("tk_ln1_g", [128, KP])
        ln1_b = sb("tk_ln1_b", [128, KP])
        gain = sb("tk_gain", [R, E])
        shift = sb("tk_shift", [R, E])
        place = sb("tk_place", [R, E])
        stats = sb("tk_stats", [R, 2, 2, 6])
        mv = sb("tk_mv", [R, 2, 2])
        std = sb("tk_std", [R, 2])
        rstd = sb("tk_rstd", [R, 2])
        mv2 = sb("tk_mv2", [R, 2, 2])
        std2 = sb("tk_std2", [R, 2])
        rstd2 = sb("tk_rstd2", [R, 2])
        z_normed = sb("tk_z_normed", [R, 2, E])
        z_gained = sb("tk_z_gained", [R, 2, E])
        zeros = sb("tk_zeros", [128, 2048])
        turned = [space.ps(stack, f"tk_turned{i}", [128, 2, 512]) for i in range(2)]
        z = [space.ps(stack, f"tk_z{i}", [128, 512]) for i in range(2)]

        const_loaded = space.sem("tk_const_loaded")
        gain_cleared = space.sem("tk_gain_cleared")
        ident_zeroed = space.sem("tk_ident_zeroed")
        ident_ready = space.sem("tk_ident_ready")
        place_ready = space.sem("tk_place_ready")
        patches_loaded = [space.sem(f"tk_patches_loaded{i}") for i in range(2)]
        normed_ready = space.sem("tk_normed_ready")
        turned_ready = space.sem("tk_turned_ready")
        normedT_by_act = space.sem("tk_normedT_by_act")
        normedT_by_vec = space.sem("tk_normedT_by_vec")
        z_ready = space.sem("tk_z_ready")
        z_normed_ready = space.sem("tk_z_normed_ready")
        vec_step = space.sem("tk_vec_step")
        moments_ready = space.sem("tk_moments_ready")
        std_ready = space.sem("tk_std_ready")
        gained_ready = space.sem("tk_gained_ready")
        zeros_ready = space.sem("tk_zeros_ready")
        cleared = space.sem("tk_cleared")
        all_const = 16 * (4 + 5 * SPT)

        block = stack.enter_context(nc.Block())

        @block.sync
        def _(sp):
            with sp.Fori(0, PAIRS) as i:
                for half in range(2):
                    sp.wait_ge(normed_ready, 2 * i + half + 1)
                    sp.dma_start(patches[:, half, :], io["patches"][2 * i + half]).then_inc(patches_loaded[half], 16)

        @block.scalar
        def _(act):
            act.dma_start(proj[:, :, :], io["proj"].rearrange("(k p) n -> p k n", p=128)).then_inc(const_loaded, 16)
            act.dma_start(ln1_g[:, :], io["ln1_g"]).then_inc(const_loaded, 16)
            act.dma_start(ln1_b[:, :], io["ln1_b"]).then_inc(const_loaded, 16)
            act.dma_start(proj_bias[:, :], io["proj_bias"]).then_inc(const_loaded, 16)
            act.wait_ge(gain_cleared, 2)
            for s in range(SPT):
                first, rest = s * SEQ, (s + 1) * SEQ
                act.dma_start(gain[first + 2:rest, :], io["ln2_g"].partition_broadcast(PATCHES)).then_inc(const_loaded, 16)
                act.dma_start(shift[first + 2:rest, :], io["ln2_b"].partition_broadcast(PATCHES)).then_inc(const_loaded, 16)
                act.dma_start(shift[first + 1:first + 2, :], io["inner_cls"]).then_inc(const_loaded, 16)
                act.dma_start(place[first + 1:rest, :], io["positions"]).then_inc(const_loaded, 16)
                act.dma_start(place[first:first + 1, :], io["outer_cls"]).then_inc(const_loaded, 16)
            clears = 0
            act.wait_ge(zeros_ready, 1)
            for rows in to_clear:
                view = rows.rearrange("(p s) e -> p (s e)", p=128)
                cols = zeros.shape[1]
                assert view.shape[1] % cols == 0
                for c in range(0, view.shape[1], cols):
                    act.dma_start(view[:, c:c + cols], zeros[:, :]).then_inc(cleared, 16)
                    clears += 1
            act.wait_ge(const_loaded, all_const)
            act.wait_ge(ident_ready, 3)
            with act.Fori(0, PAIRS) as i:
                act.wait_ge(moments_ready, 4 * i + 2)
                act.activation(std[:, :], mv[:, :, 1], ACT.Sqrt, bias=eps[:, :]).then_inc(std_ready, 1)
                for half in range(2):
                    act.wait_ge(turned_ready, 2 * i + half + 1)
                    for k in range(KP // 2, KP):
                        ins = act.activation(normedT[:, half, k, :], turned[half][:, 1, (k - KP // 2) * R:(k - KP // 2 + 1) * R],
                                             ACT.Identity, bias=ln1_b[:, k:k + 1], scale=ln1_g[:, k:k + 1])
                    ins.then_inc(normedT_by_act, 1)
                act.wait_ge(moments_ready, 4 * i + 4)
                act.activation(std2[:, :], mv2[:, :, 1], ACT.Sqrt, bias=eps[:, :]).then_inc(std_ready, 1)
            act.wait_ge(cleared, 16 * clears)

        @block.gpsimd
        def _(pool):
            pool.memset(gain[:, :], 0.0).then_inc(gain_cleared, 1)
            pool.memset(shift[:, :], 0.0).then_inc(gain_cleared, 1)
            pool.memset(eps[:, :], LN_EPS).then_inc(ident_ready, 1)
            pool.memset(ones_row[:, :], 1.0).then_inc(ident_ready, 1)
            pool.memset(ident[:, :], 0.0).then_inc(ident_zeroed, 1)
            pool.wait_ge(ident_zeroed, 1)
            pool.affine_select(out=ident[:, :], in_=ident[:, :], compare_op=ALU.not_equal, fill=1.0, base=0,
                               pattern=[[-1, 128]], channel_multiplier=1).then_inc(ident_ready, 1)
            pool.memset(zeros[:, :], 0.0).then_inc(zeros_ready, 1)
            pool.wait_ge(const_loaded, all_const)
            pool.tensor_tensor(place[:, :], place[:, :], shift[:, :], ALU.add).then_inc(place_ready, 1)
            pool.wait_ge(place_ready, 1)
            pool.sem_inc(gained_ready, 2)
            with pool.Fori(0, PAIRS) as i:
                for half in range(2):
                    pool.wait_ge(z_normed_ready, 2 * i + half + 1)
                    pool.tensor_tensor(z_gained[:, half, :], z_normed[:, half, :], gain[:, :], ALU.mult).then_inc(gained_ready, 1)
                    pool.wait_ge(gained_ready, 2 * i + half + 3)
                    pool.tensor_tensor(hidden[:, 2 * i + half, :], z_gained[:, half, :], place[:, :], ALU.add)

        @block.vector
        def _(v):
            step = Chain(v, vec_step, spare)
            v.sem_inc(normed_ready, 2)
            v.wait_ge(const_loaded, all_const)
            per_turn = 2 * 2 + 2
            with v.Fori(0, PAIRS) as i:
                step.enter(i, per_turn)
                for half in range(2):
                    v.wait_ge(patches_loaded[half], 16 * i + 16)
                    moments(v, step, patches[:, half, :], stats[:, half], mv[:, half, :]).then_inc(moments_ready, 1)
                v.wait_ge(std_ready, 2 * i + 1)
                step(v.reciprocal(rstd[:, :], std[:, :]))
                for half in range(2):
                    normalize(v, normed[:, half, :], patches[:, half, :], mv[:, half, :], rstd[:, half:half + 1]).then_inc(normed_ready, 1)
                for half in range(2):
                    v.wait_ge(turned_ready, 2 * i + half + 1)
                    for k in range(KP // 2):
                        ins = v.tensor_scalar(normedT[:, half, k, :], turned[half][:, 0, k * R:(k + 1) * R],
                                              ln1_g[:, k:k + 1], ln1_b[:, k:k + 1], ALU.mult, ALU.add)
                    ins.then_inc(normedT_by_vec, 1)
                for half in range(2):
                    v.wait_ge(z_ready, 2 * i + half + 1)
                    moments(v, step, z[half][0:R, 0:E], stats[:, half], mv2[:, half, :]).then_inc(moments_ready, 1)
                v.wait_ge(std_ready, 2 * i + 2)
                step(v.reciprocal(rstd2[:, :], std2[:, :]))
                for half in range(2):
                    v.wait_ge(gained_ready, 2 * i + half + 1)
                    normalize(v, z_normed[:, half, :], z[half][0:R, 0:E], mv2[:, half, :], rstd2[:, half:half + 1]).then_inc(z_normed_ready, 1)
                step.leave(PAIRS, per_turn)

        @block.tensor
        def _(pe):
            pe.wait_ge(ident_ready, 3)
            pe.wait_ge(const_loaded, all_const)
            with pe.Fori(0, PAIRS) as i:
                for half in range(2):
                    pe.wait_ge(normed_ready, 2 * i + half + 3)
                    for k in range(KP):
                        c, j = divmod(k, KP // 2)
                        ins = pe.transpose(turned[half][:, c, j * R:(j + 1) * R], normed[:, half, k * 128:(k + 1) * 128],
                                           ident[0:R, 0:R])
                    ins.then_inc(turned_ready, 1)
                for half in range(2):
                    pe.wait_ge(normedT_by_act, 2 * i + half + 1)
                    pe.wait_ge(normedT_by_vec, 2 * i + half + 1)
                    for k in range(KP):
                        pe.matmul(z[half][0:R, 0:E], normedT[:, half, k, :], proj[:, k, :], start=(k == 0), stop=False)
                    pe.matmul(z[half][0:R, 0:E], ones_row[:, 0:R], proj_bias[:, :], start=False, stop=True).then_inc(z_ready, 1)


def attend(nc, space, io, hidden, ident, eps, spare):
    D = 64
    scale = (3.0 / D) ** 0.5
    with ExitStack() as stack:
        def sb(name, shape, dt=F32):
            return space.sb(stack, name, shape, dt)

        wq = sb("at_wq", [128, KE, D])
        wk = sb("at_wk", [128, KE, D])
        wv = sb("at_wv", [128, KE, D])
        wo = sb("at_wo", [D, E])
        same = sb("at_same", [R, R])
        stats = sb("at_stats", [R, 2, 1, 6])
        mv = sb("at_mv", [R, 2, 2])
        std = sb("at_std", [R, 2])
        rstd = sb("at_rstd", [R, 2])
        normed = sb("at_normed", [R, 2, E])
        normedT = sb("at_normedT", [128, 2, KE, R])
        qkT = sb("at_qkT", [D, 2, 2, R])
        vals = sb("at_vals", [R, 2, D])
        scoresT = sb("at_scoresT", [R, 2, R])
        contextT = sb("at_contextT", [D, 2, R])
        ps_turned = [space.ps(stack, f"at_ps_turned{i}", [128, 512]) for i in range(2)]
        ps_qkv = [space.ps(stack, f"at_ps_qkv{i}", [128, 512]) for i in range(2)]
        ps_mix = [space.ps(stack, f"at_ps_mix{i}", [128, 512]) for i in range(2)]
        ps_out = [space.ps(stack, f"at_ps_out{i}", [128, 512]) for i in range(2)]

        loaded = space.sem("at_loaded")
        same_step = space.sem("at_same_step")
        vec_step = space.sem("at_vec_step")
        moments_ready = space.sem("at_moments_ready")
        std_ready = space.sem("at_std_ready")
        normed_ready = space.sem("at_normed_ready")
        turned_ready = space.sem("at_turned_ready")
        normedT_ready = space.sem("at_normedT_ready")
        qkv_ready = space.sem("at_qkv_ready")
        qkv_copied = space.sem("at_qkv_copied")
        scores_ready = space.sem("at_scores_ready")
        scores_masked = space.sem("at_scores_masked")
        context_ready = space.sem("at_context_ready")
        context_copied = space.sem("at_context_copied")
        out_ready = space.sem("at_out_ready")
        added = space.sem("at_added")

        block = stack.enter_context(nc.Block())

        @block.sync
        def _(sp):
            for w, name in ((wq, "wqT"), (wk, "wkT"), (wv, "wvT")):
                sp.dma_start(w[:, :, :], io[name].rearrange("(k p) n -> p k n", p=128)).then_inc(loaded, 16)
            sp.dma_start(wo[:, :], io["woT"]).then_inc(loaded, 16)

        @block.gpsimd
        def _(pool):
            pool.memset(same[:, :], scale).then_inc(same_step, 1)
            pool.wait_ge(same_step, 1)
            cols = same[:, :].rearrange("p (s t) -> p s t", s=SPT)
            pool.affine_select(out=cols, in_=cols, compare_op=ALU.is_ge, fill=0.0, base=0,
                               pattern=[[-SEQ, SPT], [0, SEQ]], channel_multiplier=1).then_inc(same_step, 1)
            pool.wait_ge(same_step, 2)
            pool.affine_select(out=cols, in_=cols, compare_op=ALU.is_ge, fill=0.0, base=SEQ - 1,
                               pattern=[[SEQ, SPT], [0, SEQ]], channel_multiplier=-1).then_inc(same_step, 1)

        @block.vector
        def _(v):
            step = Chain(v, vec_step, spare)
            v.wait_ge(same_step, 3)
            per_turn = 2 + 1
            with v.Fori(0, PAIRS) as i:
                step.enter(i, per_turn)
                for half in range(2):
                    moments(v, step, hidden[:, 2 * i + half, :], stats[:, half], mv[:, half, :]).then_inc(moments_ready, 1)
                v.wait_ge(std_ready, i + 1)
                step(v.reciprocal(rstd[:, :], std[:, :]))
                for half in range(2):
                    normalize(v, normed[:, half, :], hidden[:, 2 * i + half, :], mv[:, half, :],
                              rstd[:, half:half + 1]).then_inc(normed_ready, 1)
                for half in range(2):
                    v.wait_ge(scores_ready, 2 * i + half + 1)
                    v.tensor_tensor(scoresT[:, half, :], ps_mix[half][0:R, 0:R], same[:, :], ALU.mult).then_inc(scores_masked, 1)
                for half in range(2):
                    v.wait_ge(out_ready, 2 * i + half + 1)
                    v.tensor_tensor(hidden[:, 2 * i + half, :], hidden[:, 2 * i + half, :], ps_out[half][0:R, 0:E],
                                    ALU.add).then_inc(added, 1)
                step.leave(PAIRS, per_turn)

        @block.scalar
        def _(act):
            with act.Fori(0, PAIRS) as i:
                act.wait_ge(moments_ready, 2 * i + 2)
                act.activation(std[:, :], mv[:, :, 1], ACT.Sqrt, bias=eps[:, :]).then_inc(std_ready, 1)
                for half in range(2):
                    act.wait_ge(turned_ready, 2 * i + half + 1)
                    act.copy(normedT[:, half, :, :].rearrange("p k r -> p (k r)"), ps_turned[half][:, 0:G2]).then_inc(normedT_ready, 1)
                for half in range(2):
                    act.wait_ge(qkv_ready, 2 * i + half + 1)
                    act.copy(qkT[:, half, :, :].rearrange("p k r -> p (k r)"), ps_qkv[half][0:D, 0:G2])
                    act.copy(vals[:, half, :], ps_qkv[half][0:R, G2:G2 + D]).then_inc(qkv_copied, 1)
                for half in range(2):
                    act.wait_ge(context_ready, 2 * i + half + 1)
                    act.copy(contextT[:, half, :], ps_mix[half][0:D, 128:128 + R]).then_inc(context_copied, 1)

        @block.tensor
        def _(pe):
            pe.wait_ge(loaded, 64)
            with pe.Fori(0, PAIRS) as i:
                for half in range(2):
                    pe.wait_ge(normed_ready, 2 * i + half + 1)
                    for k in range(KE):
                        ins = pe.transpose(ps_turned[half][:, k * R:(k + 1) * R], normed[:, half, k * 128:(k + 1) * 128], ident[0:R, 0:R])
                    ins.then_inc(turned_ready, 1)
                for half in range(2):
                    pe.wait_ge(normedT_ready, 2 * i + half + 1)
                    for c, w in enumerate((wq, wk)):
                        for k in range(KE):
                            pe.matmul(ps_qkv[half][0:D, c * R:(c + 1) * R], w[:, k, :], normedT[:, half, k, :],
                                      start=(k == 0), stop=(k == KE - 1))
                    for k in range(KE):
                        ins = pe.matmul(ps_qkv[half][0:R, G2:G2 + D], normedT[:, half, k, :], wv[:, k, :],
                                        start=(k == 0), stop=(k == KE - 1))
                    ins.then_inc(qkv_ready, 1)
                for half in range(2):
                    pe.wait_ge(qkv_copied, 2 * i + half + 1)
                    pe.matmul(ps_mix[half][0:R, 0:R], qkT[:, half, 1, :], qkT[:, half, 0, :], start=True, stop=True).then_inc(scores_ready, 1)
                for half in range(2):
                    pe.wait_ge(scores_masked, 2 * i + half + 1)
                    pe.matmul(ps_mix[half][0:D, 128:128 + R], vals[:, half, :], scoresT[:, half, :], start=True, stop=True).then_inc(context_ready, 1)
                for half in range(2):
                    pe.wait_ge(context_copied, 2 * i + half + 1)
                    pe.matmul(ps_out[half][0:R, 0:E], contextT[:, half, :], wo[:, :], start=True, stop=True).then_inc(out_ready, 1)


EXPERTS = 8
JOB = 256
SUB = JOB // 128
MAX_JOBS = (2 * TOK + EXPERTS * 2 * JOB) // JOB
SLOTS = (MAX_JOBS + 1) * JOB
MOST = -(-TOK // JOB)
BIG = 1e38


def route(nc, space, name, gate_dram, scores_softmaxed, hidden, normed_all, slots, shares, jobs, slot_rows,
          ident, eps, spare):
    with ExitStack() as stack:
        def sb(what, shape, dt=F32):
            return space.sb(stack, f"{name}_{what}", shape, dt)

        def sem(what):
            return space.sem(f"{name}_{what}")

        gate = sb("gate", [128, KE, EXPERTS])
        before = sb("before", [R, R])
        ones = sb("ones", [R, R])
        prefer = sb("prefer", [R, EXPERTS])
        steps_of = sb("steps_of", [R, MOST - 1])
        stats = sb("stats", [R, 2, 1, 6])
        mv = sb("mv", [R, 2, 2])
        std = sb("std", [R, 2])
        rstd = sb("rstd", [R, 2])
        normed_half = sb("normed_half", [R, 2, E])
        normedT = sb("normedT", [128, 2, KE, R])
        scores = sb("scores", [R, NT, EXPERTS])
        rest = sb("rest", [R, NT, EXPERTS])
        equal = sb("equal", [R, NT, EXPERTS])
        chosen = sb("chosen", [R, 2, NT, EXPERTS])
        both = sb("both", [R, NT, EXPERTS])
        top = sb("top", [R, 2, NT])
        pick = sb("pick", [R, 2, NT])
        expd = sb("expd", [R, NT, EXPERTS])
        total = sb("total", [R, NT])
        gap = sb("gap", [R, NT])
        run = sb("run", [R, 2, NT, EXPERTS])
        place = sb("place", [R, NT, EXPERTS])
        over = sb("over", [R, EXPERTS, MOST - 1])
        count = sb("count", [R, EXPERTS])
        ends = sb("ends", [R, 2, EXPERTS])
        first = sb("first", [R, EXPERTS])
        base = sb("base", [R, EXPERTS])
        slot_f = sb("slot_f", [R, 2, NT])
        ps_turned = [space.ps(stack, f"{name}_ps_turned{i}", [128, 512]) for i in range(2)]
        ps_gate = [space.ps(stack, f"{name}_ps_gate{i}", [128, 512]) for i in range(2)]
        ps_before = space.ps(stack, f"{name}_ps_before", [128, 512])
        ps_total = space.ps(stack, f"{name}_ps_total", [128, 512])

        loaded = sem("loaded")
        consts = sem("consts")
        const_step = sem("const_step")
        vec_step = sem("vec_step")
        moments_ready = sem("moments_ready")
        std_ready = sem("std_ready")
        normed_ready = sem("normed_ready")
        turned_ready = sem("turned_ready")
        normedT_ready = sem("normedT_ready")
        gate_ready = sem("gate_ready")
        gate_read = sem("gate_read")
        exp_in = sem("exp_in")
        exp_out = sem("exp_out")
        both_ready = sem("both_ready")
        counted = sem("counted")
        slots_ready = sem("slots_ready")
        scattered = sem("scattered")

        block = stack.enter_context(nc.Block())

        @block.sync
        def _(sp):
            sp.dma_start(gate[:, :, :], gate_dram.rearrange("(k p) n -> p k n", p=128)).then_inc(loaded, 16)

        @block.gpsimd
        def _(pool):
            pool.memset(ones[:, :], 1.0).then_inc(consts, 1)
            pool.memset(before[:, :], 1.0).then_inc(const_step, 1)
            for e in range(EXPERTS):
                ins = pool.memset(prefer[:, e:e + 1], float(EXPERTS - e))
            ins.then_inc(consts, 1)
            for c in range(MOST - 1):
                ins = pool.memset(steps_of[:, c:c + 1], float(JOB * (c + 1)))
            ins.then_inc(consts, 1)
            pool.wait_ge(const_step, 1)
            pool.affine_select(out=before[:, :], in_=before[:, :], compare_op=ALU.is_ge, fill=0.0, base=-1,
                               pattern=[[1, R]], channel_multiplier=-1).then_inc(consts, 1)
            for c in range(2):
                pool.wait_ge(slots_ready, c + 1)
                for t in range(NT):
                    pool.indirect_dma_start(slot_rows, bass.IndirectOffsetOnAxis(ap=slots[:, c, t:t + 1], axis=0),
                                            normed_all[:, t, :], None).then_inc(scattered, 16)
            pool.wait_ge(scattered, 16 * 2 * NT)

        @block.tensor
        def _(pe):
            pe.wait_ge(loaded, 16)
            with pe.Fori(0, PAIRS) as i:
                for half in range(2):
                    pe.wait_ge(normed_ready, 2 * i + half + 1)
                    for k in range(KE):
                        ins = pe.transpose(ps_turned[half][:, k * R:(k + 1) * R], normed_half[:, half, k * 128:(k + 1) * 128],
                                           ident[0:R, 0:R])
                    ins.then_inc(turned_ready, 1)
                for half in range(2):
                    pe.wait_ge(normedT_ready, 2 * i + half + 1)
                    for k in range(KE):
                        ins = pe.matmul(ps_gate[half][0:R, 0:EXPERTS], normedT[:, half, k, :], gate[:, k, :],
                                        start=(k == 0), stop=(k == KE - 1))
                    ins.then_inc(gate_ready, 1)
            pe.wait_ge(both_ready, 1)
            pe.wait_ge(consts, 4)
            flat = both[:, :, :].rearrange("p t e -> p (t e)")
            pe.matmul(ps_before[0:R, 0:NT * EXPERTS], before[:, :], flat, start=True, stop=True)
            pe.matmul(ps_total[0:R, 0:NT * EXPERTS], ones[:, :], flat, start=True, stop=True).then_inc(counted, 1)

        @block.scalar
        def _(act):
            with act.Fori(0, PAIRS) as i:
                act.wait_ge(moments_ready, 2 * i + 2)
                act.activation(std[:, :], mv[:, :, 1], ACT.Sqrt, bias=eps[:, :]).then_inc(std_ready, 1)
                for half in range(2):
                    act.wait_ge(turned_ready, 2 * i + half + 1)
                    act.copy(normedT[:, half, :, :].rearrange("p k r -> p (k r)"), ps_turned[half][:, 0:G2]).then_inc(normedT_ready, 1)
            act.wait_ge(exp_in, 1)
            if scores_softmaxed:
                act.activation(expd[:, :, :], rest[:, :, :], ACT.Exp).then_inc(exp_out, 1)
            else:
                act.activation(total[:, :], gap[:, :], ACT.Exp).then_inc(exp_out, 1)

        @block.vector
        def _(v):
            step = Chain(v, vec_step, spare)
            per_turn = 2 + 1
            with v.Fori(0, PAIRS) as i:
                step.enter(i, per_turn)
                for half in range(2):
                    moments(v, step, hidden[:, 2 * i + half, :], stats[:, half], mv[:, half, :]).then_inc(moments_ready, 1)
                v.wait_ge(std_ready, i + 1)
                step(v.reciprocal(rstd[:, :], std[:, :]))
                for half in range(2):
                    normalize(v, normed_half[:, half, :], hidden[:, 2 * i + half, :], mv[:, half, :],
                              rstd[:, half:half + 1]).then_inc(normed_ready, 1)
                    v.wait_ge(normed_ready, 2 * i + half + 1)
                    v.tensor_copy(normed_all[:, 2 * i + half, :], normed_half[:, half, :])
                for half in range(2):
                    v.wait_ge(gate_ready, 2 * i + half + 1)
                    v.tensor_copy(scores[:, 2 * i + half, :], ps_gate[half][0:R, 0:EXPERTS]).then_inc(gate_read, 1)
                step.leave(PAIRS, per_turn)
            v.wait_ge(gate_read, NT)
            v.wait_ge(consts, 4)

            def per_token(x):
                return x.unsqueeze(2).broadcast_to([R, NT, EXPERTS])

            def per_expert(x):
                return x.unsqueeze(1).broadcast_to([R, NT, EXPERTS])

            if scores_softmaxed:
                step(v.tensor_reduce(top[:, 0, :], scores[:, :, :], AX.X, ALU.max))
                v.tensor_tensor(rest[:, :, :], scores[:, :, :], per_token(top[:, 0, :]), ALU.subtract).then_inc(exp_in, 1)
                v.wait_ge(exp_out, 1)
                step(v.tensor_reduce(total[:, :], expd[:, :, :], AX.X, ALU.add))
                step(v.reciprocal(gap[:, :], total[:, :]))
                step(v.tensor_tensor(scores[:, :, :], expd[:, :, :], per_token(gap[:, :]), ALU.mult))
            for c, values in enumerate((scores, rest)):
                step(v.tensor_reduce(top[:, c, :], values[:, :, :], AX.X, ALU.max))
                step(v.tensor_tensor(equal[:, :, :], values[:, :, :], per_token(top[:, c, :]), ALU.is_equal))
                step(v.tensor_tensor(place[:, :, :], equal[:, :, :], per_expert(prefer[:, :]), ALU.mult))
                step(v.tensor_reduce(pick[:, c, :], place[:, :, :], AX.X, ALU.max))
                step(v.tensor_tensor(chosen[:, c], per_expert(prefer[:, :]), per_token(pick[:, c, :]), ALU.is_equal))
                if c == 0:
                    step(v.scalar_tensor_tensor(rest[:, :, :].rearrange("p t e -> p (t e)"),
                                                chosen[:, 0].rearrange("p t e -> p (t e)"), -BIG,
                                                scores[:, :, :].rearrange("p t e -> p (t e)"), ALU.mult, ALU.add))
            v.tensor_tensor(both[:, :, :], chosen[:, 0], chosen[:, 1], ALU.add).then_inc(both_ready, 1)
            if scores_softmaxed:
                step(v.scalar_tensor_tensor(total[:, :], top[:, 0, :], 1e-20, top[:, 1, :], ALU.add, ALU.add))
                step(v.reciprocal(gap[:, :], total[:, :]))
                step(v.tensor_tensor(shares[:, 0, :], top[:, 0, :], gap[:, :], ALU.mult))
                step(v.tensor_tensor(shares[:, 1, :], top[:, 1, :], gap[:, :], ALU.mult))
            else:
                v.tensor_tensor(gap[:, :], top[:, 1, :], top[:, 0, :], ALU.subtract).then_inc(exp_in, 1)
                v.wait_ge(exp_out, 1)
                step(v.tensor_scalar(pick[:, 0, :], total[:, :], 1.0, None, ALU.add))
                step(v.reciprocal(shares[:, 0, :], pick[:, 0, :]))
                step(v.tensor_tensor(shares[:, 1, :], total[:, :], shares[:, 0, :], ALU.mult))
            v.wait_ge(counted, 1)
            step(v.tensor_copy(run[:, 0].rearrange("p t e -> p (t e)"), ps_total[0:R, 0:NT * EXPERTS]))
            now, reach = 0, 1
            while reach < NT:
                a, b = run[:, now], run[:, 1 - now]
                step(v.tensor_copy(b[:, 0:reach, :], a[:, 0:reach, :]))
                step(v.tensor_tensor(b[:, reach:NT, :], a[:, reach:NT, :], a[:, 0:NT - reach, :], ALU.add))
                now, reach = 1 - now, 2 * reach
            runs = run[:, now]
            step(v.tensor_tensor(over[:, :, :], runs[:, NT - 1, :].unsqueeze(2).broadcast_to([R, EXPERTS, MOST - 1]),
                                 steps_of[:, :].unsqueeze(1).broadcast_to([R, EXPERTS, MOST - 1]), ALU.is_gt))
            step(v.tensor_reduce(count[:, :], over[:, :, :], AX.X, ALU.add))
            step(v.tensor_scalar(count[:, :], count[:, :], 1.0, 2.0, ALU.add, ALU.max))
            step(v.tensor_copy(ends[:, 0, :], count[:, :]))
            now2, reach = 0, 1
            while reach < EXPERTS:
                a, b = ends[:, now2], ends[:, 1 - now2]
                step(v.tensor_copy(b[:, 0:reach], a[:, 0:reach]))
                step(v.tensor_tensor(b[:, reach:EXPERTS], a[:, reach:EXPERTS], a[:, 0:EXPERTS - reach], ALU.add))
                now2, reach = 1 - now2, 2 * reach
            step(v.tensor_tensor(first[:, :], ends[:, now2], count[:, :], ALU.subtract))
            step(v.tensor_copy(jobs[:, 0:EXPERTS], first[0:1, :]))
            step(v.tensor_copy(jobs[:, EXPERTS:EXPERTS + 1], ends[0:1, now2, EXPERTS - 1:EXPERTS]))
            step(v.tensor_scalar(base[:, :], first[:, :], float(JOB), None, ALU.mult))
            step(v.tensor_tensor(place[:, :, :].rearrange("p t e -> p (t e)"), ps_before[0:R, 0:NT * EXPERTS],
                                 runs.rearrange("p t e -> p (t e)"), ALU.add))
            step(v.tensor_tensor(place[:, :, :].rearrange("p t e -> p (t e)"), place[:, :, :].rearrange("p t e -> p (t e)"),
                                 ps_total[0:R, 0:NT * EXPERTS], ALU.subtract))
            step(v.tensor_tensor(place[:, :, :], place[:, :, :], per_expert(base[:, :]), ALU.add))
            for c in range(2):
                step(v.tensor_tensor(equal[:, :, :], chosen[:, c], place[:, :, :], ALU.mult))
                step(v.tensor_reduce(slot_f[:, c, :], equal[:, :, :], AX.X, ALU.add))
                v.tensor_copy(slots[:, c, :], slot_f[:, c, :]).then_inc(slots_ready, 1)


def load_rows(eng, sem, tile, dram):
    rows = dram.shape[0]
    whole = rows // 128
    n = 1
    eng.dma_start(tile[:, 0:whole, :], dram[0:whole * 128].rearrange("(k p) n -> p k n", p=128)).then_inc(sem, 16)
    if rows % 128:
        eng.dma_start(tile[0:rows % 128, whole, :], dram[whole * 128:rows]).then_inc(sem, 16)
        n += 1
    return n


def run_experts(nc, space, name, ups_dram, up_bias_dram, down_dram, down_bias_dram, inner, jobs, slot_rows, out_rows, ident):
    gated = len(ups_dram) == 2
    KD = -(-inner // 128)
    width = [min(128, inner - m * 128) for m in range(KD)]
    U = len(ups_dram)
    with ExitStack() as stack:
        def sb(what, shape, dt=F32):
            return space.sb(stack, f"{name}_{what}", shape, dt)

        def sem(what):
            return space.sem(f"{name}_{what}")

        up_raw = sb("up_raw", [128, U, KE, inner])
        down_raw = sb("down_raw", [128, KD, E])
        up_hi = [sb(f"up_hi{p}", [128, U, KE, inner], F32R) for p in range(2)]
        up_lo = [sb(f"up_lo{p}", [128, U, KE, inner], F32R) for p in range(2)]
        down_hi = [sb(f"down_hi{p}", [128, KD, E], F32R) for p in range(2)]
        down_lo = [sb(f"down_lo{p}", [128, KD, E], F32R) for p in range(2)]
        if not gated:
            up_bias = sb("up_bias", [128, EXPERTS, KD])
            down_bias = [sb(f"down_bias{p}", [128, E]) for p in range(2)]
        rows = sb("rows", [128, SUB, E])
        rowsT_hi = sb("rowsT_hi", [128, KE, JOB], F32R)
        rowsT_lo = sb("rowsT_lo", [128, KE, JOB], F32R)
        RING = 4 if not gated else KD
        act_out = sb("act_out", [128, RING, JOB])
        inner_f = sb("inner_f", [128, KD, JOB]) if gated else act_out
        inner_hi = sb("inner_hi", [128, KD, JOB], F32R)
        inner_lo = sb("inner_lo", [128, KD, JOB], F32R)
        result = sb("result", [128, SUB, E])
        ps_rowsT = space.ps(stack, f"{name}_ps_rowsT", [128, KE, JOB])
        BANKS = 4 if not gated else KD
        ps_up = [space.ps(stack, f"{name}_ps_up{b}", [128, 512]) for b in range(BANKS)]
        ps_down = [space.ps(stack, f"{name}_ps_down{s}", [128, 512]) for s in range(SUB)]

        raw_loaded = sem("raw_loaded")
        bias_loaded = [sem(f"bias_loaded{p}") for p in range(2)]
        up_bias_loaded = sem("up_bias_loaded")
        weights_by_act = sem("weights_by_act")
        weights_by_vec = sem("weights_by_vec")
        rows_loaded = sem("rows_loaded")
        rowsT_ready = sem("rowsT_ready")
        rowsT_hi_ready = sem("rowsT_hi_ready")
        rowsT_split = sem("rowsT_split")
        up_ready = sem("up_ready")
        act_done = sem("act_done")
        inner_done = sem("inner_done")
        inner_hi_done = sem("inner_hi_done")
        inner_split = sem("inner_split")
        down_ready = sem("down_ready")
        result_ready = sem("result_ready")
        result_stored = sem("result_stored")
        raw_dmas = U + (2 if inner % 128 else 1)

        def expert_jobs(eng, e):
            first, end = (eng.value_load(jobs[0:1, n:n + 1], min_val=2 * n, max_val=MAX_JOBS - 2 * (EXPERTS - n))
                          for n in (e, e + 1))
            return first, end

        block = stack.enter_context(nc.Block())

        @block.sync
        def _(sp):
            def load_weights(e):
                if e >= 1:
                    sp.wait_ge(weights_by_act, e)
                    sp.wait_ge(weights_by_vec, e)
                n = 0
                for u, dram in enumerate(ups_dram):
                    n += load_rows(sp, raw_loaded, up_raw[:, u], dram[e])
                n += load_rows(sp, raw_loaded, down_raw, down_dram[e])
                assert n == raw_dmas

            def load_bias(e):
                if not gated:
                    sp.dma_start(down_bias[e % 2][:, :], down_bias_dram[e].partition_broadcast(128)).then_inc(bias_loaded[e % 2], 16)

            def load_rows_of(job):
                sp.dma_start(rows[:, :, :], slot_rows.rearrange("(j s p) e -> j p s e", s=SUB, p=128)[job]).then_inc(rows_loaded, 16)

            def one_job(j):
                sp.wait_ge(rowsT_ready, j + 1)
                load_rows_of(j + 1)

            def store(j):
                sp.wait_ge(result_ready, j + 2)
                sp.dma_start(out_rows.rearrange("(j s p) e -> j p s e", s=SUB, p=128)[j], result[:, :, :]).then_inc(result_stored, 16)

            load_weights(0)
            if not gated:
                sp.dma_start(up_bias[:, :, :], up_bias_dram).then_inc(up_bias_loaded, 16)
            load_bias(0)
            load_rows_of(0)
            load_weights(1)
            for e in range(EXPERTS):
                first, end = expert_jobs(sp, e)
                one_job(first)
                store(first)
                if e + 1 < EXPERTS:
                    load_bias(e + 1)
                if e + 2 < EXPERTS:
                    load_weights(e + 2)
                with sp.Fori(first + 1, end) as j:
                    one_job(j)
                    store(j)

        @block.gpsimd
        def _(pool):
            _, end = expert_jobs(pool, EXPERTS - 1)
            pool.wait_ge(result_stored, 16 * (end + 1))

        @block.scalar
        def _(act):
            def split_high(e, part, parts):
                p = e % 2
                for u in range(U):
                    for k in range(KE):
                        a, b = inner * part // parts, inner * (part + 1) // parts
                        ins = act.copy(up_hi[p][:, u, k, a:b], up_raw[:, u, k, a:b])
                a, b = KD * part // parts, KD * (part + 1) // parts
                for k in range(a, b):
                    ins = act.copy(down_hi[p][0:width[k], k, :], down_raw[0:width[k], k, :])
                if part == parts - 1:
                    ins.then_inc(weights_by_act, 1)

            def one_job(e, j, split_next):
                for m in range(KD):
                    act.wait_ge(up_ready, KD * j + m + 1)
                    r = m % RING
                    if gated:
                        act.activation(act_out[0:width[m], r, :], ps_up[m][0:width[m], 0:JOB], ACT.Silu).then_inc(act_done, 1)
                    else:
                        act.activation(act_out[:, r, :], ps_up[m % BANKS][:, 0:JOB], ACT.Gelu, bias=up_bias[:, e, m:m + 1]).then_inc(act_done, 1)
                    if split_next:
                        if m == 0:
                            act.wait_ge(raw_loaded, 16 * raw_dmas * (e + 2))
                        split_high(e + 1, m, KD)

            act.wait_ge(raw_loaded, 16 * raw_dmas)
            split_high(0, 0, 1)
            if not gated:
                act.wait_ge(up_bias_loaded, 16)
            for e in range(EXPERTS):
                first, end = expert_jobs(act, e)
                one_job(e, first, e + 1 < EXPERTS)
                with act.Fori(first + 1, end) as j:
                    one_job(e, j, False)

        @block.vector
        def _(v):
            def split_low(e, part, parts):
                p = e % 2
                for u in range(U):
                    a, b = inner * part // parts, inner * (part + 1) // parts
                    v.tensor_tensor(up_lo[p][:, u, :, a:b], up_raw[:, u, :, a:b], up_hi[p][:, u, :, a:b].bitcast(F32), ALU.subtract)
                a, b = KD * part // parts, KD * (part + 1) // parts
                for k in range(a, b):
                    w = width[k]
                    ins = v.tensor_tensor(down_lo[p][0:w, k, :], down_raw[0:w, k, :], down_hi[p][0:w, k, :].bitcast(F32), ALU.subtract)
                if part == parts - 1:
                    ins.then_inc(weights_by_vec, 1)

            def turn_rows(j):
                v.wait_ge(rowsT_ready, j + 1)
                v.tensor_copy(rowsT_hi[:, :, :], ps_rowsT[:, :, :]).then_inc(rowsT_hi_ready, 1)
                v.wait_ge(rowsT_hi_ready, j + 1)
                v.tensor_tensor(rowsT_lo[:, :, :], ps_rowsT[:, :, :], rowsT_hi[:, :, :].bitcast(F32), ALU.subtract).then_inc(rowsT_split, 1)

            def one_job(e, j, split_next):
                for m in range(KD):
                    w, n = width[m], KD * j + m + 1
                    v.wait_ge(act_done, n)
                    if gated:
                        v.tensor_tensor(inner_f[0:w, m, :], act_out[0:w, m, :], ps_up[m][0:w, JOB:2 * JOB], ALU.mult).then_inc(inner_done, 1)
                        v.wait_ge(inner_done, n)
                    source = inner_f[0:w, m % RING, :]
                    v.tensor_copy(inner_hi[0:w, m, :], source).then_inc(inner_hi_done, 1)
                    v.wait_ge(inner_hi_done, n)
                    v.tensor_tensor(inner_lo[0:w, m, :], source, inner_hi[0:w, m, :].bitcast(F32), ALU.subtract).then_inc(inner_split, 1)
                    if split_next and m >= 1:
                        if m == KD - 1:
                            v.wait_ge(weights_by_act, e + 2)
                            split_low(e + 1, 0, 1)
                turn_rows(j + 1)
                v.wait_ge(down_ready, j + 1)
                v.wait_ge(result_stored, 16 * (j + 1))
                for s in range(SUB):
                    if gated:
                        ins = v.tensor_copy(result[:, s, :], ps_down[s][:, 0:E])
                    else:
                        if s == 0:
                            v.wait_ge(bias_loaded[e % 2], 16 * (e // 2 + 1))
                        ins = v.tensor_tensor(result[:, s, :], ps_down[s][:, 0:E], down_bias[e % 2][:, :], ALU.add)
                ins.then_inc(result_ready, 1)

            v.sem_inc(inner_split, RING)
            v.sem_inc(result_ready, 1)
            v.sem_inc(result_stored, 16)
            v.wait_ge(weights_by_act, 1)
            split_low(0, 0, 1)
            turn_rows(0)
            for e in range(EXPERTS):
                first, end = expert_jobs(v, e)
                one_job(e, first, e + 1 < EXPERTS)
                with v.Fori(first + 1, end) as j:
                    one_job(e, j, False)

        @block.tensor
        def _(pe):
            def turn_rows(j):
                pe.wait_ge(rows_loaded, 16 * (j + 1))
                for k in range(KE):
                    for s in range(SUB):
                        ins = pe.transpose(ps_rowsT[:, k, s * 128:(s + 1) * 128], rows[:, s, k * 128:(k + 1) * 128], ident[:, :])
                ins.then_inc(rowsT_ready, 1)

            def one_job(e, j):
                p = e % 2
                pe.wait_ge(rowsT_split, j + 1)
                for m in range(KD):
                    w = width[m]
                    pe.wait_ge(inner_split, KD * j + m + 1)
                    for u in range(U):
                        out = ps_up[m % BANKS][0:w, u * JOB:(u + 1) * JOB]
                        for k in range(KE):
                            for c, (wt, xt) in enumerate(((up_hi, rowsT_hi), (up_hi, rowsT_lo), (up_lo, rowsT_hi))):
                                ins = pe.matmul(out, wt[p][:, u, k, m * 128:m * 128 + w], xt[:, k, :],
                                                start=(k == 0 and c == 0), stop=(k == KE - 1 and c == 2))
                    ins.then_inc(up_ready, 1)
                turn_rows(j + 1)
                pe.wait_ge(result_ready, j + 1)
                for m in range(KD):
                    w = width[m]
                    pe.wait_ge(inner_split, KD * j + m + 1 + RING)
                    for s in range(SUB):
                        for c, (xt, wt) in enumerate(((inner_hi, down_hi), (inner_lo, down_hi), (inner_hi, down_lo))):
                            ins = pe.matmul(ps_down[s][:, 0:E], xt[0:w, m, s * 128:(s + 1) * 128], wt[p][0:w, m, :],
                                            start=(m == 0 and c == 0), stop=(m == KD - 1 and c == 2))
                ins.then_inc(down_ready, 1)

            turn_rows(0)
            for e in range(EXPERTS):
                first, end = expert_jobs(pe, e)
                pe.wait_ge(weights_by_act, e + 1)
                pe.wait_ge(weights_by_vec, e + 1)
                one_job(e, first)
                with pe.Fori(first + 1, end) as j:
                    one_job(e, j)


HEADS = 32
HD = 64
DIM = HEADS * HD
STATE = 128
LEVELS = 7
TAPS = 4
CONV_TILES = (2 * STATE + DIM) // 128
Z_TILES = DIM // 128
FM_TILES = CONV_TILES + Z_TILES
DTL = HEADS * (1 + LEVELS)
GROUP = 4
GROUPS = HEADS // GROUP
LROWS = LEVELS * SPT
CHUNK = 16
CHUNKS = [(a, min(a + CHUNK, SEQ)) for a in range(0, SEQ, CHUNK)]
assert 1 + (SEQ - 1).bit_length() == LEVELS and DTL == 256 and SEQ % 2 == 0
RMS_EPS = 1e-5


def split_projection(nc, space, in_dram, w_hi, w_lo, out_dram, norm_dram, w_out):
    with ExitStack() as stack:
        N = FM_TILES * 128 + DTL
        COLS = 512
        CH = N // COLS
        assert CH * COLS == N
        raw = [space.sb(stack, f"sp_raw{p}", [128, KE, COLS]) for p in range(2)]
        norm = space.sb(stack, "sp_norm", [128, Z_TILES])
        raw_out = space.sb(stack, "sp_raw_out", [128, Z_TILES, E])
        loaded = [space.sem(f"sp_loaded{p}") for p in range(2)]
        out_loaded = space.sem("sp_out_loaded")
        high_done = space.sem("sp_high_done")
        low_done = space.sem("sp_low_done")
        block = stack.enter_context(nc.Block())
        view = in_dram.rearrange("(k p) n -> p k n", p=128)

        @block.sync
        def _(sp):
            for c in range(CH):
                if c >= 2:
                    sp.wait_ge(low_done, c - 1)
                sp.dma_start(raw[c % 2][:, :, :], view[:, :, c * COLS:(c + 1) * COLS]).then_inc(loaded[c % 2], 16)
                if c == 1:
                    sp.dma_start(norm[:, :], norm_dram).then_inc(out_loaded, 16)
                    sp.dma_start(raw_out[:, :, :], out_dram.rearrange("(m p) n -> p m n", p=128)).then_inc(out_loaded, 16)

        @block.scalar
        def _(act):
            for c in range(CH):
                act.wait_ge(loaded[c % 2], 16 * (c // 2 + 1))
                act.copy(w_hi[:, :, c * COLS:(c + 1) * COLS], raw[c % 2][:, :, :]).then_inc(high_done, 1)
            act.wait_ge(out_loaded, 32)
            for m in range(Z_TILES):
                act.activation(w_out[:, m, :], raw_out[:, m, :], ACT.Copy, scale=norm[:, m:m + 1])

        @block.vector
        def _(v):
            for c in range(CH):
                v.wait_ge(high_done, c + 1)
                part = slice(c * COLS, (c + 1) * COLS)
                v.tensor_tensor(w_lo[:, :, part], raw[c % 2][:, :, :], w_hi[:, :, part].bitcast(F32), ALU.subtract).then_inc(low_done, 1)


def mix_sequences(nc, space, io, stream, expert_rows, slots, shares, w_hi, w_lo, w_out, lam_rows, ident, eps, spare):
    with ExitStack() as stack:
        def sb(what, shape, dt=F32):
            return space.sb(stack, f"mx_{what}", shape, dt)

        def sem(what):
            return space.sem(f"mx_{what}")

        fm_bias = sb("fm_bias", [128, FM_TILES])
        taps = sb("taps", [128, CONV_TILES, TAPS])
        skip = sb("skip", [128, Z_TILES])
        dtl_bias = sb("dtl_bias", [R, DTL])
        dt_bias = sb("dt_bias", [R, HEADS])
        factor = sb("factor", [R, DTL])
        a_log = sb("a_log", [R, HEADS])
        a_exp = sb("a_exp", [R, HEADS])
        out_bias = sb("out_bias", [R, E])
        later = sb("later", [R, R])
        upto = sb("upto", [R, SEQ])
        causal = sb("causal", [R, R])
        block_of = sb("block_of", [R, R])
        odd = sb("odd", [R, 2])
        level_of = sb("level_of", [LROWS, SEQ // 2, R])
        ones = sb("ones", [128, 1])
        one = sb("one", [R, 1])
        index = sb("index", [R, 2, 2], U32)
        gathered = sb("gathered", [R, 2, 2, E])
        raw_in = sb("raw_in", [R, 2, E])
        ahead = sb("ahead", [R, 2, E])
        residual = sb("residual", [R, 2, E])
        stats = sb("stats", [R, 2, 1, 6])
        mv = sb("mv", [R, 2, 2])
        std = sb("std", [R, 2])
        rstd = sb("rstd", [R, 2])
        normed = gathered[:, :, 0, :]
        normedT_hi = sb("normedT_hi", [128, KE, G2], F32R)
        normedT_lo = sb("normedT_lo", [128, KE, G2], F32R)
        soft = sb("soft", [R, 2, DTL])
        even_part = sb("even_part", [R, 2, HEADS])
        decay_in = sb("decay_in", [R, 2, HEADS])
        level_rows = sb("level_rows", [LROWS, 2, SEQ * HEADS])
        padded = sb("padded", [128, 3, 2 * SPT, SEQ + TAPS - 1])
        conv = sb("conv", [128, 3, 2 * SPT, SEQ])
        xs = sb("xs", [128, CONV_TILES, G2])
        zs = sb("zs", [128, Z_TILES, G2])
        steps = sb("steps", [R, 2, CHUNK * HEADS])
        decay = sb("decay", [R, 2, CHUNK * HEADS])
        weighed = sb("weighed", [R, 2, CHUNK * HEADS])
        qk_all = sb("qk_all", [R, 2, R])
        qk = sb("qk", [R, 2, SEQ])
        att = sb("att", [R, HEADS, 2, SEQ])
        att_block = sb("att_block", [R, 2, GROUP * 2, R])
        vals = sb("vals", [R, 2, 2, GROUP, HD])
        logd, miss = (vals[:, b].rearrange("p t h d -> p t (h d)") for b in range(2))
        dtl, grown = (att_block[:, b].rearrange("p n r -> p (n r)")[:, 0:2 * DTL].rearrange("p (t c) -> p t c", t=2) for b in range(2))
        y = sb("y", [128, 2, 2, G2])
        sumsq = sb("sumsq", [R, 2])
        rms = sb("rms", [R, 2])
        inv_rms = sb("inv_rms", [R, 2])
        result = sb("result", [R, 2, E])

        ps_turned = space.ps(stack, "mx_ps_turned", [128, 512])
        ps_fm = [space.ps(stack, f"mx_ps_fm{b}", [128, 512]) for b in range(2)]
        ps_decay = space.ps(stack, "mx_ps_decay", [128, 512])
        ps_level = space.ps(stack, "mx_ps_level", [128, 512])
        ps_chan = ps_fm + [ps_decay, ps_level]
        ps_dtl = space.ps(stack, "mx_ps_dtl", [128, 512])
        ps_out = [space.ps(stack, f"mx_ps_out{h}", [128, 512]) for h in range(2)]
        SS = KE * G2

        consts = sem("consts")
        padded_zero = sem("padded_zero")
        ones_ready = sem("ones_ready")
        a_ready = sem("a_ready")
        bias_ready = sem("bias_ready")
        index_ready = sem("index_ready")
        gather_done = [[sem(f"gather_done{h}{c}") for c in range(2)] for h in range(2)]
        stream_in = sem("stream_in")
        ahead_ready = sem("ahead_ready")
        residual_ready = sem("residual_ready")
        moments_ready = sem("moments_ready")
        std_ready = sem("std_ready")
        normed_ready = sem("normed_ready")
        turned_ready = sem("turned_ready")
        normedT_ready = sem("normedT_ready")
        dtl_ready = sem("dtl_ready")
        dtl_read = sem("dtl_read")
        tail_ready = sem("tail_ready")
        grown_ready = sem("grown_ready")
        logd_ready = sem("logd_ready")
        act_step = sem("act_step")
        soft_ready = sem("soft_ready")
        lam_stored = sem("lam_stored")
        levels_loaded = sem("levels_loaded")
        decay_in_ready = sem("decay_in_ready")
        fm_ready = sem("fm_ready")
        fm_read = sem("fm_read")
        conv_done = sem("conv_done")
        xs_ready = sem("xs_ready")
        zs_ready = sem("zs_ready")
        steps_ready = sem("steps_ready")
        decay_ps_ready = sem("decay_ps_ready")
        decay_ready = sem("decay_ready")
        qk_ps_ready = sem("qk_ps_ready")
        qk_ready = sem("qk_ready")
        weighed_ready = sem("weighed_ready")
        level_ps_ready = sem("level_ps_ready")
        att_ready = sem("att_ready")
        xT_ready = sem("xT_ready")
        vals_ready = sem("vals_ready")
        block_ready = sem("block_ready")
        y_ps_ready = sem("y_ps_ready")
        y_read = sem("y_read")
        yz_ready = sem("yz_ready")
        squares_ready = sem("squares_ready")
        out_ready = sem("out_ready")
        sumsq_ready = sem("sumsq_ready")
        rms_ready = sem("rms_ready")
        out_read = sem("out_read")
        result_stored = sem("result_stored")
        vec_step = sem("vec_step")
        NC = len(CHUNKS)
        DC = 2 * NC

        const_loads = [(fm_bias[:, :], io["fm_bias"]), (taps[:, :, :], io["taps"]), (skip[:, :], io["skip"]),
                       (dtl_bias[:, :], io["dtl_bias"].partition_broadcast(R)), (dt_bias[:, :], io["dt_bias"].partition_broadcast(R)),
                       (factor[:, HEADS:DTL], io["factor"].partition_broadcast(R)), (a_log[:, :], io["a_log"].partition_broadcast(R)),
                       (out_bias[:, :], io["out_bias"].partition_broadcast(R)), (later[:, :], io["later"]), (upto[:, :], io["upto"]),
                       (causal[:, :], io["causal"]), (block_of[:, :], io["block_of"]), (odd[:, :], io["odd"]),
                       (level_of[:, :, :], io["level_of"])]
        all_consts = 16 * len(const_loads)

        block = stack.enter_context(nc.Block())

        @block.sync
        def _(sp):
            for dst, src in const_loads:
                sp.dma_start(dst, src).then_inc(consts, 16)

            def front_load(i):
                sp.dma_start(raw_in[:, :, :], stream.rearrange("(i t) r e -> i r t e", t=2)[i]).then_inc(stream_in, 16)

            def turn(i, last):
                if not last:
                    sp.wait_ge(ahead_ready, 2 * i + 2)
                    front_load(i + 1)
                sp.wait_ge(soft_ready, i + 1)
                for h in range(2):
                    sp.dma_start(lam_rows[h].rearrange("l r h -> r l h"), soft[:, h, HEADS:DTL].rearrange("r (l h) -> r l h", l=LEVELS)).then_inc(lam_stored, 16)
                sp.wait_ge(lam_stored, 32 * i + 32)
                for h in range(2):
                    sp.dma_start(level_rows[:, h, :], lam_rows[h].rearrange("l (b t) h -> (l b) (t h)", b=SPT)).then_inc(levels_loaded, 16)
                sp.wait_ge(out_read, i + 2)
                sp.dma_start(stream.rearrange("(i t) r e -> i r t e", t=2)[i], result[:, :, :]).then_inc(result_stored, 16)

            front_load(0)
            with sp.Fori(0, PAIRS - 1) as i:
                turn(i, False)
            turn(PAIRS - 1, True)
            sp.wait_ge(result_stored, 16 * (PAIRS + 1))

        @block.gpsimd
        def _(pool):
            pool.memset(padded[:, :, :, :], 0.0).then_inc(padded_zero, 1)
            pool.memset(factor[:, 0:HEADS], 1.0).then_inc(ones_ready, 1)
            pool.memset(one[:, :], 1.0).then_inc(ones_ready, 1)
            pool.memset(ones[:, :], 1.0).then_inc(ones_ready, 1)
            pool.wait_ge(consts, all_consts)
            pool.tensor_tensor(dtl_bias[:, 0:HEADS], dtl_bias[:, 0:HEADS], dt_bias[:, :], ALU.add).then_inc(bias_ready, 1)

            def front_gather(i):
                for h in range(2):
                    for c in range(2):
                        pool.indirect_dma_start(gathered[:, h, c, :], None, expert_rows,
                                                bass.IndirectOffsetOnAxis(ap=index[:, h, c:c + 1], axis=0)).then_inc(gather_done[h][c], 16)

            def turn(i, last):
                pool.wait_ge(ahead_ready, 2 * i + 2)
                if not last:
                    pool.wait_ge(index_ready, i + 2)
                pool.wait_ge(out_read, i + 1)
                pool.tensor_tensor(residual[:, :, :], ahead[:, :, :], out_bias[:, :].unsqueeze(1).broadcast_to([R, 2, E]),
                                   ALU.add).then_inc(residual_ready, 1)
                if not last:
                    front_gather(i + 1)
                pool.wait_ge(decay_in_ready, i + 1)
                for n in range(DC):
                    h, (a, b) = n // NC, CHUNKS[n % NC]
                    cols = (b - a) * HEADS
                    pool.wait_ge(decay_ready, DC * i + n + 1)
                    pool.tensor_tensor(steps[:, n % 2, 0:cols].rearrange("p (t h) -> p t h", h=HEADS),
                                       decay_in[:, h, :].unsqueeze(1).broadcast_to([R, b - a, HEADS]),
                                       upto[:, a:b].unsqueeze(2).broadcast_to([R, b - a, HEADS]), ALU.mult).then_inc(steps_ready, 1)

                    def weigh(n):
                        h, (a, b) = n // NC, CHUNKS[n % NC]
                        cols = (b - a) * HEADS
                        pool.wait_ge(decay_ready, DC * i + n + 3)
                        pool.wait_ge(qk_ready, i + 1)
                        pool.wait_ge(att_ready, DC * i + n + 1)
                        pool.tensor_tensor(weighed[:, n % 2, 0:cols].rearrange("p (t h) -> p t h", h=HEADS),
                                           decay[:, n % 2, 0:cols].rearrange("p (t h) -> p t h", h=HEADS),
                                           qk[:, h, a:b].unsqueeze(2).broadcast_to([R, b - a, HEADS]), ALU.mult).then_inc(weighed_ready, 1)
                    if n >= 1:
                        weigh(n - 1)
                weigh(DC - 1)

            pool.wait_ge(index_ready, 1)
            front_gather(0)
            with pool.Fori(0, PAIRS - 1) as i:
                turn(i, False)
            turn(PAIRS - 1, True)

        @block.scalar
        def _(act):
            act.sem_inc(fm_read, 4)
            act.sem_inc(decay_ready, 2)
            act.wait_ge(consts, all_consts)
            act.activation(a_exp[:, :], a_log[:, :], ACT.Exp).then_inc(a_ready, 1)
            act.wait_ge(padded_zero, 1)
            act.wait_ge(ones_ready, 3)

            def front(i):
                act.wait_ge(moments_ready, 2 * i + 2)
                act.activation(std[:, :], mv[:, :, 1], ACT.Sqrt, bias=eps[:, :]).then_inc(std_ready, 1)

            def turn(i, last):
                act.wait_ge(tail_ready, i + 1)
                act.activation(grown[:, :, :], dtl[:, :, :], ACT.Abs).then_inc(act_step, 1)
                act.wait_ge(act_step, i + 1)
                act.activation(grown[:, :, :], grown[:, :, :], ACT.Exp, scale=-1.0).then_inc(grown_ready, 1)
                act.wait_ge(grown_ready, i + 1)
                act.activation(logd[:, :, :], grown[:, :, :], ACT.Ln, bias=one[:, :]).then_inc(logd_ready, 1)
                for n in range(CONV_TILES + 2):
                    if n < CONV_TILES:
                        q = n if n < 2 else 2 * n - 2
                        act.wait_ge(fm_ready, FM_TILES * i + q + 1)
                        src = ps_chan[q % 4][:, 0:G2].rearrange("p (s t) -> p s t", t=SEQ)
                        act.activation(padded[:, n % 3, :, TAPS - 1:], src, ACT.Identity, bias=fm_bias[:, n:n + 1]).then_inc(fm_read, 1)
                        if n >= 2:
                            q, m = q + 1, n - 2
                            act.wait_ge(fm_ready, FM_TILES * i + q + 1)
                            act.activation(zs[:, m, :], ps_chan[q % 4][:, 0:G2], ACT.Silu,
                                           bias=fm_bias[:, CONV_TILES + m:CONV_TILES + m + 1]).then_inc(fm_read, 1)
                    if n >= 2:
                        act.wait_ge(conv_done, CONV_TILES * i + n - 1)
                        act.activation(xs[:, n - 2, :], conv[:, (n - 2) % 3].rearrange("p s t -> p (s t)"), ACT.Silu).then_inc(xs_ready, 1)
                for n in range(DC):
                    cols = (CHUNKS[n % NC][1] - CHUNKS[n % NC][0]) * HEADS
                    act.wait_ge(decay_ps_ready, DC * i + n + 1)
                    if n >= 2:
                        act.wait_ge(weighed_ready, DC * i + n - 1)
                    act.activation(decay[:, n % 2, 0:cols], ps_decay[0:R, 0:cols], ACT.Exp).then_inc(decay_ready, 1)
                if not last:
                    front(i + 1)
                for g in range(GROUPS):
                    act.wait_ge(yz_ready, GROUPS * i + g + 1)
                    act.activation(y[:, g % 2], zs[:, 2 * g:2 * g + 2, :], ACT.Square).then_inc(squares_ready, 1)
                act.wait_ge(sumsq_ready, i + 1)
                act.activation(rms[:, :], sumsq[:, :], ACT.Sqrt, bias=eps[:, :], scale=1.0 / DIM).then_inc(rms_ready, 1)

            front(0)
            with act.Fori(0, PAIRS - 1) as i:
                turn(i, False)
            turn(PAIRS - 1, True)

        @block.vector
        def _(v):
            step = Chain(v, vec_step, spare)

            def front(i):
                v.tensor_copy(index[:, :, :], slots[:, :, bass.ds(2 * i, 2)].rearrange("p c h -> p h c")).then_inc(index_ready, 1)

            def front_rest(i):
                v.wait_ge(stream_in, 16 * i + 16)
                for h in range(2):
                    v.wait_ge(gather_done[h][0], 16 * i + 16)
                    step(v.scalar_tensor_tensor(ahead[:, h, :], gathered[:, h, 0, :], shares[:, 0, bass.ds(2 * i + h, 1)],
                                                raw_in[:, h, :], ALU.mult, ALU.add))
                    v.wait_ge(gather_done[h][1], 16 * i + 16)
                    v.scalar_tensor_tensor(ahead[:, h, :], gathered[:, h, 1, :], shares[:, 1, bass.ds(2 * i + h, 1)],
                                           ahead[:, h, :], ALU.mult, ALU.add).then_inc(ahead_ready, 1)
                    v.wait_ge(ahead_ready, 2 * i + h + 1)
                    moments(v, step, ahead[:, h, :], stats[:, h], mv[:, h, :]).then_inc(moments_ready, 1)
                v.wait_ge(std_ready, i + 1)
                step(v.reciprocal(rstd[:, :], std[:, :]))
                for h in range(2):
                    normalize(v, normed[:, h, :], ahead[:, h, :], mv[:, h, :], rstd[:, h:h + 1]).then_inc(normed_ready, 1)
                v.wait_ge(turned_ready, i + 1)
                src = ps_turned[:, 0:SS].rearrange("p (k r) -> p k r", k=KE)
                step(v.tensor_copy(normedT_hi[:, :, :], src))
                v.tensor_tensor(normedT_lo[:, :, :], src, normedT_hi[:, :, :].bitcast(F32), ALU.subtract).then_inc(normedT_ready, 1)

            per_turn = 5 + CONV_TILES * 3 + 1 + (2 * 2 + 1 + 1) + 1

            def turn(i, last):
                if not last:
                    front(i + 1)
                v.wait_ge(dtl_ready, i + 1)
                v.tensor_tensor(miss[:, :, :], ps_dtl[0:R, :].rearrange("p (h c) -> p h c", h=2),
                                dtl_bias[:, :].unsqueeze(1).broadcast_to([R, 2, DTL]), ALU.add).then_inc(dtl_read, 1)
                v.wait_ge(dtl_read, i + 1)
                v.tensor_tensor(dtl[:, :, :], miss[:, :, :], factor[:, :].unsqueeze(1).broadcast_to([R, 2, DTL]), ALU.mult).then_inc(tail_ready, 1)
                v.wait_ge(grown_ready, i + 1)
                step(v.tensor_scalar(soft[:, :, :], grown[:, :, :], 1.0, None, ALU.add))
                step(v.scalar_tensor_tensor(miss[:, :, :], soft[:, :, :], -1.0, grown[:, :, :], ALU.add, ALU.subtract))
                v.wait_ge(logd_ready, i + 1)
                step(v.tensor_tensor(miss[:, :, :], logd[:, :, :], miss[:, :, :], ALU.subtract))
                step(v.scalar_tensor_tensor(soft[:, :, :], dtl[:, :, :], 0.0, miss[:, :, :], ALU.max, ALU.add))
                v.scalar_tensor_tensor(decay_in[:, :, :], soft[:, :, 0:HEADS], -1.0, a_exp[:, :].unsqueeze(1).broadcast_to([R, 2, HEADS]),
                                       ALU.mult, ALU.mult).then_inc(decay_in_ready, 1)
                step(v.tensor_scalar(even_part[:, :, :], soft[:, :, 2 * HEADS:3 * HEADS], odd[:, 1:2], None, ALU.mult))
                v.scalar_tensor_tensor(soft[:, :, HEADS:2 * HEADS], soft[:, :, HEADS:2 * HEADS], odd[:, 0:1], even_part[:, :, :],
                                       ALU.mult, ALU.add).then_inc(soft_ready, 1)
                for n in range(CONV_TILES):
                    q = n if n < 2 else 2 * n - 2
                    v.wait_ge(fm_read, FM_TILES * i + q + 1 + 4)
                    src, dst = padded[:, n % 3], conv[:, n % 3]
                    step(v.tensor_scalar(dst, src[:, :, TAPS - 1:TAPS - 1 + SEQ], taps[:, n, TAPS - 1:TAPS], None, ALU.mult))
                    for c in range(TAPS - 1):
                        ins = v.scalar_tensor_tensor(dst, src[:, :, c:c + SEQ], taps[:, n, c:c + 1], dst, ALU.mult, ALU.add)
                        if c < TAPS - 2:
                            step(ins)
                    ins.then_inc(conv_done, 1)
                v.wait_ge(qk_ps_ready, i + 1)
                for h in range(2):
                    ins = v.tensor_tensor(qk_all[:, h, :], ps_out[h][0:R, E:E + R], causal[:, :], ALU.mult)
                step(ins)
                for h in range(2):
                    ins = v.tensor_reduce(qk[:, h, :], qk_all[:, h, :].rearrange("p (b t) -> p t b", b=SPT), AX.X, ALU.add)
                ins.then_inc(qk_ready, 1)
                for n in range(DC):
                    h, (a, b) = n // NC, CHUNKS[n % NC]
                    cols = (b - a) * HEADS
                    v.wait_ge(weighed_ready, DC * i + n + 1)
                    v.wait_ge(level_ps_ready, DC * i + n + 1)
                    v.tensor_tensor(att[:, :, h, a:b].rearrange("p h t -> p t h"),
                                    weighed[:, n % 2, 0:cols].rearrange("p (t h) -> p t h", h=HEADS),
                                    ps_level[0:R, 0:cols].rearrange("p (t h) -> p t h", h=HEADS), ALU.mult).then_inc(att_ready, 1)
                v.wait_ge(residual_ready, i + 1)
                if not last:
                    front_rest(i + 1)
                v.wait_ge(att_ready, DC * (i + 1) + 2)
                for g in range(GROUPS + 1):
                    if g < GROUPS:
                        if g >= 2:
                            v.wait_ge(y_ps_ready, GROUPS * i + g - 1)
                        v.wait_ge(xT_ready, GROUPS * i + g + 1)
                        v.tensor_tensor(vals[:, g % 2], [ps_decay, ps_level][g % 2][0:R, :].rearrange("p (c h d) -> p c h d", c=2, h=GROUP),
                                        soft[:, :, g * GROUP:(g + 1) * GROUP].unsqueeze(3).broadcast_to([R, 2, GROUP, HD]),
                                        ALU.mult).then_inc(vals_ready, 1)
                        v.tensor_tensor(att_block[:, g % 2].rearrange("p n (b t) -> p n b t", b=SPT),
                                        att[:, g * GROUP:(g + 1) * GROUP].rearrange("p h c t -> p (h c) t").unsqueeze(2).broadcast_to([R, 2 * GROUP, SPT, SEQ]),
                                        block_of[:, :].rearrange("p (b t) -> p b t", b=SPT).unsqueeze(1).broadcast_to([R, 2 * GROUP, SPT, SEQ]),
                                        ALU.mult).then_inc(block_ready, 1)
                    if g >= 1:
                        k = g - 1
                        v.wait_ge(y_ps_ready, GROUPS * i + k + 1)
                        for m in range(2):
                            ins = v.scalar_tensor_tensor(y[:, k % 2, m, :], xs[:, 2 + 2 * k + m, :], skip[:, 2 * k + m:2 * k + m + 1],
                                                         ps_fm[k % 2][:, m * G2:(m + 1) * G2], ALU.mult, ALU.add)
                        ins.then_inc(y_read, 1)
                        v.wait_ge(y_read, GROUPS * i + k + 2)
                        v.tensor_tensor(zs[:, 2 * k:2 * k + 2, :], zs[:, 2 * k:2 * k + 2, :], y[:, k % 2], ALU.mult).then_inc(yz_ready, 1)
                v.wait_ge(out_ready, i + 1)
                v.tensor_reduce(sumsq[:, :], ps_turned[0:R, SS:SS + 2 * Z_TILES].rearrange("p (h m) -> p h m", h=2), AX.X, ALU.add).then_inc(sumsq_ready, 1)
                v.wait_ge(rms_ready, i + 1)
                step(v.reciprocal(inv_rms[:, :], rms[:, :]))
                v.wait_ge(result_stored, 16 * (i + 1))
                for h in range(2):
                    ins = v.scalar_tensor_tensor(result[:, h, :], ps_out[h][0:R, 0:E], inv_rms[:, h:h + 1], residual[:, h, :], ALU.mult, ALU.add)
                ins.then_inc(out_read, 1)

            v.sem_inc(att_ready, 2)
            v.sem_inc(y_read, 1)
            v.sem_inc(out_read, 1)
            v.sem_inc(result_stored, 16)
            v.wait_ge(consts, all_consts)
            v.wait_ge(ones_ready, 3)
            v.wait_ge(bias_ready, 1)
            v.wait_ge(a_ready, 1)
            front(0)
            front_rest(0)
            with v.Fori(0, PAIRS - 1) as i:
                step.enter(i, per_turn)
                turn(i, False)
                step.leave(PAIRS - 1, per_turn)
            turn(PAIRS - 1, True)

        @block.tensor
        def _(pe):
            pe.wait_ge(consts, all_consts)
            pe.wait_ge(ones_ready, 3)
            three = lambda hi_a, lo_a, hi_b, lo_b: ((hi_a, hi_b), (hi_a, lo_b), (lo_a, hi_b))

            def front(i):
                pe.wait_ge(normed_ready, 2 * i + 2)
                for k in range(KE):
                    for h in range(2):
                        ins = pe.transpose(ps_turned[:, k * G2 + h * R:k * G2 + (h + 1) * R], normed[:, h, k * 128:(k + 1) * 128], ident[0:R, 0:R])
                ins.then_inc(turned_ready, 1)

            def project(i, q, tile):
                pe.wait_ge(fm_read, FM_TILES * i + q + 1)
                out = ps_chan[q % 4][:, 0:G2]
                for k in range(KE):
                    for c, (w, x) in enumerate(three(w_hi, w_lo, normedT_hi, normedT_lo)):
                        ins = pe.matmul(out, w[:, k, tile * 128:(tile + 1) * 128], x[:, k, :], start=(k == 0 and c == 0), stop=(k == KE - 1 and c == 2))
                ins.then_inc(fm_ready, 1)

            def turn_x(i, g):
                if g == 0:
                    pe.wait_ge(decay_ready, DC * (i + 1) + 2)
                    pe.wait_ge(xs_ready, CONV_TILES * (i + 1))
                if g == 1:
                    pe.wait_ge(att_ready, DC * (i + 1) + 2)
                if g >= 2:
                    pe.wait_ge(vals_ready, GROUPS * i + g - 1)
                out = (ps_decay, ps_level)[g % 2]
                for h in range(2):
                    for m in range(2):
                        ins = pe.transpose(out[0:R, h * 256 + m * 128:h * 256 + (m + 1) * 128], xs[:, 2 + 2 * g + m, h * R:(h + 1) * R], ident[:, :])
                ins.then_inc(xT_ready, 1)

            def heads(i, g):
                pe.wait_ge(vals_ready, GROUPS * i + g + 1)
                pe.wait_ge(block_ready, GROUPS * i + g + 1)
                if g >= 2:
                    pe.wait_ge(y_read, GROUPS * i + g)
                for n in range(GROUP):
                    m, low = divmod(n, 2)
                    for h in range(2):
                        ins = pe.matmul(ps_fm[g % 2][low * HD:(low + 1) * HD, m * G2 + h * R:m * G2 + (h + 1) * R],
                                        vals[:, g % 2, h, n, :], att_block[:, g % 2, 2 * n + h, :], start=True, stop=True)
                ins.then_inc(y_ps_ready, 1)

            def project_out(i, g):
                pe.wait_ge(yz_ready, GROUPS * i + g + 1)
                for m in range(2 * g, 2 * g + 2):
                    for h in range(2):
                        ins = pe.matmul(ps_out[h][0:R, 0:E], zs[:, m, h * R:(h + 1) * R], w_out[:, m, :], start=(m == 0), stop=(m == Z_TILES - 1))
                pe.wait_ge(squares_ready, GROUPS * i + g + 1)
                for m in range(2 * g, 2 * g + 2):
                    for h in range(2):
                        ins = pe.matmul(ps_turned[0:R, SS + h * Z_TILES + m:SS + h * Z_TILES + m + 1], y[:, g % 2, m % 2, h * R:(h + 1) * R],
                                        ones[:, :], start=True, stop=True)
                if g == GROUPS - 1:
                    ins.then_inc(out_ready, 1)

            def turn(i, last):
                pe.wait_ge(normedT_ready, i + 1)
                for h in range(2):
                    for k in range(KE):
                        for c, (x, w) in enumerate(three(normedT_hi, normedT_lo, w_hi, w_lo)):
                            ins = pe.matmul(ps_dtl[0:R, h * DTL:(h + 1) * DTL], x[:, k, h * R:(h + 1) * R], w[:, k, FM_TILES * 128:FM_TILES * 128 + DTL],
                                            start=(k == 0 and c == 0), stop=(k == KE - 1 and c == 2))
                ins.then_inc(dtl_ready, 1)
                pe.wait_ge(y_read, GROUPS * i + 1)
                project(i, 0, 0)
                project(i, 1, 1)
                for m in range(Z_TILES):
                    project(i, 2 + 2 * m, 2 + m)
                    project(i, 3 + 2 * m, CONV_TILES + m)
                pe.wait_ge(xs_ready, CONV_TILES * i + 2)
                pe.wait_ge(out_read, i + 1)
                for h in range(2):
                    ins = pe.matmul(ps_out[h][0:R, E:E + R], xs[:, 0, h * R:(h + 1) * R], xs[:, 1, h * R:(h + 1) * R], start=True, stop=True)
                ins.then_inc(qk_ps_ready, 1)
                pe.wait_ge(fm_read, FM_TILES * (i + 1) + 4)
                pe.wait_ge(levels_loaded, 32 * i + 32)
                for n in range(DC):
                    h, (a, b) = n // NC, CHUNKS[n % NC]
                    cols = (b - a) * HEADS
                    pe.wait_ge(steps_ready, DC * i + n + 1)
                    pe.wait_ge(decay_ready, DC * i + n + 2)
                    pe.matmul(ps_decay[0:R, 0:cols], later[:, :], steps[:, n % 2, 0:cols], start=True, stop=True).then_inc(decay_ps_ready, 1)
                    pe.wait_ge(att_ready, DC * i + n + 2)
                    for m in range(a // 2, b // 2):
                        ins = pe.matmul(ps_level[0:R, (2 * m - a) * HEADS:(2 * m - a + 2) * HEADS], level_of[:, m, :],
                                        level_rows[:, h, 2 * m * HEADS:(2 * m + 2) * HEADS], start=True, stop=True)
                    ins.then_inc(level_ps_ready, 1)
                if not last:
                    front(i + 1)
                for g in range(GROUPS + 2):
                    if g < GROUPS:
                        turn_x(i, g)
                    if 1 <= g <= GROUPS:
                        heads(i, g - 1)
                    if g >= 2:
                        project_out(i, g - 2)

            front(0)
            with pe.Fori(0, PAIRS - 1) as i:
                turn(i, False)
            turn(PAIRS - 1, True)


def share_and_finish(nc, space, io, hidden, normed_all, expert_rows, slots, shares, out, ident):
    INNER = 704
    KD = -(-INNER // 128)
    width = [min(128, INNER - m * 128) for m in range(KD)]
    names = ("swg", "swu")
    with ExitStack() as stack:
        def sb(what, shape, dt=F32):
            return space.sb(stack, f"sh_{what}", shape, dt)

        def sem(what):
            return space.sem(f"sh_{what}")

        up_raw = sb("up_raw", [128, 2, KE, INNER])
        down_raw = sb("down_raw", [128, KD, E])
        up_hi = sb("up_hi", [128, 2, KE, INNER], F32R)
        up_lo = sb("up_lo", [128, 2, KE, INNER], F32R)
        down_hi = sb("down_hi", [128, KD, E], F32R)
        down_lo = sb("down_lo", [128, KD, E], F32R)
        normed = sb("normed", [R, 2, E])
        normedT_hi = sb("normedT_hi", [128, KE, G2], F32R)
        normedT_lo = sb("normedT_lo", [128, KE, G2], F32R)
        silu = sb("silu", [128, KD, G2])
        inner_f = sb("inner_f", [128, KD, G2])
        inner_hi = sb("inner_hi", [128, KD, G2], F32R)
        inner_lo = sb("inner_lo", [128, KD, G2], F32R)
        index = sb("index", [R, 2, 2], U32)
        gathered = sb("gathered", [R, 2, 2, E])
        sums = sb("sums", [R, 2, 2, E])
        result = sb("result", [R, 2, E])
        mark = sb("mark", [1, 2])
        ps_turned = space.ps(stack, "sh_ps_turned", [128, 512])
        RING = 3
        ps_up = [space.ps(stack, f"sh_ps_up{b}", [128, 512]) for b in range(RING)]
        ps_down = [space.ps(stack, f"sh_ps_down{h}", [128, 512]) for h in range(2)]

        loaded = sem("loaded")
        high_done = sem("high_done")
        low_done = sem("low_done")
        normed_ready = sem("normed_ready")
        turned_ready = sem("turned_ready")
        normedT_ready = sem("normedT_ready")
        up_ready = sem("up_ready")
        silu_done = sem("silu_done")
        inner_done = sem("inner_done")
        inner_split = sem("inner_split")
        down_ready = sem("down_ready")
        index_ready = sem("index_ready")
        gather_done = [[sem(f"gather_done{h}{c}") for c in range(2)] for h in range(2)]
        shares_added = sem("shares_added")
        result_ready = sem("result_ready")
        stored = sem("stored")
        marked = sem("marked")
        vec_step = sem("vec_step")

        block = stack.enter_context(nc.Block())

        @block.sync
        def _(sp):
            n = load_rows(sp, loaded, up_raw[:, 0], io["swg"]) + load_rows(sp, loaded, up_raw[:, 1], io["swu"])
            n += load_rows(sp, loaded, down_raw, io["swd"])
            assert n == 4
            with sp.Fori(0, PAIRS - 1) as i:
                sp.wait_ge(result_ready, i + 2)
                sp.dma_start(out[0:(NT - 2) * R].rearrange("(i t r) e -> i r t e", r=R, t=2)[i],
                             result[:, :, :]).then_inc(stored, 16)
            done, end = (NT - 2) * R, BATCH * SEQ
            sp.wait_ge(result_ready, PAIRS + 1)
            sp.dma_start(out[done:done + R], result[:, 0, :]).then_inc(stored, 16)
            sp.dma_start(out[done + R:end], result[0:end - done - R, 1, :]).then_inc(stored, 16)
            sp.wait_ge(stored, 16 * (PAIRS + 2))

        @block.gpsimd
        def _(pool):
            def gather(i):
                for h in range(2):
                    for c in range(2):
                        pool.indirect_dma_start(gathered[:, h, c, :], None, expert_rows,
                                                bass.IndirectOffsetOnAxis(ap=index[:, h, c:c + 1], axis=0)).then_inc(gather_done[h][c], 16)

            pool.memset(mark[:, 0:1], 0.0).then_inc(marked, 1)
            pool.wait_ge(marked, 1)
            with pool.Fori(0, PAIRS) as i:
                pool.wait_ge(index_ready, i + 1)
                pool.tensor_tensor(mark[:, 1:2], mark[:, 0:1], mark[:, 0:1], ALU.add).then_inc(marked, 1)
                gather(i)

        @block.scalar
        def _(act):
            act.wait_ge(loaded, 64)
            act.copy(up_hi[:, :, :, :], up_raw[:, :, :, :])
            for k in range(KD):
                ins = act.copy(down_hi[0:width[k], k, :], down_raw[0:width[k], k, :])
            ins.then_inc(high_done, 1)
            with act.Fori(0, PAIRS) as i:
                for m in range(KD):
                    act.wait_ge(up_ready, KD * i + m + 1)
                    act.activation(silu[0:width[m], m, :], ps_up[m % RING][0:width[m], 0:G2], ACT.Silu).then_inc(silu_done, 1)

        @block.vector
        def _(v):
            step = Chain(v, vec_step)

            def front(i):
                v.tensor_copy(normed[:, :, :], normed_all[:, bass.ds(2 * i, 2), :]).then_inc(normed_ready, 1)

            def turn_rows(i):
                v.wait_ge(turned_ready, i + 1)
                src = ps_turned[:, 0:KE * G2].rearrange("p (k r) -> p k r", k=KE)
                step(v.tensor_copy(normedT_hi[:, :, :], src))
                v.tensor_tensor(normedT_lo[:, :, :], src, normedT_hi[:, :, :].bitcast(F32), ALU.subtract).then_inc(normedT_ready, 1)

            def turn(i, last):
                v.wait_ge(marked, i + 1)
                v.tensor_copy(index[:, :, :], slots[:, :, bass.ds(2 * i, 2)].rearrange("p c h -> p h c")).then_inc(index_ready, 1)
                if not last:
                    front(i + 1)
                for m in range(KD):
                    w = width[m]
                    v.wait_ge(silu_done, KD * i + m + 1)
                    v.tensor_tensor(inner_f[0:w, m, :], silu[0:w, m, :], ps_up[m % RING][0:w, G2:2 * G2], ALU.mult).then_inc(inner_done, 1)
                    v.wait_ge(inner_done, KD * i + m + 1 + RING)
                    step(v.tensor_copy(inner_hi[0:w, m, :], inner_f[0:w, m, :]))
                    v.tensor_tensor(inner_lo[0:w, m, :], inner_f[0:w, m, :], inner_hi[0:w, m, :].bitcast(F32), ALU.subtract).then_inc(inner_split, 1)
                if not last:
                    turn_rows(i + 1)
                for c in range(2):
                    for h in range(2):
                        v.wait_ge(gather_done[h][c], 16 * i + 16)
                        before = hidden[:, 2 * i + h, :] if c == 0 else sums[:, 0, h, :]
                        ins = v.scalar_tensor_tensor(sums[:, c, h, :], gathered[:, h, c, :], shares[:, c, bass.ds(2 * i + h, 1)], before, ALU.mult, ALU.add)
                    step(ins)
                v.wait_ge(down_ready, i + 1)
                v.wait_ge(stored, 16 * i + 16)
                for h in range(2):
                    ins = v.tensor_tensor(result[:, h, :], ps_down[h][0:R, 0:E], sums[:, 1, h, :], ALU.add)
                ins.then_inc(result_ready, 1)

            v.sem_inc(inner_done, RING)
            v.sem_inc(result_ready, 1)
            v.sem_inc(stored, 16)
            v.wait_ge(high_done, 1)
            v.tensor_tensor(up_lo[:, :, :, :].rearrange("p u k n -> p (u k n)"), up_raw[:, :, :, :].rearrange("p u k n -> p (u k n)"),
                            up_hi[:, :, :, :].bitcast(F32).rearrange("p u k n -> p (u k n)"), ALU.subtract)
            for k in range(KD):
                w = width[k]
                ins = v.tensor_tensor(down_lo[0:w, k, :], down_raw[0:w, k, :], down_hi[0:w, k, :].bitcast(F32), ALU.subtract)
            ins.then_inc(low_done, 1)
            front(0)
            turn_rows(0)
            per_turn = KD + 1 + 2
            with v.Fori(0, PAIRS - 1) as i:
                step.enter(i, per_turn)
                turn(i, False)
                step.leave(PAIRS - 1, per_turn)
            turn(PAIRS - 1, True)

        @block.tensor
        def _(pe):
            def front(i):
                pe.wait_ge(normed_ready, i + 1)
                for k in range(KE):
                    for h in range(2):
                        ins = pe.transpose(ps_turned[:, k * G2 + h * R:k * G2 + (h + 1) * R], normed[:, h, k * 128:(k + 1) * 128], ident[0:R, 0:R])
                ins.then_inc(turned_ready, 1)

            def turn(i, last):
                pe.wait_ge(normedT_ready, i + 1)
                for m in range(KD):
                    w = width[m]
                    pe.wait_ge(inner_done, KD * i + m + 1)
                    for u in range(2):
                        for k in range(KE):
                            for c, (wt, xt) in enumerate(((up_hi, normedT_hi), (up_hi, normedT_lo), (up_lo, normedT_hi))):
                                ins = pe.matmul(ps_up[m % RING][0:w, u * G2:(u + 1) * G2], wt[:, u, k, m * 128:m * 128 + w], xt[:, k, :],
                                                start=(k == 0 and c == 0), stop=(k == KE - 1 and c == 2))
                    ins.then_inc(up_ready, 1)
                if not last:
                    front(i + 1)
                pe.wait_ge(result_ready, i + 1)
                for m in range(KD):
                    w = width[m]
                    pe.wait_ge(inner_split, KD * i + m + 1)
                    for h in range(2):
                        for c, (xt, wt) in enumerate(((inner_hi, down_hi), (inner_lo, down_hi), (inner_hi, down_lo))):
                            ins = pe.matmul(ps_down[h][0:R, 0:E], xt[0:w, m, h * R:(h + 1) * R], wt[0:w, m, :],
                                            start=(m == 0 and c == 0), stop=(m == KD - 1 and c == 2))
                ins.then_inc(down_ready, 1)

            pe.wait_ge(low_done, 1)
            front(0)
            with pe.Fori(0, PAIRS - 1) as i:
                turn(i, False)
            turn(PAIRS - 1, True)


def tower(nc, io, out, upto=9):
    with ExitStack() as outer:
        space = Space(nc)
        ident = space.sb(outer, "ident", [128, 128])
        ones_row = space.sb(outer, "ones_row", [1, 128])
        eps = space.sb(outer, "eps", [R, 1])
        spare = space.sb(outer, "spare", [1, 1])
        slots = space.sb(outer, "slots", [R, 2, NT], U32)
        shares = space.sb(outer, "shares", [R, 2, NT])
        jobs = space.sb(outer, "jobs", [1, EXPERTS + 1], I32)
        slot_rows = nc.dram_tensor("slot_rows", (SLOTS, E), F32, kind="Internal").ap()
        expert_rows = nc.dram_tensor("expert_rows", (SLOTS, E), F32, kind="Internal").ap()
        stream = nc.dram_tensor("stream", (NT, R, E), F32, kind="Internal").ap()
        lam_rows = nc.dram_tensor("lam_rows", (2, LEVELS, R, HEADS), F32, kind="Internal").ap()

        with space.part(), ExitStack() as first:
            hidden = space.sb(first, "hidden0", [R, NT, E])
            tokenize(nc, space, io, hidden, [slot_rows, expert_rows], ident, ones_row, eps, spare)
            attend(nc, space, io, hidden, ident, eps, spare)
            with ExitStack() as scope:
                normed_all = space.sb(scope, "normed_all0", [R, NT, E])
                route(nc, space, "r0", io["gate0"], False, hidden, normed_all, slots, shares, jobs, slot_rows, ident, eps, spare)
            move_stream(nc, space, "to_stream", stream.rearrange("t r e -> r t e"), hidden[:, :, :])
        with space.part():
            run_experts(nc, space, "x0", [io["w_in"]], io["b_in"], io["w_out"], io["b_out"], 1024, jobs, slot_rows, expert_rows, ident)
        with space.part(), ExitStack() as scope:
            w_hi = space.sb(scope, "w_hi", [128, KE, FM_TILES * 128 + DTL], F32R)
            w_lo = space.sb(scope, "w_lo", [128, KE, FM_TILES * 128 + DTL], F32R)
            w_out = space.sb(scope, "w_out", [128, Z_TILES, E])
            split_projection(nc, space, io["in_proj"], w_hi, w_lo, io["out_proj"], io["norm_w"], w_out)
            mix_sequences(nc, space, io, stream, expert_rows, slots, shares, w_hi, w_lo, w_out, lam_rows, ident, eps, spare)
        with space.part(), ExitStack() as last:
            hidden = space.sb(last, "hidden1", [R, NT, E])
            normed_all = space.sb(last, "normed_all1", [R, NT, E])
            move_stream(nc, space, "from_stream", hidden[:, :, :], stream.rearrange("t r e -> r t e"))
            route(nc, space, "r1", io["gate1"], True, hidden, normed_all, slots, shares, jobs, slot_rows, ident, eps, spare)
            run_experts(nc, space, "x1", [io["wg"], io["wu"]], None, io["wd"], None, 352, jobs, slot_rows, expert_rows, ident)
            share_and_finish(nc, space, io, hidden, normed_all, expert_rows, slots, shares, out, ident)


def move_stream(nc, space, name, dst, src):
    with ExitStack() as stack:
        moved = space.sem(f"{name}_moved")
        block = stack.enter_context(nc.Block())

        @block.sync
        def _(sp):
            sp.dma_start(dst, src).then_inc(moved, 16)
            sp.wait_ge(moved, 16)


def lay_out(a):
    import numpy as np

    x = np.asarray(a["x"])
    side, size = 6, 16
    patches = x.reshape(BATCH, 3, side, size, side, size).transpose(0, 2, 4, 3, 5, 1).reshape(BATCH, PATCHES, PD)
    tokens = np.zeros((NT * SPT, SEQ, PD), x.dtype)
    tokens[:BATCH, 2:] = patches
    w = {k: np.asarray(v) for k, v in a.items() if k != "x"}

    chan = np.arange(4 * DIM)
    z, xc, bc = chan[0:DIM], chan[DIM:2 * DIM], chan[2 * DIM:2 * DIM + 2 * STATE]
    dt = 2 * DIM + 2 * STATE + np.arange(HEADS)
    all_levels = 15
    level_chan = (2 * DIM + 2 * STATE + HEADS + all_levels * np.arange(HEADS)[None, :]
                  + np.array([1, 0] + list(range(2, LEVELS)))[:, None]).reshape(-1)
    order = np.concatenate([bc, xc, z, dt, level_chan])
    bias = w["L1_attn_in_proj_b"][order]
    conv = np.concatenate([w["L1_attn_conv_w"][DIM:], w["L1_attn_conv_w"][:DIM]])

    seq, pos = np.divmod(np.arange(R), SEQ)
    same = seq[:, None] == seq[None, :]
    later = same & (pos[:, None] > pos[None, :])
    upto = pos[:, None] <= np.arange(SEQ)[None, :]
    causal = same & (pos[:, None] <= pos[None, :])
    odd = np.stack([pos % 2 == 1, pos % 2 == 0], axis=1)
    level_of = np.zeros((LEVELS, SPT, SEQ // 2, SPT, SEQ), bool)
    for m in range(SEQ // 2):
        for key in range(2 * m + 2):
            row = key - 2 * m if key >= 2 * m else (key ^ (2 * m)).bit_length()
            for b in range(SPT):
                level_of[row, b, m, b, key] = True
    flat = {
        "later": later, "upto": upto, "causal": causal, "block_of": same, "odd": odd,
        "level_of": level_of.reshape(LROWS, SEQ // 2, R),
    }
    laid = {
        "patches": tokens.reshape(NT, R, PD),
        "proj": w["L0_tok_W_proj"],
        "proj_bias": w["L0_tok_b_proj"].reshape(1, E),
        "ln1_g": w["L0_tok_ln1_g"].reshape(KP, 128).T,
        "ln1_b": w["L0_tok_ln1_b"].reshape(KP, 128).T,
        "ln2_g": w["L0_tok_ln2_g"],
        "ln2_b": w["L0_tok_ln2_b"],
        "inner_cls": w["L0_tok_cls_token"].reshape(1, E),
        "positions": w["L0_tok_pos_emb"].reshape(PATCHES + 1, E),
        "outer_cls": w["cls_tok"].reshape(1, E),
        "wqT": w["L0_attn_wq"].T,
        "wkT": w["L0_attn_wk"].T,
        "wvT": w["L0_attn_wv"].T,
        "woT": w["L0_attn_wo"].T,
        "gate0": w["L0_ffn_W_gate"],
        "w_in": w["L0_ffn_W_in"],
        "b_in": w["L0_ffn_b_in"].reshape(EXPERTS, -1, 128).transpose(2, 0, 1),
        "w_out": w["L0_ffn_W_out"],
        "b_out": w["L0_ffn_b_out"],
        "in_proj": w["L1_attn_in_proj_w"][order].T,
        "fm_bias": bias[:FM_TILES * 128].reshape(FM_TILES, 128).T,
        "dtl_bias": bias[FM_TILES * 128:],
        "taps": conv.reshape(CONV_TILES, 128, TAPS).transpose(1, 0, 2),
        "dt_bias": w["L1_attn_dt_bias"],
        "factor": w["L1_attn_L"][:, [1, 0] + list(range(2, LEVELS))].T.reshape(-1),
        "a_log": w["L1_attn_A_log"],
        "skip": np.repeat(w["L1_attn_D"], HD).reshape(Z_TILES, 128).T,
        "norm_w": w["L1_attn_norm_w"].reshape(Z_TILES, 128).T,
        "out_proj": w["L1_attn_out_proj_w"].T,
        "out_bias": w["L1_attn_out_proj_b"],
        "gate1": w["L1_ffn_gate_w"].T,
        "wg": w["L1_ffn_wg"],
        "wu": w["L1_ffn_wu"],
        "wd": w["L1_ffn_wd"],
        "swg": w["L1_ffn_swg"],
        "swu": w["L1_ffn_swu"],
        "swd": w["L1_ffn_swd"],
    }
    laid |= {k: np.where(v, np.float32(1), np.float32(0)) for k, v in flat.items()}
    return {k: np.ascontiguousarray(v) for k, v in laid.items()}


def kernel(**inputs):
    import concourse.bacc as bacc
    from concourse.bass_utils import run_bass_kernel_spmd

    nc = bacc.Bacc("TRN2", target_bir_lowering=False, num_devices=1)
    laid = lay_out(inputs)
    io = {k: nc.dram_tensor(f"in_{k}", v.shape, mybir.dt.from_np(v.dtype), kind="ExternalInput").ap() for k, v in laid.items()}
    out = nc.dram_tensor("out", (BATCH * SEQ, E), F32, kind="ExternalOutput").ap()
    tower(nc, io, out)
    r = run_bass_kernel_spmd(nc, [{f"in_{k}": v for k, v in laid.items()}], core_ids=[0])
    return r.results[0]["out"].reshape(BATCH, SEQ, E)
```

```python
import concourse.bass as bass
from concourse import mybir
from contextlib import ExitStack, contextmanager

F32 = mybir.dt.float32
F32R = mybir.dt.float32r
U32 = mybir.dt.uint32
I32 = mybir.dt.int32
ALU = mybir.AluOpType
ACT = mybir.ActivationFunctionType
AX = mybir.AxisListType

BATCH = 64
PATCHES = 36
SEQ = PATCHES + 2
E = 256
KE = E // 128
PD = 3 * 16 * 16
KP = PD // 128
SPT = 3
R = SPT * SEQ
NT = -(-BATCH // SPT)
TOK = NT * R
PAIRS = NT // 2
G2 = 2 * R
LN_EPS = 1e-5
assert NT % 2 == 0 and R <= 128


class Chain:

    def __init__(self, eng, sem, spare=None):
        self.eng, self.sem, self.n, self.base = eng, sem, 0, 0
        self.spare = spare

    def __call__(self, ins, apart=False):
        self.n += 1
        ins.then_inc(self.sem, 1)
        self.eng.wait_ge(self.sem, self.base + self.n)
        if apart:
            self.eng.memset(self.spare[:, :], 0.0)

    def enter(self, turn, per_turn):
        self.start = self.n
        self.base = turn * per_turn

    def leave(self, turns, per_turn):
        assert self.n - self.start == per_turn, (self.n - self.start, per_turn)
        self.base = 0
        self.n = self.start + turns * per_turn


def moments(v, step, x, stats, mv):
    n = x.shape[-1]
    chunk = n // 2 if n > 512 else n
    for c in range(n // chunk):
        ins = v.bn_stats(stats[:, c, :], x[:, c * chunk:(c + 1) * chunk])
    step(ins, apart=True)
    return v.bn_aggr(mv, stats[:, 0:n // chunk, :].rearrange("p c s -> p (c s)"))


def normalize(v, out, x, mv, rstd):
    return v.tensor_scalar(out, x, mv[:, 0:1], rstd, ALU.subtract, ALU.mult)


class Space:

    def __init__(self, nc):
        self.nc, self.sems = nc, []

    @contextmanager
    def part(self):
        yield
        self.nc.clear_and_free_semaphores(self.sems)
        self.nc.all_engine_barrier()
        self.sems = []

    def sb(self, stack, name, shape, dt=F32):
        return stack.enter_context(self.nc.sbuf_tensor(name, shape, dt))

    def sb_twice(self, stack, name, shape, dt, name2, shape2, dt2=F32):
        base = -(-self.nc.sbuf_base // 32) * 32
        first = self.sb(stack, name, shape, dt)
        return first, self.nc.alloc_sbuf_tensor_at(name2, shape2, dt2, offset=base)

    def ps(self, stack, name, shape):
        return stack.enter_context(self.nc.psum_tensor(name, shape, F32))

    def sem(self, name):
        self.sems.append(self.nc.alloc_semaphore(name=name))
        return self.sems[-1]


def tokenize(nc, space, io, hidden, to_clear, ident, ones_row, eps, spare):
    with ExitStack() as stack:
        def sb(name, shape, dt=F32):
            return space.sb(stack, name, shape, dt)

        patches = sb("tk_patches", [R, 2, PD])
        normed = sb("tk_normed", [R, 2, PD])
        normedT = sb("tk_normedT", [128, 2, KP, R])
        proj = sb("tk_proj", [128, KP, E])
        proj_bias = sb("tk_proj_bias", [1, E])
        ln1_g = sb("tk_ln1_g", [128, KP])
        ln1_b = sb("tk_ln1_b", [128, KP])
        gain = sb("tk_gain", [R, E])
        shift = sb("tk_shift", [R, E])
        place = sb("tk_place", [R, E])
        stats = sb("tk_stats", [R, 2, 2, 6])
        z_stats = sb("tk_z_stats", [R, 2, 2, 6])
        mv = sb("tk_mv", [R, 2, 2])
        std = sb("tk_std", [R, 2])
        rstd = sb("tk_rstd", [R, 2])
        mv2 = sb("tk_mv2", [R, 2, 2])
        std2 = sb("tk_std2", [R, 2])
        rstd2 = sb("tk_rstd2", [R, 2])
        z_normed = sb("tk_z_normed", [R, 2, E])
        z_gained = sb("tk_z_gained", [R, 2, E])
        zeros = sb("tk_zeros", [128, 2048])
        turned = [space.ps(stack, f"tk_turned{i}", [128, 2, 512]) for i in range(2)]
        z = [space.ps(stack, f"tk_z{i}", [128, 512]) for i in range(2)]

        const_loaded = space.sem("tk_const_loaded")
        gain_cleared = space.sem("tk_gain_cleared")
        ident_zeroed = space.sem("tk_ident_zeroed")
        ident_ready = space.sem("tk_ident_ready")
        place_ready = space.sem("tk_place_ready")
        patches_loaded = [space.sem(f"tk_patches_loaded{i}") for i in range(2)]
        normed_ready = space.sem("tk_normed_ready")
        turned_ready = space.sem("tk_turned_ready")
        normedT_by_act = space.sem("tk_normedT_by_act")
        normedT_by_vec = space.sem("tk_normedT_by_vec")
        z_ready = space.sem("tk_z_ready")
        z_normed_ready = space.sem("tk_z_normed_ready")
        vec_step = space.sem("tk_vec_step")
        moments_ready = space.sem("tk_moments_ready")
        std_ready = space.sem("tk_std_ready")
        z_moments_ready = space.sem("tk_z_moments_ready")
        z_std_ready = space.sem("tk_z_std_ready")
        gained_ready = space.sem("tk_gained_ready")
        zeros_ready = space.sem("tk_zeros_ready")
        cleared = space.sem("tk_cleared")
        all_const = 16 * (4 + 5 * SPT)

        block = stack.enter_context(nc.Block())

        @block.sync
        def _(sp):
            with sp.Fori(0, PAIRS) as i:
                for half in range(2):
                    sp.wait_ge(normed_ready, 2 * i + half + 1)
                    sp.dma_start(patches[:, half, :], io["patches"][2 * i + half]).then_inc(patches_loaded[half], 16)

        @block.scalar
        def _(act):
            act.dma_start(proj[:, :, :], io["proj"].rearrange("(k p) n -> p k n", p=128)).then_inc(const_loaded, 16)
            act.dma_start(ln1_g[:, :], io["ln1_g"]).then_inc(const_loaded, 16)
            act.dma_start(ln1_b[:, :], io["ln1_b"]).then_inc(const_loaded, 16)
            act.dma_start(proj_bias[:, :], io["proj_bias"]).then_inc(const_loaded, 16)
            act.wait_ge(gain_cleared, 2)
            for s in range(SPT):
                first, rest = s * SEQ, (s + 1) * SEQ
                act.dma_start(gain[first + 2:rest, :], io["ln2_g"].partition_broadcast(PATCHES)).then_inc(const_loaded, 16)
                act.dma_start(shift[first + 2:rest, :], io["ln2_b"].partition_broadcast(PATCHES)).then_inc(const_loaded, 16)
                act.dma_start(shift[first + 1:first + 2, :], io["inner_cls"]).then_inc(const_loaded, 16)
                act.dma_start(place[first + 1:rest, :], io["positions"]).then_inc(const_loaded, 16)
                act.dma_start(place[first:first + 1, :], io["outer_cls"]).then_inc(const_loaded, 16)
            clears = 0
            act.wait_ge(zeros_ready, 1)
            for rows in to_clear:
                view = rows.rearrange("(p s) e -> p (s e)", p=128)
                cols = zeros.shape[1]
                assert view.shape[1] % cols == 0
                for c in range(0, view.shape[1], cols):
                    act.dma_start(view[:, c:c + cols], zeros[:, :]).then_inc(cleared, 16)
                    clears += 1
            act.wait_ge(const_loaded, all_const)
            act.wait_ge(ident_ready, 3)

            def std_of(i, mv, std, count):
                act.wait_ge((moments_ready, z_moments_ready)[count], 2 * i + 2)
                act.activation(std[:, :], mv[:, :, 1], ACT.Sqrt, bias=eps[:, :]).then_inc((std_ready, z_std_ready)[count], 1)

            def turned_high(i):
                for half in range(2):
                    act.wait_ge(turned_ready, 2 * i + half + 1)
                    for k in range(KP // 2, KP):
                        ins = act.activation(normedT[:, half, k, :], turned[half][:, 1, (k - KP // 2) * R:(k - KP // 2 + 1) * R],
                                             ACT.Identity, bias=ln1_b[:, k:k + 1], scale=ln1_g[:, k:k + 1])
                    ins.then_inc(normedT_by_act, 1)

            std_of(0, mv, std, 0)
            turned_high(0)
            with act.Fori(0, PAIRS - 1) as i:
                std_of(i + 1, mv, std, 0)
                std_of(i, mv2, std2, 1)
                turned_high(i + 1)
            std_of(PAIRS - 1, mv2, std2, 1)
            act.wait_ge(cleared, 16 * clears)

        @block.gpsimd
        def _(pool):
            pool.memset(gain[:, :], 0.0).then_inc(gain_cleared, 1)
            pool.memset(shift[:, :], 0.0).then_inc(gain_cleared, 1)
            pool.memset(eps[:, :], LN_EPS).then_inc(ident_ready, 1)
            pool.memset(ones_row[:, :], 1.0).then_inc(ident_ready, 1)
            pool.memset(ident[:, :], 0.0).then_inc(ident_zeroed, 1)
            pool.wait_ge(ident_zeroed, 1)
            pool.affine_select(out=ident[:, :], in_=ident[:, :], compare_op=ALU.not_equal, fill=1.0, base=0,
                               pattern=[[-1, 128]], channel_multiplier=1).then_inc(ident_ready, 1)
            pool.memset(zeros[:, :], 0.0).then_inc(zeros_ready, 1)
            pool.wait_ge(const_loaded, all_const)
            pool.tensor_tensor(place[:, :], place[:, :], shift[:, :], ALU.add).then_inc(place_ready, 1)
            pool.wait_ge(place_ready, 1)
            pool.sem_inc(gained_ready, 2)
            with pool.Fori(0, PAIRS) as i:
                for half in range(2):
                    pool.wait_ge(z_normed_ready, 2 * i + half + 3)
                    pool.tensor_tensor(z_gained[:, half, :], z_normed[:, half, :], gain[:, :], ALU.mult).then_inc(gained_ready, 1)
                    pool.wait_ge(gained_ready, 2 * i + half + 3)
                    pool.tensor_tensor(hidden[:, 2 * i + half, :], z_gained[:, half, :], place[:, :], ALU.add)

        @block.vector
        def _(v):
            step = Chain(v, vec_step, spare)

            def front_normed(i):
                for half in range(2):
                    v.wait_ge(patches_loaded[half], 16 * i + 16)
                    moments(v, step, patches[:, half, :], stats[:, half], mv[:, half, :]).then_inc(moments_ready, 1)
                v.wait_ge(std_ready, i + 1)
                step(v.reciprocal(rstd[:, :], std[:, :]))
                for half in range(2):
                    normalize(v, normed[:, half, :], patches[:, half, :], mv[:, half, :], rstd[:, half:half + 1]).then_inc(normed_ready, 1)

            def turned_low(i, half):
                v.wait_ge(turned_ready, 2 * i + half + 1)
                for k in range(KP // 2):
                    ins = v.tensor_scalar(normedT[:, half, k, :], turned[half][:, 0, k * R:(k + 1) * R],
                                          ln1_g[:, k:k + 1], ln1_b[:, k:k + 1], ALU.mult, ALU.add)
                ins.then_inc(normedT_by_vec, 1)

            def z_moments(i, half):
                v.wait_ge(z_ready, 2 * i + half + 1)
                moments(v, step, z[half][0:R, 0:E], z_stats[:, half], mv2[:, half, :]).then_inc(z_moments_ready, 1)

            def z_normalized(i, half):
                v.wait_ge(gained_ready, 2 * i + half + 1)
                normalize(v, z_normed[:, half, :], z[half][0:R, 0:E], mv2[:, half, :], rstd2[:, half:half + 1]).then_inc(z_normed_ready, 1)

            def turn(i, last):
                if not last:
                    front_normed(i + 1)
                z_moments(i, 0)
                z_moments(i, 1)
                if not last:
                    turned_low(i + 1, 0)
                v.wait_ge(z_std_ready, i + 1)
                step(v.reciprocal(rstd2[:, :], std2[:, :]))
                z_normalized(i, 0)
                if not last:
                    turned_low(i + 1, 1)
                z_normalized(i, 1)

            v.sem_inc(normed_ready, 2)
            v.sem_inc(z_normed_ready, 2)
            v.wait_ge(const_loaded, all_const)
            front_normed(0)
            turned_low(0, 0)
            turned_low(0, 1)
            per_turn = 2 * 2 + 2
            with v.Fori(0, PAIRS - 1) as i:
                step.enter(i, per_turn)
                turn(i, False)
                step.leave(PAIRS - 1, per_turn)
            turn(PAIRS - 1, True)

        @block.tensor
        def _(pe):
            def front_turn(i):
                for half in range(2):
                    pe.wait_ge(normed_ready, 2 * i + half + 3)
                    for k in range(KP):
                        c, j = divmod(k, KP // 2)
                        ins = pe.transpose(turned[half][:, c, j * R:(j + 1) * R], normed[:, half, k * 128:(k + 1) * 128],
                                           ident[0:R, 0:R])
                    ins.then_inc(turned_ready, 1)

            def project(i):
                for half in range(2):
                    pe.wait_ge(normedT_by_act, 2 * i + half + 1)
                    pe.wait_ge(normedT_by_vec, 2 * i + half + 1)
                    pe.wait_ge(z_normed_ready, 2 * i + half + 1)
                    for k in range(KP):
                        pe.matmul(z[half][0:R, 0:E], normedT[:, half, k, :], proj[:, k, :], start=(k == 0), stop=False)
                    pe.matmul(z[half][0:R, 0:E], ones_row[:, 0:R], proj_bias[:, :], start=False, stop=True).then_inc(z_ready, 1)

            pe.wait_ge(ident_ready, 3)
            pe.wait_ge(const_loaded, all_const)
            front_turn(0)
            with pe.Fori(0, PAIRS - 1) as i:
                project(i)
                front_turn(i + 1)
            project(PAIRS - 1)


def attend(nc, space, io, hidden, ident, eps, spare):
    D = 64
    scale = (3.0 / D) ** 0.5
    with ExitStack() as stack:
        def sb(name, shape, dt=F32):
            return space.sb(stack, name, shape, dt)

        wq = sb("at_wq", [128, KE, D])
        wk = sb("at_wk", [128, KE, D])
        wv = sb("at_wv", [128, KE, D])
        wo = sb("at_wo", [D, E])
        same = sb("at_same", [R, R])
        stats = sb("at_stats", [R, 2, 1, 6])
        mv = sb("at_mv", [R, 2, 2])
        std = sb("at_std", [R, 2])
        rstd = sb("at_rstd", [R, 2])
        normed = sb("at_normed", [R, 2, E])
        normedT = sb("at_normedT", [128, 2, KE, R])
        qkT = sb("at_qkT", [D, 2, 2, R])
        vals = sb("at_vals", [R, 2, D])
        scoresT = sb("at_scoresT", [R, 2, R])
        contextT = sb("at_contextT", [D, 2, R])
        ps_turned = [space.ps(stack, f"at_ps_turned{i}", [128, 512]) for i in range(2)]
        ps_qkv = [space.ps(stack, f"at_ps_qkv{i}", [128, 512]) for i in range(2)]
        ps_mix = [space.ps(stack, f"at_ps_mix{i}", [128, 512]) for i in range(2)]
        ps_out = [space.ps(stack, f"at_ps_out{i}", [128, 512]) for i in range(2)]

        loaded = space.sem("at_loaded")
        same_step = space.sem("at_same_step")
        vec_step = space.sem("at_vec_step")
        moments_ready = space.sem("at_moments_ready")
        std_ready = space.sem("at_std_ready")
        normed_ready = space.sem("at_normed_ready")
        turned_ready = space.sem("at_turned_ready")
        normedT_ready = space.sem("at_normedT_ready")
        qkv_ready = space.sem("at_qkv_ready")
        qkv_copied = space.sem("at_qkv_copied")
        scores_ready = space.sem("at_scores_ready")
        scores_masked = space.sem("at_scores_masked")
        context_ready = space.sem("at_context_ready")
        context_copied = space.sem("at_context_copied")
        out_ready = space.sem("at_out_ready")
        added = space.sem("at_added")

        block = stack.enter_context(nc.Block())

        @block.sync
        def _(sp):
            for w, name in ((wq, "wqT"), (wk, "wkT"), (wv, "wvT")):
                sp.dma_start(w[:, :, :], io[name].rearrange("(k p) n -> p k n", p=128)).then_inc(loaded, 16)
            sp.dma_start(wo[:, :], io["woT"]).then_inc(loaded, 16)

        @block.gpsimd
        def _(pool):
            pool.memset(same[:, :], scale).then_inc(same_step, 1)
            pool.wait_ge(same_step, 1)
            cols = same[:, :].rearrange("p (s t) -> p s t", s=SPT)
            pool.affine_select(out=cols, in_=cols, compare_op=ALU.is_ge, fill=0.0, base=0,
                               pattern=[[-SEQ, SPT], [0, SEQ]], channel_multiplier=1).then_inc(same_step, 1)
            pool.wait_ge(same_step, 2)
            pool.affine_select(out=cols, in_=cols, compare_op=ALU.is_ge, fill=0.0, base=SEQ - 1,
                               pattern=[[SEQ, SPT], [0, SEQ]], channel_multiplier=-1).then_inc(same_step, 1)

        @block.vector
        def _(v):
            step = Chain(v, vec_step, spare)

            def front_moments(i):
                for half in range(2):
                    moments(v, step, hidden[:, 2 * i + half, :], stats[:, half], mv[:, half, :]).then_inc(moments_ready, 1)

            def front_normed(i):
                v.wait_ge(std_ready, i + 1)
                step(v.reciprocal(rstd[:, :], std[:, :]))
                for half in range(2):
                    normalize(v, normed[:, half, :], hidden[:, 2 * i + half, :], mv[:, half, :],
                              rstd[:, half:half + 1]).then_inc(normed_ready, 1)

            def turn(i, last):
                if not last:
                    front_moments(i + 1)
                for half in range(2):
                    v.wait_ge(scores_ready, 2 * i + half + 1)
                    v.tensor_tensor(scoresT[:, half, :], ps_mix[half][0:R, 0:R], same[:, :], ALU.mult).then_inc(scores_masked, 1)
                if not last:
                    front_normed(i + 1)
                for half in range(2):
                    v.wait_ge(out_ready, 2 * i + half + 1)
                    v.tensor_tensor(hidden[:, 2 * i + half, :], hidden[:, 2 * i + half, :], ps_out[half][0:R, 0:E],
                                    ALU.add).then_inc(added, 1)

            v.wait_ge(same_step, 3)
            front_moments(0)
            front_normed(0)
            per_turn = 2 + 1
            with v.Fori(0, PAIRS - 1) as i:
                step.enter(i, per_turn)
                turn(i, False)
                step.leave(PAIRS - 1, per_turn)
            turn(PAIRS - 1, True)

        @block.scalar
        def _(act):
            def front_std(i):
                act.wait_ge(moments_ready, 2 * i + 2)
                act.activation(std[:, :], mv[:, :, 1], ACT.Sqrt, bias=eps[:, :]).then_inc(std_ready, 1)

            def front_turned(i):
                for half in range(2):
                    act.wait_ge(turned_ready, 2 * i + half + 1)
                    act.copy(normedT[:, half, :, :].rearrange("p k r -> p (k r)"), ps_turned[half][:, 0:G2]).then_inc(normedT_ready, 1)

            def front_qkv(i):
                for half in range(2):
                    act.wait_ge(qkv_ready, 2 * i + half + 1)
                    act.copy(qkT[:, half, :, :].rearrange("p k r -> p (k r)"), ps_qkv[half][0:D, 0:G2])
                    act.copy(vals[:, half, :], ps_qkv[half][0:R, G2:G2 + D]).then_inc(qkv_copied, 1)

            def turn(i, last):
                if not last:
                    front_std(i + 1)
                    front_turned(i + 1)
                for half in range(2):
                    act.wait_ge(context_ready, 2 * i + half + 1)
                    act.copy(contextT[:, half, :], ps_mix[half][0:D, 128:128 + R]).then_inc(context_copied, 1)
                if not last:
                    front_qkv(i + 1)

            front_std(0)
            front_turned(0)
            front_qkv(0)
            with act.Fori(0, PAIRS - 1) as i:
                turn(i, False)
            turn(PAIRS - 1, True)

        @block.tensor
        def _(pe):
            def front_turn(i):
                for half in range(2):
                    pe.wait_ge(normed_ready, 2 * i + half + 1)
                    for k in range(KE):
                        ins = pe.transpose(ps_turned[half][:, k * R:(k + 1) * R], normed[:, half, k * 128:(k + 1) * 128], ident[0:R, 0:R])
                    ins.then_inc(turned_ready, 1)

            def front_qkv(i):
                for half in range(2):
                    pe.wait_ge(normedT_ready, 2 * i + half + 1)
                    for c, w in enumerate((wq, wk)):
                        for k in range(KE):
                            pe.matmul(ps_qkv[half][0:D, c * R:(c + 1) * R], w[:, k, :], normedT[:, half, k, :],
                                      start=(k == 0), stop=(k == KE - 1))
                    for k in range(KE):
                        ins = pe.matmul(ps_qkv[half][0:R, G2:G2 + D], normedT[:, half, k, :], wv[:, k, :],
                                        start=(k == 0), stop=(k == KE - 1))
                    ins.then_inc(qkv_ready, 1)

            def turn(i, last):
                for half in range(2):
                    pe.wait_ge(qkv_copied, 2 * i + half + 1)
                    pe.matmul(ps_mix[half][0:R, 0:R], qkT[:, half, 1, :], qkT[:, half, 0, :], start=True, stop=True).then_inc(scores_ready, 1)
                if not last:
                    front_turn(i + 1)
                for half in range(2):
                    pe.wait_ge(scores_masked, 2 * i + half + 1)
                    pe.matmul(ps_mix[half][0:D, 128:128 + R], vals[:, half, :], scoresT[:, half, :], start=True, stop=True).then_inc(context_ready, 1)
                if not last:
                    front_qkv(i + 1)
                for half in range(2):
                    pe.wait_ge(context_copied, 2 * i + half + 1)
                    pe.matmul(ps_out[half][0:R, 0:E], contextT[:, half, :], wo[:, :], start=True, stop=True).then_inc(out_ready, 1)

            pe.wait_ge(loaded, 64)
            front_turn(0)
            front_qkv(0)
            with pe.Fori(0, PAIRS - 1) as i:
                turn(i, False)
            turn(PAIRS - 1, True)


EXPERTS = 8
JOB = 256
SUB = JOB // 128
MAX_JOBS = (2 * TOK + EXPERTS * 2 * JOB) // JOB
SLOTS = (MAX_JOBS + 1) * JOB
MOST = -(-TOK // JOB)
BIG = 1e38


def route(nc, space, name, gate_dram, scores_softmaxed, hidden, normed_all, slots, shares, jobs,
          ident, eps, spare):
    with ExitStack() as stack:
        def sb(what, shape, dt=F32):
            return space.sb(stack, f"{name}_{what}", shape, dt)

        def sem(what):
            return space.sem(f"{name}_{what}")

        gate = sb("gate", [128, KE, EXPERTS])
        before = sb("before", [R, R])
        ones = sb("ones", [R, R])
        prefer = sb("prefer", [R, EXPERTS])
        steps_of = sb("steps_of", [R, MOST - 1])
        stats = sb("stats", [R, 2, 1, 6])
        mv = sb("mv", [R, 2, 2])
        std = sb("std", [R, 2])
        rstd = sb("rstd", [R, 2])
        normed_half = sb("normed_half", [R, 2, E])
        normedT = sb("normedT", [128, 2, KE, R])
        scores = sb("scores", [R, NT, EXPERTS])
        rest = sb("rest", [R, NT, EXPERTS])
        equal = sb("equal", [R, NT, EXPERTS])
        chosen = sb("chosen", [R, 2, NT, EXPERTS])
        both = sb("both", [R, NT, EXPERTS])
        top = sb("top", [R, 2, NT])
        pick = sb("pick", [R, 2, NT])
        expd = sb("expd", [R, NT, EXPERTS])
        total = sb("total", [R, NT])
        gap = sb("gap", [R, NT])
        run = sb("run", [R, 2, NT, EXPERTS])
        place = sb("place", [R, NT, EXPERTS])
        over = sb("over", [R, EXPERTS, MOST - 1])
        count = sb("count", [R, EXPERTS])
        ends = sb("ends", [R, 2, EXPERTS])
        first = sb("first", [R, EXPERTS])
        base = sb("base", [R, EXPERTS])
        slot_f = sb("slot_f", [R, 2, NT])
        ps_turned = [space.ps(stack, f"{name}_ps_turned{i}", [128, 512]) for i in range(2)]
        ps_gate = [space.ps(stack, f"{name}_ps_gate{i}", [128, 512]) for i in range(2)]
        ps_before = space.ps(stack, f"{name}_ps_before", [128, 512])
        ps_total = space.ps(stack, f"{name}_ps_total", [128, 512])

        loaded = sem("loaded")
        consts = sem("consts")
        const_step = sem("const_step")
        vec_step = sem("vec_step")
        moments_ready = sem("moments_ready")
        std_ready = sem("std_ready")
        normed_ready = sem("normed_ready")
        turned_ready = sem("turned_ready")
        normedT_ready = sem("normedT_ready")
        gate_ready = sem("gate_ready")
        gate_read = sem("gate_read")
        exp_in = sem("exp_in")
        exp_out = sem("exp_out")
        both_ready = sem("both_ready")
        counted = sem("counted")

        block = stack.enter_context(nc.Block())

        @block.sync
        def _(sp):
            sp.dma_start(gate[:, :, :], gate_dram.rearrange("(k p) n -> p k n", p=128)).then_inc(loaded, 16)

        @block.gpsimd
        def _(pool):
            pool.memset(ones[:, :], 1.0).then_inc(consts, 1)
            pool.memset(before[:, :], 1.0).then_inc(const_step, 1)
            for e in range(EXPERTS):
                ins = pool.memset(prefer[:, e:e + 1], float(EXPERTS - e))
            ins.then_inc(consts, 1)
            for c in range(MOST - 1):
                ins = pool.memset(steps_of[:, c:c + 1], float(JOB * (c + 1)))
            ins.then_inc(consts, 1)
            pool.wait_ge(const_step, 1)
            pool.affine_select(out=before[:, :], in_=before[:, :], compare_op=ALU.is_ge, fill=0.0, base=-1,
                               pattern=[[1, R]], channel_multiplier=-1).then_inc(consts, 1)

        @block.tensor
        def _(pe):
            pe.wait_ge(loaded, 16)
            with pe.Fori(0, PAIRS) as i:
                for half in range(2):
                    pe.wait_ge(normed_ready, 2 * i + half + 1)
                    for k in range(KE):
                        ins = pe.transpose(ps_turned[half][:, k * R:(k + 1) * R], normed_half[:, half, k * 128:(k + 1) * 128],
                                           ident[0:R, 0:R])
                    ins.then_inc(turned_ready, 1)
                for half in range(2):
                    pe.wait_ge(normedT_ready, 2 * i + half + 1)
                    for k in range(KE):
                        ins = pe.matmul(ps_gate[half][0:R, 0:EXPERTS], normedT[:, half, k, :], gate[:, k, :],
                                        start=(k == 0), stop=(k == KE - 1))
                    ins.then_inc(gate_ready, 1)
            pe.wait_ge(both_ready, 1)
            pe.wait_ge(consts, 4)
            flat = both[:, :, :].rearrange("p t e -> p (t e)")
            pe.matmul(ps_before[0:R, 0:NT * EXPERTS], before[:, :], flat, start=True, stop=True)
            pe.matmul(ps_total[0:R, 0:NT * EXPERTS], ones[:, :], flat, start=True, stop=True).then_inc(counted, 1)

        @block.scalar
        def _(act):
            with act.Fori(0, PAIRS) as i:
                act.wait_ge(moments_ready, 2 * i + 2)
                act.activation(std[:, :], mv[:, :, 1], ACT.Sqrt, bias=eps[:, :]).then_inc(std_ready, 1)
                for half in range(2):
                    act.wait_ge(turned_ready, 2 * i + half + 1)
                    act.copy(normedT[:, half, :, :].rearrange("p k r -> p (k r)"), ps_turned[half][:, 0:G2]).then_inc(normedT_ready, 1)
            act.wait_ge(exp_in, 1)
            if scores_softmaxed:
                act.activation(expd[:, :, :], rest[:, :, :], ACT.Exp).then_inc(exp_out, 1)
            else:
                act.activation(total[:, :], gap[:, :], ACT.Exp).then_inc(exp_out, 1)

        @block.vector
        def _(v):
            step = Chain(v, vec_step, spare)
            per_turn = 2 + 1
            with v.Fori(0, PAIRS) as i:
                step.enter(i, per_turn)
                for half in range(2):
                    moments(v, step, hidden[:, 2 * i + half, :], stats[:, half], mv[:, half, :]).then_inc(moments_ready, 1)
                v.wait_ge(std_ready, i + 1)
                step(v.reciprocal(rstd[:, :], std[:, :]))
                for half in range(2):
                    normalize(v, normed_half[:, half, :], hidden[:, 2 * i + half, :], mv[:, half, :],
                              rstd[:, half:half + 1]).then_inc(normed_ready, 1)
                    v.wait_ge(normed_ready, 2 * i + half + 1)
                    v.tensor_copy(normed_all[:, 2 * i + half, :], normed_half[:, half, :])
                for half in range(2):
                    v.wait_ge(gate_ready, 2 * i + half + 1)
                    v.tensor_copy(scores[:, 2 * i + half, :], ps_gate[half][0:R, 0:EXPERTS]).then_inc(gate_read, 1)
                step.leave(PAIRS, per_turn)
            v.wait_ge(gate_read, NT)
            v.wait_ge(consts, 4)

            def per_token(x):
                return x.unsqueeze(2).broadcast_to([R, NT, EXPERTS])

            def per_expert(x):
                return x.unsqueeze(1).broadcast_to([R, NT, EXPERTS])

            if scores_softmaxed:
                step(v.tensor_reduce(top[:, 0, :], scores[:, :, :], AX.X, ALU.max))
                v.tensor_tensor(rest[:, :, :], scores[:, :, :], per_token(top[:, 0, :]), ALU.subtract).then_inc(exp_in, 1)
                v.wait_ge(exp_out, 1)
                step(v.tensor_reduce(total[:, :], expd[:, :, :], AX.X, ALU.add))
                step(v.reciprocal(gap[:, :], total[:, :]))
                step(v.tensor_tensor(scores[:, :, :], expd[:, :, :], per_token(gap[:, :]), ALU.mult))
            for c, values in enumerate((scores, rest)):
                step(v.tensor_reduce(top[:, c, :], values[:, :, :], AX.X, ALU.max))
                step(v.tensor_tensor(equal[:, :, :], values[:, :, :], per_token(top[:, c, :]), ALU.is_equal))
                step(v.tensor_tensor(place[:, :, :], equal[:, :, :], per_expert(prefer[:, :]), ALU.mult))
                step(v.tensor_reduce(pick[:, c, :], place[:, :, :], AX.X, ALU.max))
                step(v.tensor_tensor(chosen[:, c], per_expert(prefer[:, :]), per_token(pick[:, c, :]), ALU.is_equal))
                if c == 0:
                    step(v.scalar_tensor_tensor(rest[:, :, :].rearrange("p t e -> p (t e)"),
                                                chosen[:, 0].rearrange("p t e -> p (t e)"), -BIG,
                                                scores[:, :, :].rearrange("p t e -> p (t e)"), ALU.mult, ALU.add))
            v.tensor_tensor(both[:, :, :], chosen[:, 0], chosen[:, 1], ALU.add).then_inc(both_ready, 1)
            if scores_softmaxed:
                step(v.scalar_tensor_tensor(total[:, :], top[:, 0, :], 1e-20, top[:, 1, :], ALU.add, ALU.add))
                step(v.reciprocal(gap[:, :], total[:, :]))
                step(v.tensor_tensor(shares[:, 0, :], top[:, 0, :], gap[:, :], ALU.mult))
                step(v.tensor_tensor(shares[:, 1, :], top[:, 1, :], gap[:, :], ALU.mult))
            else:
                v.tensor_tensor(gap[:, :], top[:, 1, :], top[:, 0, :], ALU.subtract).then_inc(exp_in, 1)
                v.wait_ge(exp_out, 1)
                step(v.tensor_scalar(pick[:, 0, :], total[:, :], 1.0, None, ALU.add))
                step(v.reciprocal(shares[:, 0, :], pick[:, 0, :]))
                step(v.tensor_tensor(shares[:, 1, :], total[:, :], shares[:, 0, :], ALU.mult))
            v.wait_ge(counted, 1)
            step(v.tensor_copy(run[:, 0].rearrange("p t e -> p (t e)"), ps_total[0:R, 0:NT * EXPERTS]))
            now, reach = 0, 1
            while reach < NT:
                a, b = run[:, now], run[:, 1 - now]
                step(v.tensor_copy(b[:, 0:reach, :], a[:, 0:reach, :]))
                step(v.tensor_tensor(b[:, reach:NT, :], a[:, reach:NT, :], a[:, 0:NT - reach, :], ALU.add))
                now, reach = 1 - now, 2 * reach
            runs = run[:, now]
            step(v.tensor_tensor(over[:, :, :], runs[:, NT - 1, :].unsqueeze(2).broadcast_to([R, EXPERTS, MOST - 1]),
                                 steps_of[:, :].unsqueeze(1).broadcast_to([R, EXPERTS, MOST - 1]), ALU.is_gt))
            step(v.tensor_reduce(count[:, :], over[:, :, :], AX.X, ALU.add))
            step(v.tensor_scalar(count[:, :], count[:, :], 1.0, 2.0, ALU.add, ALU.max))
            step(v.tensor_copy(ends[:, 0, :], count[:, :]))
            now2, reach = 0, 1
            while reach < EXPERTS:
                a, b = ends[:, now2], ends[:, 1 - now2]
                step(v.tensor_copy(b[:, 0:reach], a[:, 0:reach]))
                step(v.tensor_tensor(b[:, reach:EXPERTS], a[:, reach:EXPERTS], a[:, 0:EXPERTS - reach], ALU.add))
                now2, reach = 1 - now2, 2 * reach
            step(v.tensor_tensor(first[:, :], ends[:, now2], count[:, :], ALU.subtract))
            step(v.tensor_copy(jobs[:, 0:EXPERTS], first[0:1, :]))
            step(v.tensor_copy(jobs[:, EXPERTS:EXPERTS + 1], ends[0:1, now2, EXPERTS - 1:EXPERTS]))
            step(v.tensor_scalar(base[:, :], first[:, :], float(JOB), None, ALU.mult))
            step(v.tensor_tensor(place[:, :, :].rearrange("p t e -> p (t e)"), ps_before[0:R, 0:NT * EXPERTS],
                                 runs.rearrange("p t e -> p (t e)"), ALU.add))
            step(v.tensor_tensor(place[:, :, :].rearrange("p t e -> p (t e)"), place[:, :, :].rearrange("p t e -> p (t e)"),
                                 ps_total[0:R, 0:NT * EXPERTS], ALU.subtract))
            step(v.tensor_tensor(place[:, :, :], place[:, :, :], per_expert(base[:, :]), ALU.add))
            for c in range(2):
                step(v.tensor_tensor(equal[:, :, :], chosen[:, c], place[:, :, :], ALU.mult))
                step(v.tensor_reduce(slot_f[:, c, :], equal[:, :, :], AX.X, ALU.add))
                v.tensor_copy(slots[:, c, :], slot_f[:, c, :])


def load_rows(eng, sem, tile, dram):
    rows = dram.shape[0]
    whole = rows // 128
    n = 1
    eng.dma_start(tile[:, 0:whole, :], dram[0:whole * 128].rearrange("(k p) n -> p k n", p=128)).then_inc(sem, 16)
    if rows % 128:
        eng.dma_start(tile[0:rows % 128, whole, :], dram[whole * 128:rows]).then_inc(sem, 16)
        n += 1
    return n


def run_experts(nc, space, name, ups_dram, up_bias_dram, down_dram, down_bias_dram, inner, jobs, slot_rows, out_rows, ident):
    gated = len(ups_dram) == 2
    KD = -(-inner // 128)
    width = [min(128, inner - m * 128) for m in range(KD)]
    U = len(ups_dram)
    with ExitStack() as stack:
        def sb(what, shape, dt=F32):
            return space.sb(stack, f"{name}_{what}", shape, dt)

        def sem(what):
            return space.sem(f"{name}_{what}")

        up_raw = sb("up_raw", [128, U, KE, inner])
        down_raw = sb("down_raw", [128, KD, E])
        up_hi = [sb(f"up_hi{p}", [128, U, KE, inner], F32R) for p in range(2)]
        up_lo = [sb(f"up_lo{p}", [128, U, KE, inner], F32R) for p in range(2)]
        down_hi = [sb(f"down_hi{p}", [128, KD, E], F32R) for p in range(2)]
        down_lo = [sb(f"down_lo{p}", [128, KD, E], F32R) for p in range(2)]
        if not gated:
            up_bias = sb("up_bias", [128, EXPERTS, KD])
            down_bias = [sb(f"down_bias{p}", [128, E]) for p in range(2)]
        rows = sb("rows", [128, SUB, E])
        rowsT_hi = sb("rowsT_hi", [128, KE, JOB], F32R)
        rowsT_lo = sb("rowsT_lo", [128, KE, JOB], F32R)
        RING = 4 if not gated else KD
        act_out = sb("act_out", [128, RING, JOB])
        inner_f = sb("inner_f", [128, KD, JOB]) if gated else act_out
        inner_hi = sb("inner_hi", [128, KD, JOB], F32R)
        inner_lo = sb("inner_lo", [128, KD, JOB], F32R)
        result = sb("result", [128, SUB, E])
        ps_rowsT = space.ps(stack, f"{name}_ps_rowsT", [128, KE, JOB])
        BANKS = 4 if not gated else KD
        ps_up = [space.ps(stack, f"{name}_ps_up{b}", [128, 512]) for b in range(BANKS)]
        ps_down = [space.ps(stack, f"{name}_ps_down{s}", [128, 512]) for s in range(SUB)]

        raw_loaded = sem("raw_loaded")
        bias_loaded = [sem(f"bias_loaded{p}") for p in range(2)]
        up_bias_loaded = sem("up_bias_loaded")
        weights_by_act = sem("weights_by_act")
        weights_by_vec = sem("weights_by_vec")
        rows_loaded = sem("rows_loaded")
        rowsT_ready = sem("rowsT_ready")
        rowsT_hi_ready = sem("rowsT_hi_ready")
        rowsT_split = sem("rowsT_split")
        up_ready = sem("up_ready")
        act_done = sem("act_done")
        inner_done = sem("inner_done")
        inner_hi_done = sem("inner_hi_done")
        inner_split = sem("inner_split")
        down_ready = sem("down_ready")
        result_ready = sem("result_ready")
        result_stored = sem("result_stored")
        raw_dmas = U + (2 if inner % 128 else 1)

        def expert_jobs(eng, e):
            first, end = (eng.value_load(jobs[0:1, n:n + 1], min_val=2 * n, max_val=MAX_JOBS - 2 * (EXPERTS - n))
                          for n in (e, e + 1))
            return first, end

        block = stack.enter_context(nc.Block())

        @block.sync
        def _(sp):
            def load_weights(e):
                if e >= 1:
                    sp.wait_ge(weights_by_act, e)
                    sp.wait_ge(weights_by_vec, e)
                n = 0
                for u, dram in enumerate(ups_dram):
                    n += load_rows(sp, raw_loaded, up_raw[:, u], dram[e])
                n += load_rows(sp, raw_loaded, down_raw, down_dram[e])
                assert n == raw_dmas

            def load_bias(e):
                if not gated:
                    sp.dma_start(down_bias[e % 2][:, :], down_bias_dram[e].partition_broadcast(128)).then_inc(bias_loaded[e % 2], 16)

            def load_rows_of(job):
                sp.dma_start(rows[:, :, :], slot_rows.rearrange("(j s p) e -> j p s e", s=SUB, p=128)[job]).then_inc(rows_loaded, 16)

            def one_job(j):
                sp.wait_ge(rowsT_ready, j + 1)
                load_rows_of(j + 1)

            def store(j):
                sp.wait_ge(result_ready, j + 2)
                sp.dma_start(out_rows.rearrange("(j s p) e -> j p s e", s=SUB, p=128)[j], result[:, :, :]).then_inc(result_stored, 16)

            load_weights(0)
            if not gated:
                sp.dma_start(up_bias[:, :, :], up_bias_dram).then_inc(up_bias_loaded, 16)
            load_bias(0)
            load_rows_of(0)
            load_weights(1)
            for e in range(EXPERTS):
                first, end = expert_jobs(sp, e)
                one_job(first)
                store(first)
                if e + 1 < EXPERTS:
                    load_bias(e + 1)
                if e + 2 < EXPERTS:
                    load_weights(e + 2)
                with sp.Fori(first + 1, end) as j:
                    one_job(j)
                    store(j)

        @block.gpsimd
        def _(pool):
            _, end = expert_jobs(pool, EXPERTS - 1)
            pool.wait_ge(result_stored, 16 * (end + 1))

        @block.scalar
        def _(act):
            def split_high(e, part, parts):
                p = e % 2
                for u in range(U):
                    for k in range(KE):
                        a, b = inner * part // parts, inner * (part + 1) // parts
                        ins = act.copy(up_hi[p][:, u, k, a:b], up_raw[:, u, k, a:b])
                a, b = KD * part // parts, KD * (part + 1) // parts
                for k in range(a, b):
                    ins = act.copy(down_hi[p][0:width[k], k, :], down_raw[0:width[k], k, :])
                if part == parts - 1:
                    ins.then_inc(weights_by_act, 1)

            def one_job(e, j, split_next):
                for m in range(KD):
                    act.wait_ge(up_ready, KD * j + m + 1)
                    r = m % RING
                    if gated:
                        act.activation(act_out[0:width[m], r, :], ps_up[m][0:width[m], 0:JOB], ACT.Silu).then_inc(act_done, 1)
                    else:
                        act.activation(act_out[:, r, :], ps_up[m % BANKS][:, 0:JOB], ACT.Gelu, bias=up_bias[:, e, m:m + 1]).then_inc(act_done, 1)
                    if split_next:
                        if m == 0:
                            act.wait_ge(raw_loaded, 16 * raw_dmas * (e + 2))
                        split_high(e + 1, m, KD)

            act.wait_ge(raw_loaded, 16 * raw_dmas)
            split_high(0, 0, 1)
            if not gated:
                act.wait_ge(up_bias_loaded, 16)
            for e in range(EXPERTS):
                first, end = expert_jobs(act, e)
                one_job(e, first, e + 1 < EXPERTS)
                with act.Fori(first + 1, end) as j:
                    one_job(e, j, False)

        @block.vector
        def _(v):
            def split_low(e, part, parts):
                p = e % 2
                for u in range(U):
                    a, b = inner * part // parts, inner * (part + 1) // parts
                    v.tensor_tensor(up_lo[p][:, u, :, a:b], up_raw[:, u, :, a:b], up_hi[p][:, u, :, a:b].bitcast(F32), ALU.subtract)
                a, b = KD * part // parts, KD * (part + 1) // parts
                for k in range(a, b):
                    w = width[k]
                    ins = v.tensor_tensor(down_lo[p][0:w, k, :], down_raw[0:w, k, :], down_hi[p][0:w, k, :].bitcast(F32), ALU.subtract)
                if part == parts - 1:
                    ins.then_inc(weights_by_vec, 1)

            def turn_rows(j):
                v.wait_ge(rowsT_ready, j + 1)
                v.tensor_copy(rowsT_hi[:, :, :], ps_rowsT[:, :, :]).then_inc(rowsT_hi_ready, 1)
                v.wait_ge(rowsT_hi_ready, j + 1)
                v.tensor_tensor(rowsT_lo[:, :, :], ps_rowsT[:, :, :], rowsT_hi[:, :, :].bitcast(F32), ALU.subtract).then_inc(rowsT_split, 1)

            def one_job(e, j, split_next):
                for m in range(KD):
                    w, n = width[m], KD * j + m + 1
                    v.wait_ge(act_done, n)
                    if gated:
                        v.tensor_tensor(inner_f[0:w, m, :], act_out[0:w, m, :], ps_up[m][0:w, JOB:2 * JOB], ALU.mult).then_inc(inner_done, 1)
                        v.wait_ge(inner_done, n)
                    source = inner_f[0:w, m % RING, :]
                    v.tensor_copy(inner_hi[0:w, m, :], source).then_inc(inner_hi_done, 1)
                    v.wait_ge(inner_hi_done, n)
                    v.tensor_tensor(inner_lo[0:w, m, :], source, inner_hi[0:w, m, :].bitcast(F32), ALU.subtract).then_inc(inner_split, 1)
                    if split_next and m >= 1:
                        if m == KD - 1:
                            v.wait_ge(weights_by_act, e + 2)
                            split_low(e + 1, 0, 1)
                turn_rows(j + 1)
                v.wait_ge(down_ready, j + 1)
                v.wait_ge(result_stored, 16 * (j + 1))
                for s in range(SUB):
                    if gated:
                        ins = v.tensor_copy(result[:, s, :], ps_down[s][:, 0:E])
                    else:
                        if s == 0:
                            v.wait_ge(bias_loaded[e % 2], 16 * (e // 2 + 1))
                        ins = v.tensor_tensor(result[:, s, :], ps_down[s][:, 0:E], down_bias[e % 2][:, :], ALU.add)
                ins.then_inc(result_ready, 1)

            v.sem_inc(inner_split, RING)
            v.sem_inc(result_ready, 1)
            v.sem_inc(result_stored, 16)
            v.wait_ge(weights_by_act, 1)
            split_low(0, 0, 1)
            turn_rows(0)
            for e in range(EXPERTS):
                first, end = expert_jobs(v, e)
                one_job(e, first, e + 1 < EXPERTS)
                with v.Fori(first + 1, end) as j:
                    one_job(e, j, False)

        @block.tensor
        def _(pe):
            def turn_rows(j):
                pe.wait_ge(rows_loaded, 16 * (j + 1))
                for k in range(KE):
                    for s in range(SUB):
                        ins = pe.transpose(ps_rowsT[:, k, s * 128:(s + 1) * 128], rows[:, s, k * 128:(k + 1) * 128], ident[:, :])
                ins.then_inc(rowsT_ready, 1)

            def one_job(e, j):
                p = e % 2
                pe.wait_ge(rowsT_split, j + 1)
                for m in range(KD):
                    w = width[m]
                    pe.wait_ge(inner_split, KD * j + m + 1)
                    for u in range(U):
                        out = ps_up[m % BANKS][0:w, u * JOB:(u + 1) * JOB]
                        for k in range(KE):
                            for c, (wt, xt) in enumerate(((up_hi, rowsT_hi), (up_hi, rowsT_lo), (up_lo, rowsT_hi))):
                                ins = pe.matmul(out, wt[p][:, u, k, m * 128:m * 128 + w], xt[:, k, :],
                                                start=(k == 0 and c == 0), stop=(k == KE - 1 and c == 2))
                    ins.then_inc(up_ready, 1)
                turn_rows(j + 1)
                pe.wait_ge(result_ready, j + 1)
                for m in range(KD):
                    w = width[m]
                    pe.wait_ge(inner_split, KD * j + m + 1 + RING)
                    for s in range(SUB):
                        for c, (xt, wt) in enumerate(((inner_hi, down_hi), (inner_lo, down_hi), (inner_hi, down_lo))):
                            ins = pe.matmul(ps_down[s][:, 0:E], xt[0:w, m, s * 128:(s + 1) * 128], wt[p][0:w, m, :],
                                            start=(m == 0 and c == 0), stop=(m == KD - 1 and c == 2))
                ins.then_inc(down_ready, 1)

            turn_rows(0)
            for e in range(EXPERTS):
                first, end = expert_jobs(pe, e)
                pe.wait_ge(weights_by_act, e + 1)
                pe.wait_ge(weights_by_vec, e + 1)
                one_job(e, first)
                with pe.Fori(first + 1, end) as j:
                    one_job(e, j)


HEADS = 32
HD = 64
DIM = HEADS * HD
STATE = 128
LEVELS = 7
TAPS = 4
CONV_TILES = (2 * STATE + DIM) // 128
Z_TILES = DIM // 128
FM_TILES = CONV_TILES + Z_TILES
DTL = HEADS * (1 + LEVELS)
GROUP = 4
GROUPS = HEADS // GROUP
LROWS = 2 * LEVELS * SPT
CHUNK = 16
CHUNKS = [(a, min(a + CHUNK, SEQ)) for a in range(0, SEQ, CHUNK)]
assert 1 + (SEQ - 1).bit_length() == LEVELS and DTL == 256 and SEQ % 2 == 0
RMS_EPS = 1e-5


def split_and_scatter(nc, space, in_dram, w_hi, w_lo, out_dram, norm_dram, w_out, slots, normed_all, slot_rows, hidden, stream):
    with ExitStack() as stack:
        N = FM_TILES * 128 + DTL
        COLS = 512
        CH = N // COLS
        assert CH * COLS == N
        raw = [space.sb(stack, f"sp_raw{p}", [128, KE, COLS]) for p in range(2)]
        norm = space.sb(stack, "sp_norm", [128, Z_TILES])
        raw_out = space.sb(stack, "sp_raw_out", [128, Z_TILES, E])
        loaded = [space.sem(f"sp_loaded{p}") for p in range(2)]
        out_loaded = space.sem("sp_out_loaded")
        high_done = space.sem("sp_high_done")
        low_done = space.sem("sp_low_done")
        scattered = space.sem("sp_scattered")
        stream_stored = space.sem("sp_stream_stored")
        block = stack.enter_context(nc.Block())
        view = in_dram.rearrange("(k p) n -> p k n", p=128)

        @block.gpsimd
        def _(pool):
            scatter_rows(pool, scattered, slots, normed_all, slot_rows)

        @block.sync
        def _(sp):
            sp.dma_start(stream.rearrange("t r e -> r t e"), hidden[:, :, :]).then_inc(stream_stored, 16)
            for c in range(CH):
                if c >= 2:
                    sp.wait_ge(low_done, c - 1)
                sp.dma_start(raw[c % 2][:, :, :], view[:, :, c * COLS:(c + 1) * COLS]).then_inc(loaded[c % 2], 16)
                if c == 1:
                    sp.dma_start(norm[:, :], norm_dram).then_inc(out_loaded, 16)
                    sp.dma_start(raw_out[:, :, :], out_dram.rearrange("(m p) n -> p m n", p=128)).then_inc(out_loaded, 16)
            sp.wait_ge(stream_stored, 16)

        @block.scalar
        def _(act):
            for c in range(CH):
                act.wait_ge(loaded[c % 2], 16 * (c // 2 + 1))
                act.copy(w_hi[:, :, c * COLS:(c + 1) * COLS], raw[c % 2][:, :, :]).then_inc(high_done, 1)
            act.wait_ge(out_loaded, 32)
            for m in range(Z_TILES):
                act.activation(w_out[:, m, :], raw_out[:, m, :], ACT.Copy, scale=norm[:, m:m + 1])

        @block.vector
        def _(v):
            for c in range(CH):
                v.wait_ge(high_done, c + 1)
                part = slice(c * COLS, (c + 1) * COLS)
                v.tensor_tensor(w_lo[:, :, part], raw[c % 2][:, :, :], w_hi[:, :, part].bitcast(F32), ALU.subtract).then_inc(low_done, 1)


def mix_sequences(nc, space, io, stream, expert_rows, slots, shares, w_hi, w_lo, w_out, lam_rows, ident, eps, spare):
    with ExitStack() as stack:
        def sb(what, shape, dt=F32):
            return space.sb(stack, f"mx_{what}", shape, dt)

        def sem(what):
            return space.sem(f"mx_{what}")

        RING = 4
        STEPS = 3

        fm_bias = sb("fm_bias", [128, FM_TILES])
        taps = sb("taps", [128, CONV_TILES, TAPS])
        skip = sb("skip", [128, Z_TILES])
        dtl_bias = sb("dtl_bias", [R, DTL])
        dt_bias = sb("dt_bias", [R, HEADS])
        factor = sb("factor", [R, DTL])
        a_log = sb("a_log", [R, HEADS])
        a_exp = sb("a_exp", [R, HEADS])
        out_bias = sb("out_bias", [R, E])
        later = sb("later", [R, R], F32R)
        upto = sb("upto", [R, SEQ])
        causal = sb("causal", [R, R])
        block_of = sb("block_of", [R, R])
        odd = sb("odd", [R, 2])
        level_of = sb("level_of", [LROWS, SEQ // 2, R], F32R)
        ones = sb("ones", [128, 1])
        one = sb("one", [R, 1])
        index = sb("index", [R, 2, 2], U32)
        gathered = sb("gathered", [R, 2, 2, E])
        raw_in = sb("raw_in", [R, 2, E])
        ahead = sb("ahead", [R, 2, E])
        residual = sb("residual", [R, 2, E])
        stats = sb("stats", [R, 2, 1, 6])
        mv = sb("mv", [R, 2, 2])
        std = sb("std", [R, 2])
        rstd = sb("rstd", [R, 2])
        normed = gathered[:, :, 0, :]
        normedT_hi = sb("normedT_hi", [128, KE, G2], F32R)
        normedT_lo = sb("normedT_lo", [128, KE, G2], F32R)
        soft = sb("soft", [R, 2, DTL])
        decay_in = sb("decay_in", [R, 2, HEADS])
        even_part = decay_in
        dt_now = sb("dt_now", [R, 2, HEADS])
        decay_parts = sb("decay_parts", [R, 2, 2, HEADS], F32R)
        level_parts = sb("level_parts", [R, 2, 2, LEVELS * HEADS], F32R)
        level_rows = sb("level_rows", [LROWS, 2, SEQ * HEADS], F32R)
        first_bias = sb("first_bias", [128, CONV_TILES])
        padded = sb("padded", [128, RING, 2 * SPT, SEQ + TAPS - 1])
        conv = sb("conv", [128, RING, 2 * SPT, SEQ])
        xs = sb("xs", [128, CONV_TILES, G2])
        zs = sb("zs", [128, Z_TILES, G2])
        steps, att_block = space.sb_twice(stack, "mx_steps", [R, STEPS, 2, CHUNK * HEADS], F32R, "mx_att_block", [R, 2, GROUP * 2, R])
        decay = sb("decay", [R, 2, CHUNK * HEADS])
        qk_all = sb("qk_all", [R, 2, R])
        qk = sb("qk", [R, 2, SEQ])
        att = sb("att", [R, HEADS, 2, SEQ])
        vals = sb("vals", [R, 2, 2, GROUP, HD])
        logd, miss = (decay[:, b].rearrange("p (t c) -> p t c", t=2) for b in range(2))
        dtl, grown = (gathered[:, b].rearrange("p c e -> p (c e)").rearrange("p (t c) -> p t c", t=2) for b in range(2))
        shared = sb("shared", [128, 2, CHUNK * HEADS])
        weighed = shared[0:R]
        y = shared[:, :, 0:2 * G2].rearrange("p b (m r) -> p b m r", m=2)
        sumsq = sb("sumsq", [R, 2])
        rms = sb("rms", [R, 2])
        inv_rms = sb("inv_rms", [R, 2])
        sums_result = sb("sums_result", [128, 2, E])
        squares_sum = sums_result.rearrange("p h e -> p (h e)")[:, 0:2 * G2].rearrange("p (m r) -> p m r", m=2)
        result = sums_result[0:R]

        ps_turned = space.ps(stack, "mx_ps_turned", [128, 512])
        ps_fm = [space.ps(stack, f"mx_ps_fm{b}", [128, 512]) for b in range(2)]
        ps_decay = space.ps(stack, "mx_ps_decay", [128, 512])
        ps_level = space.ps(stack, "mx_ps_level", [128, 512])
        ps_decays = [ps_decay, ps_fm[0]]
        ps_levels = [ps_level, ps_fm[1]]
        ps_chan = ps_fm + [ps_decay, ps_level]
        ps_dtl = space.ps(stack, "mx_ps_dtl", [128, 512])
        ps_out = [space.ps(stack, f"mx_ps_out{h}", [128, 512]) for h in range(2)]
        SS = KE * G2

        consts = sem("consts")
        masks_cast = sem("masks_cast")
        padded_zero = sem("padded_zero")
        ones_ready = sem("ones_ready")
        a_ready = sem("a_ready")
        bias_ready = sem("bias_ready")
        index_ready = sem("index_ready")
        gather_done = [[sem(f"gather_done{h}{c}") for c in range(2)] for h in range(2)]
        stream_in = sem("stream_in")
        ahead_ready = sem("ahead_ready")
        residual_ready = sem("residual_ready")
        moments_ready = sem("moments_ready")
        std_ready = sem("std_ready")
        normed_ready = sem("normed_ready")
        turned_ready = sem("turned_ready")
        normedT_ready = sem("normedT_ready")
        dtl_ready = sem("dtl_ready")
        dtl_read = sem("dtl_read")
        tail_ready = sem("tail_ready")
        grown_ready = sem("grown_ready")
        logd_ready = sem("logd_ready")
        act_step = sem("act_step")
        soft_ready = sem("soft_ready")
        lam_stored = sem("lam_stored")
        levels_loaded = sem("levels_loaded")
        decay_in_ready = sem("decay_in_ready")
        fm_ready = sem("fm_ready")
        fm_read = sem("fm_read")
        conv_done = sem("conv_done")
        xs_ready = sem("xs_ready")
        zs_ready = sem("zs_ready")
        steps_ready = sem("steps_ready")
        decay_ps_ready = sem("decay_ps_ready")
        decay_ready = sem("decay_ready")
        qk_ps_ready = sem("qk_ps_ready")
        qk_ready = sem("qk_ready")
        weighed_ready = sem("weighed_ready")
        level_ps_ready = sem("level_ps_ready")
        att_ready = sem("att_ready")
        xT_ready = sem("xT_ready")
        vals_ready = sem("vals_ready")
        block_ready = sem("block_ready")
        y_ps_ready = sem("y_ps_ready")
        y_read = sem("y_read")
        yz_ready = sem("yz_ready")
        squares_ready = sem("squares_ready")
        squares_added = sem("squares_added")
        conv_step = sem("conv_step")
        first_bias_ready = sem("first_bias_ready")
        dt_copied = sem("dt_copied")
        out_ready = sem("out_ready")
        sumsq_ready = sem("sumsq_ready")
        rms_ready = sem("rms_ready")
        out_read = sem("out_read")
        result_stored = sem("result_stored")
        vec_step = sem("vec_step")
        NC = len(CHUNKS)
        DC = 2 * NC

        const_loads = [(fm_bias[:, :], io["fm_bias"]), (taps[:, :, :], io["taps"]), (skip[:, :], io["skip"]),
                       (dtl_bias[:, :], io["dtl_bias"].partition_broadcast(R)), (dt_bias[:, :], io["dt_bias"].partition_broadcast(R)),
                       (factor[:, HEADS:DTL], io["factor"].partition_broadcast(R)), (a_log[:, :], io["a_log"].partition_broadcast(R)),
                       (out_bias[:, :], io["out_bias"].partition_broadcast(R)), (upto[:, :], io["upto"]),
                       (causal[:, :], io["causal"]), (block_of[:, :], io["block_of"]), (odd[:, :], io["odd"])]
        const_casts = [(later[:, :], io["later"]), (level_of[:, :, :], io["level_of"])]
        all_consts = 16 * len(const_loads)

        POOL_ADDS = (3, 5)

        def add_squares(eng, i, k):
            eng.wait_ge(squares_ready, GROUPS * i + k + 1)
            if k >= 2:
                eng.wait_ge(squares_added, (GROUPS - 1) * i + k - 1)
            else:
                eng.wait_ge(result_stored, 16 * (i + 1))
            before = y[:, 0] if k == 1 else squares_sum[:, :, :]
            eng.tensor_tensor(squares_sum[:, :, :], y[:, k % 2], before, ALU.add).then_inc(squares_added, 1)

        block = stack.enter_context(nc.Block())

        @block.sync
        def _(sp):
            for dst, src in const_loads:
                sp.dma_start(dst, src).then_inc(consts, 16)

            def front_load(i):
                sp.dma_start(raw_in[:, :, :], stream.rearrange("(i t) r e -> i r t e", t=2)[i]).then_inc(stream_in, 16)

            def turn(i, last):
                if not last:
                    sp.wait_ge(ahead_ready, 2 * i + 2)
                    front_load(i + 1)
                sp.wait_ge(soft_ready, i + 1)
                for h in range(2):
                    sp.dma_start(lam_rows[h].rearrange("p l r h -> r (p l) h"), level_parts[:, h].bitcast(F32).rearrange("r p (l h) -> r (p l) h", l=LEVELS)).then_inc(lam_stored, 16)
                sp.wait_ge(out_read, i + 2)
                sp.dma_start(stream.rearrange("(i t) r e -> i r t e", t=2)[i], result[:, :, :]).then_inc(result_stored, 16)

            front_load(0)
            with sp.Fori(0, PAIRS - 1) as i:
                turn(i, False)
            turn(PAIRS - 1, True)
            sp.wait_ge(result_stored, 16 * (PAIRS + 1))

        @block.gpsimd
        def _(pool):
            pool.memset(padded[:, :, :, :], 0.0).then_inc(padded_zero, 1)
            pool.memset(factor[:, 0:HEADS], 1.0).then_inc(ones_ready, 1)
            pool.memset(one[:, :], 1.0).then_inc(ones_ready, 1)
            pool.memset(ones[:, :], 1.0).then_inc(ones_ready, 1)
            for dst, src in const_casts:
                pool.dma_start(dst, src).then_inc(masks_cast, 16)
            pool.wait_ge(consts, all_consts)
            pool.tensor_tensor(dtl_bias[:, 0:HEADS], dtl_bias[:, 0:HEADS], dt_bias[:, :], ALU.add).then_inc(bias_ready, 1)
            pool.tensor_tensor(first_bias[:, :], fm_bias[:, 0:CONV_TILES], taps[:, :, TAPS - 1], ALU.mult).then_inc(first_bias_ready, 1)

            def front_gather(i):
                for h in range(2):
                    for c in range(2):
                        pool.indirect_dma_start(gathered[:, h, c, :], None, expert_rows,
                                                bass.IndirectOffsetOnAxis(ap=index[:, h, c:c + 1], axis=0)).then_inc(gather_done[h][c], 16)

            def turn(i, last):
                pool.wait_ge(ahead_ready, 2 * i + 2)
                if not last:
                    pool.wait_ge(index_ready, i + 2)
                pool.wait_ge(lam_stored, 32 * i + 32)
                pool.wait_ge(out_read, i + 1)
                pool.tensor_tensor(residual[:, :, :], ahead[:, :, :], out_bias[:, :].unsqueeze(1).broadcast_to([R, 2, E]),
                                   ALU.add).then_inc(residual_ready, 1)
                if not last:
                    front_gather(i + 1)
                for h in range(2):
                    pool.dma_start(level_rows[:, h, :], lam_rows[h].rearrange("p l (b t) h -> (p l b) (t h)", b=SPT)).then_inc(levels_loaded, 16)
                pool.wait_ge(decay_in_ready, i + 1)
                for n in range(DC):
                    h, (a, b) = n // NC, CHUNKS[n % NC]
                    cols = (b - a) * HEADS
                    if n >= STEPS:
                        pool.wait_ge(decay_ready, DC * i + n - STEPS + 3)
                    pool.tensor_tensor(steps[:, n % STEPS, :, 0:cols].rearrange("p c (t h) -> p c t h", h=HEADS),
                                       decay_parts[:, h].bitcast(F32).unsqueeze(2).broadcast_to([R, 2, b - a, HEADS]),
                                       upto[:, a:b].unsqueeze(1).unsqueeze(3).broadcast_to([R, 2, b - a, HEADS]), ALU.mult).then_inc(steps_ready, 1)
                pool.wait_ge(att_ready, DC * (i + 1) + 2)
                for g in range(GROUPS):
                    if g >= 2:
                        pool.wait_ge(y_ps_ready, GROUPS * i + g - 1)
                    pool.tensor_tensor(att_block[:, g % 2].rearrange("p n (b t) -> p n b t", b=SPT),
                                           att[:, g * GROUP:(g + 1) * GROUP].rearrange("p h c t -> p (h c) t").unsqueeze(2).broadcast_to([R, 2 * GROUP, SPT, SEQ]),
                                           block_of[:, :].rearrange("p (b t) -> p b t", b=SPT).unsqueeze(1).broadcast_to([R, 2 * GROUP, SPT, SEQ]),
                                           ALU.mult).then_inc(block_ready, 1)
                    if g - 2 in POOL_ADDS:
                        add_squares(pool, i, g - 2)

            pool.wait_ge(index_ready, 1)
            front_gather(0)
            with pool.Fori(0, PAIRS - 1) as i:
                turn(i, False)
            turn(PAIRS - 1, True)

        @block.scalar
        def _(act):
            act.sem_inc(fm_read, 4)
            act.sem_inc(decay_ready, 2)
            act.wait_ge(consts, all_consts)
            act.activation(a_exp[:, :], a_log[:, :], ACT.Exp).then_inc(a_ready, 1)
            act.wait_ge(padded_zero, 1)
            act.wait_ge(ones_ready, 3)
            act.wait_ge(first_bias_ready, 1)

            def front(i):
                act.wait_ge(moments_ready, 2 * i + 2)
                act.activation(std[:, :], mv[:, :, 1], ACT.Sqrt, bias=eps[:, :]).then_inc(std_ready, 1)

            def softplus(i):
                act.wait_ge(tail_ready, i + 1)
                act.activation(grown[:, :, :], dtl[:, :, :], ACT.Abs).then_inc(act_step, 1)
                act.wait_ge(act_step, i + 1)
                act.activation(grown[:, :, :], grown[:, :, :], ACT.Exp, scale=-1.0).then_inc(grown_ready, 1)
                act.wait_ge(grown_ready, i + 1)
                act.activation(logd[:, :, :], grown[:, :, :], ACT.Ln, bias=one[:, :]).then_inc(logd_ready, 1)

            def turn(i, last):
                for n in range(CONV_TILES + RING):
                    if n >= RING:
                        act.wait_ge(conv_done, CONV_TILES * i + n - RING + 1)
                        act.activation(xs[:, n - RING, :], conv[:, n % RING].rearrange("p s t -> p (s t)"), ACT.Silu).then_inc(xs_ready, 1)
                    if n < CONV_TILES:
                        q = n if n < 2 else 2 * n - 2
                        act.wait_ge(fm_ready, FM_TILES * i + q + 1)
                        src = ps_chan[q % 4][:, 0:G2].rearrange("p (s t) -> p s t", t=SEQ)
                        act.activation(padded[:, n % RING, :, TAPS - 1:], src, ACT.Identity, bias=fm_bias[:, n:n + 1])
                        if n >= RING:
                            act.wait_ge(xs_ready, CONV_TILES * i + n - RING + 1)
                        act.activation(conv[:, n % RING], src, ACT.Identity, bias=first_bias[:, n:n + 1], scale=taps[:, n, TAPS - 1:TAPS]).then_inc(fm_read, 1)
                        if n >= 2:
                            q, m = q + 1, n - 2
                            act.wait_ge(fm_ready, FM_TILES * i + q + 1)
                            act.activation(zs[:, m, :], ps_chan[q % 4][:, 0:G2], ACT.Silu,
                                           bias=fm_bias[:, CONV_TILES + m:CONV_TILES + m + 1]).then_inc(fm_read, 1)
                for n in range(DC):
                    cols = (CHUNKS[n % NC][1] - CHUNKS[n % NC][0]) * HEADS
                    act.wait_ge(decay_ps_ready, DC * i + n + 1)
                    if n >= 2:
                        act.wait_ge(weighed_ready, DC * i + n - 1)
                    act.activation(decay[:, n % 2, 0:cols], ps_decays[n % 2][0:R, 0:cols], ACT.Exp).then_inc(decay_ready, 1)
                if not last:
                    front(i + 1)
                for g in range(GROUPS):
                    if g == 4 and not last:
                        softplus(i + 1)
                    act.wait_ge(yz_ready, GROUPS * i + g + 1)
                    act.activation(y[:, g % 2], zs[:, 2 * g:2 * g + 2, :], ACT.Square).then_inc(squares_ready, 1)
                act.wait_ge(sumsq_ready, i + 1)
                act.activation(rms[:, :], sumsq[:, :], ACT.Sqrt, bias=eps[:, :], scale=1.0 / DIM).then_inc(rms_ready, 1)

            front(0)
            softplus(0)
            with act.Fori(0, PAIRS - 1) as i:
                turn(i, False)
            turn(PAIRS - 1, True)

        @block.vector
        def _(v):
            step = Chain(v, vec_step, spare)

            def front(i):
                v.tensor_copy(index[:, :, :], slots[:, :, bass.ds(2 * i, 2)].rearrange("p c h -> p h c")).then_inc(index_ready, 1)

            def front_shares(i):
                v.wait_ge(stream_in, 16 * i + 16)
                for h in range(2):
                    v.wait_ge(gather_done[h][0], 16 * i + 16)
                    step(v.scalar_tensor_tensor(ahead[:, h, :], gathered[:, h, 0, :], shares[:, 0, bass.ds(2 * i + h, 1)],
                                                raw_in[:, h, :], ALU.mult, ALU.add))
                    v.wait_ge(gather_done[h][1], 16 * i + 16)
                    v.scalar_tensor_tensor(ahead[:, h, :], gathered[:, h, 1, :], shares[:, 1, bass.ds(2 * i + h, 1)],
                                           ahead[:, h, :], ALU.mult, ALU.add).then_inc(ahead_ready, 1)
                    v.wait_ge(ahead_ready, 2 * i + h + 1)
                    moments(v, step, ahead[:, h, :], stats[:, h], mv[:, h, :]).then_inc(moments_ready, 1)

            def front_normed(i):
                v.wait_ge(std_ready, i + 1)
                step(v.reciprocal(rstd[:, :], std[:, :]))
                for h in range(2):
                    normalize(v, normed[:, h, :], ahead[:, h, :], mv[:, h, :], rstd[:, h:h + 1]).then_inc(normed_ready, 1)

            def front_turned(i):
                v.wait_ge(turned_ready, i + 1)
                src = ps_turned[:, 0:SS].rearrange("p (k r) -> p k r", k=KE)
                step(v.tensor_copy(normedT_hi[:, :, :], src))
                v.tensor_tensor(normedT_lo[:, :, :], src, normedT_hi[:, :, :].bitcast(F32), ALU.subtract).then_inc(normedT_ready, 1)

            def dtl_begin(i):
                v.wait_ge(dtl_ready, i + 1)
                v.tensor_tensor(miss[:, :, :], ps_dtl[0:R, :].rearrange("p (h c) -> p h c", h=2),
                                dtl_bias[:, :].unsqueeze(1).broadcast_to([R, 2, DTL]), ALU.add).then_inc(dtl_read, 1)
                v.wait_ge(dtl_read, i + 1)
                v.tensor_tensor(dtl[:, :, :], miss[:, :, :], factor[:, :].unsqueeze(1).broadcast_to([R, 2, DTL]), ALU.mult).then_inc(tail_ready, 1)

            def dtl_grown(i):
                v.wait_ge(grown_ready, i + 1)
                step(v.tensor_scalar(soft[:, :, :], grown[:, :, :], 1.0, None, ALU.add))
                step(v.scalar_tensor_tensor(miss[:, :, :], soft[:, :, :], -1.0, grown[:, :, :], ALU.add, ALU.subtract))

            def dtl_soft(i):
                v.wait_ge(logd_ready, i + 1)
                step(v.tensor_tensor(miss[:, :, :], logd[:, :, :], miss[:, :, :], ALU.subtract))
                step(v.scalar_tensor_tensor(soft[:, :, :], dtl[:, :, :], 0.0, miss[:, :, :], ALU.max, ALU.add))

            def dtl_levels(i):
                v.wait_ge(decay_in_ready, i + 1)
                step(v.tensor_scalar(even_part[:, :, :], soft[:, :, 2 * HEADS:3 * HEADS], odd[:, 1:2], None, ALU.mult))
                step(v.scalar_tensor_tensor(soft[:, :, HEADS:2 * HEADS], soft[:, :, HEADS:2 * HEADS], odd[:, 0:1], even_part[:, :, :],
                                            ALU.mult, ALU.add))
                step(v.tensor_copy(level_parts[:, :, 0, :], soft[:, :, HEADS:DTL]))
                v.tensor_tensor(level_parts[:, :, 1, :], soft[:, :, HEADS:DTL], level_parts[:, :, 0, :].bitcast(F32), ALU.subtract).then_inc(soft_ready, 1)

            def dtl_decay(i):
                step(v.scalar_tensor_tensor(decay_in[:, :, :], soft[:, :, 0:HEADS], -1.0, a_exp[:, :].unsqueeze(1).broadcast_to([R, 2, HEADS]),
                                            ALU.mult, ALU.mult))
                step(v.tensor_copy(decay_parts[:, :, 0, :], decay_in[:, :, :]))
                v.tensor_tensor(decay_parts[:, :, 1, :], decay_in[:, :, :], decay_parts[:, :, 0, :].bitcast(F32), ALU.subtract).then_inc(decay_in_ready, 1)

            per_turn = 1 + (2 * 2 + 1 + 1) + (2 + 2 + 3 + 2) + 1

            def turn(i, last):
                v.tensor_copy(dt_now[:, :, :], soft[:, :, 0:HEADS]).then_inc(dt_copied, 1)
                if not last:
                    front(i + 1)

                def taps_of(n, c):
                    if c == 0:
                        v.wait_ge(fm_read, FM_TILES * i + (n if n < 2 else 2 * n - 2) + 1 + 4)
                    else:
                        v.wait_ge(conv_step, 2 * CONV_TILES * i + 4 * (n // 2) + 2 * (c - 1) + n % 2 + 1)
                    dst = conv[:, n % RING]
                    v.scalar_tensor_tensor(dst, padded[:, n % RING, :, c:c + SEQ], taps[:, n, c:c + 1], dst,
                                           ALU.mult, ALU.add).then_inc(conv_step if c < TAPS - 2 else conv_done, 1)

                for n in range(0, CONV_TILES, 2):
                    for c in range(TAPS - 1):
                        taps_of(n, c)
                        taps_of(n + 1, c)
                    if n == CONV_TILES // 4 * 2 + 2 and not last:
                        v.wait_ge(residual_ready, i + 1)
                        front_shares(i + 1)
                v.wait_ge(qk_ps_ready, i + 1)
                for h in range(2):
                    ins = v.tensor_tensor(qk_all[:, h, :], ps_out[h][0:R, E:E + R], causal[:, :], ALU.mult)
                step(ins)
                for h in range(2):
                    ins = v.tensor_reduce(qk[:, h, :], qk_all[:, h, :].rearrange("p (b t) -> p t b", b=SPT), AX.X, ALU.add)
                ins.then_inc(qk_ready, 1)
                def weigh(n):
                    h, (a, b) = n // NC, CHUNKS[n % NC]
                    cols = (b - a) * HEADS
                    v.wait_ge(decay_ready, DC * i + n + 3)
                    if n >= 2:
                        v.wait_ge(att_ready, DC * i + n + 1)
                    v.tensor_tensor(weighed[:, n % 2, 0:cols].rearrange("p (t h) -> p t h", h=HEADS),
                                    decay[:, n % 2, 0:cols].rearrange("p (t h) -> p t h", h=HEADS),
                                    qk[:, h, a:b].unsqueeze(2).broadcast_to([R, b - a, HEADS]), ALU.mult).then_inc(weighed_ready, 1)

                v.wait_ge(qk_ready, i + 1)
                weigh(0)
                for n in range(DC):
                    h, (a, b) = n // NC, CHUNKS[n % NC]
                    cols = (b - a) * HEADS
                    if n + 1 < DC:
                        weigh(n + 1)
                    v.wait_ge(weighed_ready, DC * i + n + 1)
                    v.wait_ge(level_ps_ready, DC * i + n + 1)
                    v.tensor_tensor(att[:, :, h, a:b].rearrange("p h t -> p t h"),
                                    weighed[:, n % 2, 0:cols].rearrange("p (t h) -> p t h", h=HEADS),
                                    ps_levels[n % 2][0:R, 0:cols].rearrange("p (t h) -> p t h", h=HEADS), ALU.mult).then_inc(att_ready, 1)
                v.wait_ge(dt_copied, i + 1)

                for g in range(GROUPS + 1):
                    if g < GROUPS:
                        if g >= 2:
                            v.wait_ge(y_ps_ready, GROUPS * i + g - 1)
                        v.wait_ge(xT_ready, GROUPS * i + g + 1)
                        v.tensor_tensor(vals[:, g % 2], [ps_decay, ps_level][g % 2][0:R, :].rearrange("p (c h d) -> p c h d", c=2, h=GROUP),
                                        dt_now[:, :, g * GROUP:(g + 1) * GROUP].unsqueeze(3).broadcast_to([R, 2, GROUP, HD]),
                                        ALU.mult).then_inc(vals_ready, 1)
                    if g >= 1:
                        k = g - 1
                        v.wait_ge(y_ps_ready, GROUPS * i + k + 1)
                        if k >= 2 and k - 1 not in POOL_ADDS:
                            add_squares(v, i, k - 1)
                        if k >= 3:
                            v.wait_ge(squares_added, (GROUPS - 1) * i + k - 2)
                        elif k == 2:
                            v.wait_ge(squares_added, (GROUPS - 1) * i + 1)
                        for m in range(2):
                            ins = v.scalar_tensor_tensor(y[:, k % 2, m, :], xs[:, 2 + 2 * k + m, :], skip[:, 2 * k + m:2 * k + m + 1],
                                                         ps_fm[k % 2][:, m * G2:(m + 1) * G2], ALU.mult, ALU.add)
                        ins.then_inc(y_read, 1)
                        v.wait_ge(y_read, GROUPS * i + k + 2)
                        v.tensor_tensor(zs[:, 2 * k:2 * k + 2, :], zs[:, 2 * k:2 * k + 2, :], y[:, k % 2], ALU.mult).then_inc(yz_ready, 1)
                    if not last:
                        if g == 0:
                            front_normed(i + 1)
                        if g == 2:
                            front_turned(i + 1)
                        if g == 4:
                            dtl_begin(i + 1)
                        if g == 6:
                            dtl_grown(i + 1)
                        if g == 7:
                            dtl_soft(i + 1)
                        if g == 8:
                            dtl_decay(i + 1)
                add_squares(v, i, GROUPS - 1)
                v.wait_ge(residual_ready, i + 1)
                v.wait_ge(out_ready, i + 1)
                v.tensor_reduce(sumsq[:, :], ps_turned[0:R, SS:SS + 4].rearrange("p (h m) -> p h m", h=2), AX.X, ALU.add).then_inc(sumsq_ready, 1)
                v.wait_ge(rms_ready, i + 1)
                step(v.reciprocal(inv_rms[:, :], rms[:, :]))
                for h in range(2):
                    ins = v.scalar_tensor_tensor(result[:, h, :], ps_out[h][0:R, 0:E], inv_rms[:, h:h + 1], residual[:, h, :], ALU.mult, ALU.add)
                ins.then_inc(out_read, 1)
                if not last:
                    dtl_levels(i + 1)

            v.sem_inc(att_ready, 2)
            v.sem_inc(y_read, 1)
            v.sem_inc(out_read, 1)
            v.sem_inc(result_stored, 16)
            v.wait_ge(consts, all_consts)
            v.wait_ge(ones_ready, 3)
            v.wait_ge(bias_ready, 1)
            v.wait_ge(a_ready, 1)
            front(0)
            front_shares(0)
            front_normed(0)
            front_turned(0)
            dtl_begin(0)
            dtl_grown(0)
            dtl_soft(0)
            dtl_decay(0)
            dtl_levels(0)
            with v.Fori(0, PAIRS - 1) as i:
                step.enter(i, per_turn)
                turn(i, False)
                step.leave(PAIRS - 1, per_turn)
            turn(PAIRS - 1, True)

        @block.tensor
        def _(pe):
            pe.wait_ge(consts, all_consts)
            pe.wait_ge(masks_cast, 16 * len(const_casts))
            pe.wait_ge(ones_ready, 3)
            three = lambda hi_a, lo_a, hi_b, lo_b: ((hi_a, hi_b), (hi_a, lo_b), (lo_a, hi_b))

            def front(i):
                pe.wait_ge(normed_ready, 2 * i + 2)
                for k in range(KE):
                    for h in range(2):
                        ins = pe.transpose(ps_turned[:, k * G2 + h * R:k * G2 + (h + 1) * R], normed[:, h, k * 128:(k + 1) * 128], ident[0:R, 0:R])
                ins.then_inc(turned_ready, 1)

            def project(i, q, tile):
                pe.wait_ge(fm_read, FM_TILES * i + q + 1)
                out = ps_chan[q % 4][:, 0:G2]
                for k in range(KE):
                    for c, (w, x) in enumerate(three(w_hi, w_lo, normedT_hi, normedT_lo)):
                        ins = pe.matmul(out, w[:, k, tile * 128:(tile + 1) * 128], x[:, k, :], start=(k == 0 and c == 0), stop=(k == KE - 1 and c == 2))
                ins.then_inc(fm_ready, 1)

            def turn_x(i, g):
                if g == 0:
                    pe.wait_ge(decay_ready, DC * (i + 1) + 2)
                    pe.wait_ge(xs_ready, CONV_TILES * (i + 1))
                if g == 1:
                    pe.wait_ge(att_ready, DC * (i + 1) + 2)
                if g >= 2:
                    pe.wait_ge(vals_ready, GROUPS * i + g - 1)
                out = (ps_decay, ps_level)[g % 2]
                for h in range(2):
                    for m in range(2):
                        ins = pe.transpose(out[0:R, h * 256 + m * 128:h * 256 + (m + 1) * 128], xs[:, 2 + 2 * g + m, h * R:(h + 1) * R], ident[:, :])
                ins.then_inc(xT_ready, 1)

            def heads(i, g):
                pe.wait_ge(vals_ready, GROUPS * i + g + 1)
                pe.wait_ge(block_ready, GROUPS * i + g + 1)
                if g >= 2:
                    pe.wait_ge(y_read, GROUPS * i + g)
                for n in range(GROUP):
                    m, low = divmod(n, 2)
                    for h in range(2):
                        ins = pe.matmul(ps_fm[g % 2][low * HD:(low + 1) * HD, m * G2 + h * R:m * G2 + (h + 1) * R],
                                        vals[:, g % 2, h, n, :], att_block[:, g % 2, 2 * n + h, :], start=True, stop=True)
                ins.then_inc(y_ps_ready, 1)

            def project_out(i, g):
                pe.wait_ge(yz_ready, GROUPS * i + g + 1)
                for m in range(2 * g, 2 * g + 2):
                    for h in range(2):
                        ins = pe.matmul(ps_out[h][0:R, 0:E], zs[:, m, h * R:(h + 1) * R], w_out[:, m, :], start=(m == 0), stop=(m == Z_TILES - 1))
                if g == GROUPS - 1:
                    pe.wait_ge(squares_added, (GROUPS - 1) * (i + 1))
                    for h in range(2):
                        for m in range(2):
                            ins = pe.matmul(ps_turned[0:R, SS + 2 * h + m:SS + 2 * h + m + 1], squares_sum[:, m, h * R:(h + 1) * R],
                                            ones[:, :], start=True, stop=True)
                    ins.then_inc(out_ready, 1)

            def project_dtl(i):
                pe.wait_ge(normedT_ready, i + 1)
                for h in range(2):
                    for k in range(KE):
                        for c, (x, w) in enumerate(three(normedT_hi, normedT_lo, w_hi, w_lo)):
                            ins = pe.matmul(ps_dtl[0:R, h * DTL:(h + 1) * DTL], x[:, k, h * R:(h + 1) * R], w[:, k, FM_TILES * 128:FM_TILES * 128 + DTL],
                                            start=(k == 0 and c == 0), stop=(k == KE - 1 and c == 2))
                ins.then_inc(dtl_ready, 1)

            def turn(i, last):
                pe.wait_ge(y_read, GROUPS * i + 1)
                project(i, 0, 0)
                project(i, 1, 1)
                for m in range(Z_TILES):
                    project(i, 2 + 2 * m, 2 + m)
                    project(i, 3 + 2 * m, CONV_TILES + m)
                pe.wait_ge(xs_ready, CONV_TILES * i + 2)
                pe.wait_ge(out_read, i + 1)
                for h in range(2):
                    ins = pe.matmul(ps_out[h][0:R, E:E + R], xs[:, 0, h * R:(h + 1) * R], xs[:, 1, h * R:(h + 1) * R], start=True, stop=True)
                ins.then_inc(qk_ps_ready, 1)
                pe.wait_ge(fm_read, FM_TILES * (i + 1) + 4)
                pe.wait_ge(levels_loaded, 32 * i + 32)
                for n in range(DC):
                    h, (a, b) = n // NC, CHUNKS[n % NC]
                    cols = (b - a) * HEADS
                    pe.wait_ge(steps_ready, DC * i + n + 1)
                    pe.wait_ge(decay_ready, DC * i + n + 1)
                    for c in range(2):
                        ins = pe.matmul(ps_decays[n % 2][0:R, 0:cols], later[:, :], steps[:, n % STEPS, c, 0:cols], start=(c == 0), stop=(c == 1))
                    ins.then_inc(decay_ps_ready, 1)
                    pe.wait_ge(att_ready, DC * i + n + 1)
                    for m in range(a // 2, b // 2):
                        ins = pe.matmul(ps_levels[n % 2][0:R, (2 * m - a) * HEADS:(2 * m - a + 2) * HEADS], level_of[:, m, :],
                                        level_rows[:, h, 2 * m * HEADS:(2 * m + 2) * HEADS], start=True, stop=True)
                    ins.then_inc(level_ps_ready, 1)
                for g in range(GROUPS + 2):
                    if g == 2 and not last:
                        front(i + 1)
                    if g == 4 and not last:
                        project_dtl(i + 1)
                    if g < GROUPS:
                        turn_x(i, g)
                    if 1 <= g <= GROUPS:
                        heads(i, g - 1)
                    if g >= 2:
                        project_out(i, g - 2)

            front(0)
            project_dtl(0)
            with pe.Fori(0, PAIRS - 1) as i:
                turn(i, False)
            turn(PAIRS - 1, True)


INNER_SHARED = 704
KD_SHARED = -(-INNER_SHARED // 128)
EARLY = 4


def scatter_rows(pool, scattered, slots, normed_all, slot_rows):
    for c in range(2):
        for t in range(NT):
            pool.indirect_dma_start(slot_rows, bass.IndirectOffsetOnAxis(ap=slots[:, c, t:t + 1], axis=0),
                                    normed_all[:, t, :], None).then_inc(scattered, 16)
    pool.wait_ge(scattered, 16 * 2 * NT)


class SharedWeights:

    def __init__(self, space, stack):
        self.up_hi = space.sb(stack, "sw_up_hi", [128, 2, KE, INNER_SHARED], F32R)
        self.up_lo = space.sb(stack, "sw_up_lo", [128, 2, KE, INNER_SHARED], F32R)
        self.down_hi = space.sb(stack, "sw_down_hi", [128, KD_SHARED, E], F32R)
        self.down_lo = space.sb(stack, "sw_down_lo", [128, KD_SHARED, E], F32R)


def share_experts(nc, space, name, io, finish, weights, hidden, normed_all, slot_rows, expert_rows, slots, shares, out, ident):
    KD = KD_SHARED
    width = [min(128, INNER_SHARED - m * 128) for m in range(KD)]
    start = EARLY if finish else 0
    turns = PAIRS - EARLY if finish else EARLY
    up_hi, up_lo, down_hi, down_lo = weights.up_hi, weights.up_lo, weights.down_hi, weights.down_lo
    assert PAIRS - EARLY > EARLY
    with ExitStack() as stack:
        def sb(what, shape, dt=F32):
            return space.sb(stack, f"{name}_{what}", shape, dt)

        def sem(what):
            return space.sem(f"{name}_{what}")

        if not finish:
            up_raw = sb("up_raw", [128, 2, KE, INNER_SHARED])
            down_raw = sb("down_raw", [128, KD, E])
        normed = sb("normed", [R, 2, E])
        normedT_hi = sb("normedT_hi", [128, KE, G2], F32R)
        normedT_lo = sb("normedT_lo", [128, KE, G2], F32R)
        silu = sb("silu", [128, KD, G2])
        inner_f = sb("inner_f", [128, KD, G2])
        inner_hi = sb("inner_hi", [128, KD, G2], F32R)
        inner_lo = sb("inner_lo", [128, KD, G2], F32R)
        index = [sb(f"index{z}", [R, 2, 2], U32) for z in range(2)]
        gathered = [sb(f"gathered{z}", [R, 2, 2, E]) for z in range(2)]
        sums = [sb(f"sums{z}", [R, 2, 2, E]) for z in range(2)]
        result = [sb(f"result{z}", [R, 2, E]) for z in range(2)]
        mark = sb("mark", [1, 3])
        ps_turned = space.ps(stack, f"{name}_ps_turned", [128, 512])
        RING = 3
        ps_up = [space.ps(stack, f"{name}_ps_up{b}", [128, 512]) for b in range(RING)]
        ps_down = [space.ps(stack, f"{name}_ps_down{h}", [128, 512]) for h in range(2)]

        loaded = sem("loaded")
        scattered = sem("scattered")
        high_done = sem("high_done")
        low_done = sem("low_done")
        normed_ready = sem("normed_ready")
        turned_ready = sem("turned_ready")
        normedT_ready = sem("normedT_ready")
        up_ready = sem("up_ready")
        silu_done = sem("silu_done")
        inner_done = sem("inner_done")
        inner_split = sem("inner_split")
        down_ready = sem("down_ready")
        down_read = sem("down_read")
        index_ready = [sem(f"index_ready{z}") for z in range(2)]
        gather_done = [[[sem(f"gather_done{z}{h}{c}") for c in range(2)] for h in range(2)] for z in range(2)]
        early_ready = sem("early_ready")
        stored = [sem(f"stored{z}") for z in range(2)]
        marked = [sem(f"marked{z}") for z in range(2)]
        vec_step = sem("vec_step")

        block = stack.enter_context(nc.Block())

        @block.sync
        def _(sp):
            if not finish:
                n = load_rows(sp, loaded, up_raw[:, 0], io["swg"]) + load_rows(sp, loaded, up_raw[:, 1], io["swu"])
                n += load_rows(sp, loaded, down_raw, io["swd"])
                assert n == 4
                return
            late_rows, early_rows = (out[a * G2:b * G2].rearrange("(i t r) e -> i r t e", r=R, t=2)
                                     for a, b in ((start, PAIRS - 1), (0, EARLY)))

            for i in range(turns - 1):
                sp.wait_ge(down_read, 2 * i + 3)
                sp.dma_start(late_rows[i], result[0][:, :, :]).then_inc(stored[0], 16)
                if i < EARLY:
                    sp.wait_ge(early_ready, i + 1)
                    sp.dma_start(early_rows[i], result[1][:, :, :]).then_inc(stored[1], 16)
            done, end = (NT - 2) * R, BATCH * SEQ
            sp.wait_ge(down_read, 2 * turns + 1)
            sp.dma_start(out[done:done + R], result[0][:, 0, :]).then_inc(stored[0], 16)
            sp.dma_start(out[done + R:end], result[0][0:end - done - R, 1, :]).then_inc(stored[0], 16)
            sp.wait_ge(stored[0], 16 * (turns + 2))
            sp.wait_ge(stored[1], 16 * (EARLY + 1))

        @block.gpsimd
        def _(pool):
            if not finish:
                scatter_rows(pool, scattered, slots, normed_all, slot_rows)
                return

            def gather(i, z):
                pool.wait_ge(index_ready[z], i + 1)
                pool.tensor_tensor(mark[:, z + 1:z + 2], mark[:, 0:1], mark[:, 0:1], ALU.add).then_inc(marked[z], 1)
                for h in range(2):
                    for c in range(2):
                        pool.indirect_dma_start(gathered[z][:, h, c, :], None, expert_rows,
                                                bass.IndirectOffsetOnAxis(ap=index[z][:, h, c:c + 1], axis=0)).then_inc(gather_done[z][h][c], 16)

            pool.memset(mark[:, 0:1], 0.0).then_inc(marked[0], 1)
            pool.wait_ge(marked[0], 1)
            pool.sem_inc(marked[1], 1)
            with pool.Fori(0, EARLY) as i:
                gather(i, 0)
                gather(i, 1)
            for i in range(EARLY, turns):
                gather(i, 0)

        @block.scalar
        def _(act):
            if not finish:
                act.wait_ge(loaded, 64)
                act.copy(up_hi[:, :, :, :], up_raw[:, :, :, :])
                for k in range(KD):
                    ins = act.copy(down_hi[0:width[k], k, :], down_raw[0:width[k], k, :])
                ins.then_inc(high_done, 1)
            with act.Fori(0, turns) as i:
                for m in range(KD):
                    act.wait_ge(up_ready, KD * i + m + 1)
                    act.activation(silu[0:width[m], m, :], ps_up[m % RING][0:width[m], 0:G2], ACT.Silu).then_inc(silu_done, 1)

        @block.vector
        def _(v):
            step = Chain(v, vec_step)

            def front(i):
                v.tensor_copy(normed[:, :, :], normed_all[:, bass.ds(2 * (i + start), 2), :]).then_inc(normed_ready, 1)

            def turn_rows(i):
                v.wait_ge(turned_ready, i + 1)
                src = ps_turned[:, 0:KE * G2].rearrange("p (k r) -> p k r", k=KE)
                step(v.tensor_copy(normedT_hi[:, :, :], src))
                v.tensor_tensor(normedT_lo[:, :, :], src, normedT_hi[:, :, :].bitcast(F32), ALU.subtract).then_inc(normedT_ready, 1)

            def ask(i, z, first):
                v.wait_ge(marked[z], i + 1)
                v.tensor_copy(index[z][:, :, :], slots[:, :, bass.ds(2 * (i + first), 2)].rearrange("p c h -> p h c")).then_inc(index_ready[z], 1)

            def add_shares(i, z, first, last_out):
                for c in range(2):
                    for h in range(2):
                        v.wait_ge(gather_done[z][h][c], 16 * i + 16)
                        before = hidden[:, 2 * (i + first) + h, :] if c == 0 else sums[z][:, 0, h, :]
                        after = last_out[:, h, :] if c == 1 and last_out is not None else sums[z][:, c, h, :]
                        ins = v.scalar_tensor_tensor(after, gathered[z][:, h, c, :], shares[:, c, bass.ds(2 * (i + first) + h, 1)], before, ALU.mult, ALU.add)
                    if c == 0 or last_out is None:
                        step(ins)
                return ins

            def turn(i, early, last):
                if finish:
                    ask(i, 0, start)
                    if early:
                        ask(i, 1, 0)
                if not last:
                    front(i + 1)
                for m in range(KD):
                    w = width[m]
                    v.wait_ge(silu_done, KD * i + m + 1)
                    v.tensor_tensor(inner_f[0:w, m, :], silu[0:w, m, :], ps_up[m % RING][0:w, G2:2 * G2], ALU.mult).then_inc(inner_done, 1)
                    v.wait_ge(inner_done, KD * i + m + 1 + RING)
                    step(v.tensor_copy(inner_hi[0:w, m, :], inner_f[0:w, m, :]))
                    v.tensor_tensor(inner_lo[0:w, m, :], inner_f[0:w, m, :], inner_hi[0:w, m, :].bitcast(F32), ALU.subtract).then_inc(inner_split, 1)
                if not last:
                    turn_rows(i + 1)
                if finish:
                    add_shares(i, 0, start, None)
                    v.wait_ge(stored[0], 16 * i + 16)
                v.wait_ge(down_ready, i + 1)
                for h in range(2):
                    if finish:
                        v.tensor_tensor(result[0][:, h, :], ps_down[h][0:R, 0:E], sums[0][:, 1, h, :], ALU.add).then_inc(down_read, 1)
                    else:
                        rows = hidden[:, 2 * (i + start) + h, :]
                        v.tensor_tensor(rows, ps_down[h][0:R, 0:E], rows, ALU.add).then_inc(down_read, 1)
                if early:
                    v.wait_ge(stored[1], 16 * i + 16)
                    add_shares(i, 1, 0, result[1]).then_inc(early_ready, 1)

            v.sem_inc(inner_done, RING)
            v.sem_inc(down_read, 1)
            for z in range(2):
                v.sem_inc(stored[z], 16)
            if not finish:
                v.wait_ge(high_done, 1)
                v.tensor_tensor(up_lo[:, :, :, :].rearrange("p u k n -> p (u k n)"), up_raw[:, :, :, :].rearrange("p u k n -> p (u k n)"),
                                up_hi[:, :, :, :].bitcast(F32).rearrange("p u k n -> p (u k n)"), ALU.subtract)
                for k in range(KD):
                    w = width[k]
                    ins = v.tensor_tensor(down_lo[0:w, k, :], down_raw[0:w, k, :], down_hi[0:w, k, :].bitcast(F32), ALU.subtract)
                ins.then_inc(low_done, 1)
            front(0)
            turn_rows(0)
            if finish:
                per_turn = KD + 1 + 2 + 1
                with v.Fori(0, EARLY) as i:
                    step.enter(i, per_turn)
                    turn(i, True, False)
                    step.leave(EARLY, per_turn)
                for i in range(EARLY, turns):
                    turn(i, False, i == turns - 1)
            else:
                per_turn = KD + 1
                with v.Fori(0, turns - 1) as i:
                    step.enter(i, per_turn)
                    turn(i, False, False)
                    step.leave(turns - 1, per_turn)
                turn(turns - 1, False, True)

        @block.tensor
        def _(pe):
            def front(i):
                pe.wait_ge(normed_ready, i + 1)
                for k in range(KE):
                    for h in range(2):
                        ins = pe.transpose(ps_turned[:, k * G2 + h * R:k * G2 + (h + 1) * R], normed[:, h, k * 128:(k + 1) * 128], ident[0:R, 0:R])
                ins.then_inc(turned_ready, 1)

            def turn(i, last):
                pe.wait_ge(normedT_ready, i + 1)
                for m in range(KD):
                    w = width[m]
                    pe.wait_ge(inner_done, KD * i + m + 1)
                    for u in range(2):
                        for k in range(KE):
                            for c, (wt, xt) in enumerate(((up_hi, normedT_hi), (up_hi, normedT_lo), (up_lo, normedT_hi))):
                                ins = pe.matmul(ps_up[m % RING][0:w, u * G2:(u + 1) * G2], wt[:, u, k, m * 128:m * 128 + w], xt[:, k, :],
                                                start=(k == 0 and c == 0), stop=(k == KE - 1 and c == 2))
                    ins.then_inc(up_ready, 1)
                if not last:
                    front(i + 1)
                pe.wait_ge(down_read, 2 * i + 1)
                for m in range(KD):
                    w = width[m]
                    pe.wait_ge(inner_split, KD * i + m + 1)
                    for h in range(2):
                        for c, (xt, wt) in enumerate(((inner_hi, down_hi), (inner_lo, down_hi), (inner_hi, down_lo))):
                            ins = pe.matmul(ps_down[h][0:R, 0:E], xt[0:w, m, h * R:(h + 1) * R], wt[0:w, m, :],
                                            start=(m == 0 and c == 0), stop=(m == KD - 1 and c == 2))
                ins.then_inc(down_ready, 1)

            if not finish:
                pe.wait_ge(low_done, 1)
            front(0)
            with pe.Fori(0, turns - 1) as i:
                turn(i, False)
            turn(turns - 1, True)


def tower(nc, io, out, upto=9):
    with ExitStack() as outer:
        space = Space(nc)
        ident = space.sb(outer, "ident", [128, 128])
        ones_row = space.sb(outer, "ones_row", [1, 128])
        eps = space.sb(outer, "eps", [R, 1])
        spare = space.sb(outer, "spare", [1, 1])
        slots = space.sb(outer, "slots", [R, 2, NT], U32)
        shares = space.sb(outer, "shares", [R, 2, NT])
        jobs = space.sb(outer, "jobs", [1, EXPERTS + 1], I32)
        slot_rows = nc.dram_tensor("slot_rows", (SLOTS, E), F32, kind="Internal").ap()
        expert_rows = nc.dram_tensor("expert_rows", (SLOTS, E), F32, kind="Internal").ap()
        stream = nc.dram_tensor("stream", (NT, R, E), F32, kind="Internal").ap()
        lam_rows = nc.dram_tensor("lam_rows", (2, 2, LEVELS, R, HEADS), F32, kind="Internal").ap()

        with ExitStack() as mixer:
            w_hi = space.sb(mixer, "w_hi", [128, KE, FM_TILES * 128 + DTL], F32R)
            w_lo = space.sb(mixer, "w_lo", [128, KE, FM_TILES * 128 + DTL], F32R)
            w_out = space.sb(mixer, "w_out", [128, Z_TILES, E])
            with space.part(), ExitStack() as first:
                hidden = space.sb(first, "hidden0", [R, NT, E])
                tokenize(nc, space, io, hidden, [slot_rows, expert_rows], ident, ones_row, eps, spare)
                attend(nc, space, io, hidden, ident, eps, spare)
                normed_all = space.sb(first, "normed_all0", [R, NT, E])
                route(nc, space, "r0", io["gate0"], False, hidden, normed_all, slots, shares, jobs, ident, eps, spare)
                split_and_scatter(nc, space, io["in_proj"], w_hi, w_lo, io["out_proj"], io["norm_w"], w_out, slots, normed_all, slot_rows, hidden, stream)
            with space.part():
                run_experts(nc, space, "x0", [io["w_in"]], io["b_in"], io["w_out"], io["b_out"], 1024, jobs, slot_rows, expert_rows, ident)
            with space.part():
                mix_sequences(nc, space, io, stream, expert_rows, slots, shares, w_hi, w_lo, w_out, lam_rows, ident, eps, spare)
        with ExitStack() as last:
            hidden = space.sb(last, "hidden1", [R, NT, E])
            normed_all = space.sb(last, "normed_all1", [R, NT, E])
            weights = SharedWeights(space, last)
            rest = (weights, hidden, normed_all, slot_rows, expert_rows, slots, shares, out, ident)
            with space.part():
                move_stream(nc, space, "from_stream", hidden[:, :, :], stream.rearrange("t r e -> r t e"))
                route(nc, space, "r1", io["gate1"], True, hidden, normed_all, slots, shares, jobs, ident, eps, spare)
                share_experts(nc, space, "s0", io, False, *rest)
            with space.part():
                run_experts(nc, space, "x1", [io["wg"], io["wu"]], None, io["wd"], None, 352, jobs, slot_rows, expert_rows, ident)
                share_experts(nc, space, "s1", io, True, *rest)


def move_stream(nc, space, name, dst, src):
    with ExitStack() as stack:
        moved = space.sem(f"{name}_moved")
        block = stack.enter_context(nc.Block())

        @block.sync
        def _(sp):
            sp.dma_start(dst, src).then_inc(moved, 16)
            sp.wait_ge(moved, 16)


def lay_out(a):
    import numpy as np

    x = np.asarray(a["x"])
    side, size = 6, 16
    patches = x.reshape(BATCH, 3, side, size, side, size).transpose(0, 2, 4, 3, 5, 1).reshape(BATCH, PATCHES, PD)
    tokens = np.zeros((NT * SPT, SEQ, PD), x.dtype)
    tokens[:BATCH, 2:] = patches
    w = {k: np.asarray(v) for k, v in a.items() if k != "x"}

    chan = np.arange(4 * DIM)
    z, xc, bc = chan[0:DIM], chan[DIM:2 * DIM], chan[2 * DIM:2 * DIM + 2 * STATE]
    dt = 2 * DIM + 2 * STATE + np.arange(HEADS)
    all_levels = 15
    level_chan = (2 * DIM + 2 * STATE + HEADS + all_levels * np.arange(HEADS)[None, :]
                  + np.array([1, 0] + list(range(2, LEVELS)))[:, None]).reshape(-1)
    order = np.concatenate([bc, xc, z, dt, level_chan])
    bias = w["L1_attn_in_proj_b"][order]
    conv = np.concatenate([w["L1_attn_conv_w"][DIM:], w["L1_attn_conv_w"][:DIM]])

    seq, pos = np.divmod(np.arange(R), SEQ)
    same = seq[:, None] == seq[None, :]
    later = same & (pos[:, None] > pos[None, :])
    upto = pos[:, None] <= np.arange(SEQ)[None, :]
    causal = same & (pos[:, None] <= pos[None, :])
    odd = np.stack([pos % 2 == 1, pos % 2 == 0], axis=1)
    level_of = np.zeros((LEVELS, SPT, SEQ // 2, SPT, SEQ), bool)
    for m in range(SEQ // 2):
        for key in range(2 * m + 2):
            row = key - 2 * m if key >= 2 * m else (key ^ (2 * m)).bit_length()
            for b in range(SPT):
                level_of[row, b, m, b, key] = True
    flat = {
        "later": later, "upto": upto, "causal": causal, "block_of": same, "odd": odd,
        "level_of": np.stack([level_of, level_of]).reshape(LROWS, SEQ // 2, R),
    }
    laid = {
        "patches": tokens.reshape(NT, R, PD),
        "proj": w["L0_tok_W_proj"],
        "proj_bias": w["L0_tok_b_proj"].reshape(1, E),
        "ln1_g": w["L0_tok_ln1_g"].reshape(KP, 128).T,
        "ln1_b": w["L0_tok_ln1_b"].reshape(KP, 128).T,
        "ln2_g": w["L0_tok_ln2_g"],
        "ln2_b": w["L0_tok_ln2_b"],
        "inner_cls": w["L0_tok_cls_token"].reshape(1, E),
        "positions": w["L0_tok_pos_emb"].reshape(PATCHES + 1, E),
        "outer_cls": w["cls_tok"].reshape(1, E),
        "wqT": w["L0_attn_wq"].T,
        "wkT": w["L0_attn_wk"].T,
        "wvT": w["L0_attn_wv"].T,
        "woT": w["L0_attn_wo"].T,
        "gate0": w["L0_ffn_W_gate"],
        "w_in": w["L0_ffn_W_in"],
        "b_in": w["L0_ffn_b_in"].reshape(EXPERTS, -1, 128).transpose(2, 0, 1),
        "w_out": w["L0_ffn_W_out"],
        "b_out": w["L0_ffn_b_out"],
        "in_proj": w["L1_attn_in_proj_w"][order].T,
        "fm_bias": bias[:FM_TILES * 128].reshape(FM_TILES, 128).T,
        "dtl_bias": bias[FM_TILES * 128:],
        "taps": conv.reshape(CONV_TILES, 128, TAPS).transpose(1, 0, 2),
        "dt_bias": w["L1_attn_dt_bias"],
        "factor": w["L1_attn_L"][:, [1, 0] + list(range(2, LEVELS))].T.reshape(-1),
        "a_log": w["L1_attn_A_log"],
        "skip": np.repeat(w["L1_attn_D"], HD).reshape(Z_TILES, 128).T,
        "norm_w": w["L1_attn_norm_w"].reshape(Z_TILES, 128).T,
        "out_proj": w["L1_attn_out_proj_w"].T,
        "out_bias": w["L1_attn_out_proj_b"],
        "gate1": w["L1_ffn_gate_w"].T,
        "wg": w["L1_ffn_wg"],
        "wu": w["L1_ffn_wu"],
        "wd": w["L1_ffn_wd"],
        "swg": w["L1_ffn_swg"],
        "swu": w["L1_ffn_swu"],
        "swd": w["L1_ffn_swd"],
    }
    laid |= {k: np.where(v, np.float32(1), np.float32(0)) for k, v in flat.items()}
    return {k: np.ascontiguousarray(v) for k, v in laid.items()}


def kernel(**inputs):
    import concourse.bacc as bacc
    from concourse.bass_utils import run_bass_kernel_spmd

    nc = bacc.Bacc("TRN2", target_bir_lowering=False, num_devices=1)
    laid = lay_out(inputs)
    io = {k: nc.dram_tensor(f"in_{k}", v.shape, mybir.dt.from_np(v.dtype), kind="ExternalInput").ap() for k, v in laid.items()}
    out = nc.dram_tensor("out", (BATCH * SEQ, E), F32, kind="ExternalOutput").ap()
    tower(nc, io, out)
    r = run_bass_kernel_spmd(nc, [{f"in_{k}": v for k, v in laid.items()}], core_ids=[0])
    return r.results[0]["out"].reshape(BATCH, SEQ, E)
```

```python
import concourse.bass as bass
from concourse import mybir
from contextlib import ExitStack, contextmanager

F32 = mybir.dt.float32
F32R = mybir.dt.float32r
U32 = mybir.dt.uint32
I32 = mybir.dt.int32
ALU = mybir.AluOpType
ACT = mybir.ActivationFunctionType
AX = mybir.AxisListType

BATCH = 64
PATCHES = 36
SEQ = PATCHES + 2
E = 256
KE = E // 128
PD = 3 * 16 * 16
KP = PD // 128
SPT = 3
R = SPT * SEQ
NT = -(-BATCH // SPT)
TOK = NT * R
PAIRS = NT // 2
G2 = 2 * R
LN_EPS = 1e-5
assert NT % 2 == 0 and R <= 128


class Chain:

    def __init__(self, eng, sem, spare=None):
        self.eng, self.sem, self.n, self.base = eng, sem, 0, 0
        self.spare = spare

    def __call__(self, ins, apart=False):
        self.n += 1
        ins.then_inc(self.sem, 1)
        self.eng.wait_ge(self.sem, self.base + self.n)
        if apart:
            self.eng.memset(self.spare[:, :], 0.0)

    def enter(self, turn, per_turn):
        self.start = self.n
        self.base = turn * per_turn

    def leave(self, turns, per_turn):
        assert self.n - self.start == per_turn, (self.n - self.start, per_turn)
        self.base = 0
        self.n = self.start + turns * per_turn


def moments(v, step, x, stats, mv):
    n = x.shape[-1]
    chunk = n // 2 if n > 512 else n
    for c in range(n // chunk):
        ins = v.bn_stats(stats[:, c, :], x[:, c * chunk:(c + 1) * chunk])
    step(ins, apart=True)
    return v.bn_aggr(mv, stats[:, 0:n // chunk, :].rearrange("p c s -> p (c s)"))


ROOT_STEPS = 12


def inverse_root(v, sem, base, out, x, work, var):
    MAGIC = 0x5F3759DF
    steps = [lambda: v.tensor_scalar(x, var, LN_EPS, None, ALU.add),
             lambda: v.tensor_scalar(work.bitcast(I32), x.bitcast(I32), 1, None, ALU.logical_shift_right),
             lambda: v.tensor_scalar(out.bitcast(I32), work.bitcast(I32), -1, MAGIC, ALU.mult, ALU.add)]
    for _ in range(3):
        steps += [lambda: v.tensor_tensor(work, out, out, ALU.mult),
                  lambda: v.scalar_tensor_tensor(work, work, -0.5, x, ALU.mult, ALU.mult),
                  lambda: v.scalar_tensor_tensor(out, work, 1.5, out, ALU.add, ALU.mult)]
    assert len(steps) == ROOT_STEPS
    for n, one in enumerate(steps):
        if n:
            v.wait_ge(sem, base + n)
        one().then_inc(sem, 1)
        yield


def normalize(v, out, x, mv, rstd):
    return v.tensor_scalar(out, x, mv[:, 0:1], rstd, ALU.subtract, ALU.mult)


class Space:

    def __init__(self, nc):
        self.nc, self.sems = nc, []

    @contextmanager
    def part(self):
        yield
        self.nc.clear_and_free_semaphores(self.sems)
        self.nc.all_engine_barrier()
        self.sems = []

    def sb(self, stack, name, shape, dt=F32):
        return stack.enter_context(self.nc.sbuf_tensor(name, shape, dt))

    def sb_twice(self, stack, name, shape, dt, name2, shape2, dt2=F32):
        base = -(-self.nc.sbuf_base // 32) * 32
        first = self.sb(stack, name, shape, dt)
        return first, self.nc.alloc_sbuf_tensor_at(name2, shape2, dt2, offset=base)

    def ps(self, stack, name, shape):
        return stack.enter_context(self.nc.psum_tensor(name, shape, F32))

    def sem(self, name):
        self.sems.append(self.nc.alloc_semaphore(name=name))
        return self.sems[-1]


def tokenize(nc, space, io, hidden, to_clear, ident, ones_row, eps, spare):
    with ExitStack() as stack:
        def sb(name, shape, dt=F32):
            return space.sb(stack, name, shape, dt)

        patches = sb("tk_patches", [R, 2, PD])
        normed = sb("tk_normed", [R, 2, PD])
        normedT = sb("tk_normedT", [128, 2, KP, R])
        proj = sb("tk_proj", [128, KP, E])
        proj_bias = sb("tk_proj_bias", [1, E])
        ln1_g = sb("tk_ln1_g", [128, KP])
        ln1_b = sb("tk_ln1_b", [128, KP])
        gain = sb("tk_gain", [R, E])
        shift = sb("tk_shift", [R, E])
        place = sb("tk_place", [R, E])
        stats = sb("tk_stats", [R, 2, 2, 6])
        z_stats = sb("tk_z_stats", [R, 2, 2, 6])
        mv = sb("tk_mv", [R, 2, 2])
        std = sb("tk_std", [R, 2])
        rstd = sb("tk_rstd", [R, 2])
        mv2 = sb("tk_mv2", [R, 2, 2])
        std2 = sb("tk_std2", [R, 2])
        rstd2 = sb("tk_rstd2", [R, 2])
        z_normed = sb("tk_z_normed", [R, 2, E])
        z_gained = sb("tk_z_gained", [R, 2, E])
        pieces = PAIRS - 2
        zeros = sb("tk_zeros", [128, to_clear[0].shape[0] // (128 * pieces) * E])
        turned = [space.ps(stack, f"tk_turned{i}", [128, 2, 512]) for i in range(2)]
        z = [space.ps(stack, f"tk_z{i}", [128, 512]) for i in range(2)]

        const_loaded = space.sem("tk_const_loaded")
        rows_loaded = space.sem("tk_rows_loaded")
        gain_cleared = space.sem("tk_gain_cleared")
        ident_zeroed = space.sem("tk_ident_zeroed")
        ident_ready = space.sem("tk_ident_ready")
        place_ready = space.sem("tk_place_ready")
        patches_loaded = [space.sem(f"tk_patches_loaded{i}") for i in range(2)]
        normed_ready = space.sem("tk_normed_ready")
        turned_ready = space.sem("tk_turned_ready")
        normedT_by_act = space.sem("tk_normedT_by_act")
        normedT_by_vec = space.sem("tk_normedT_by_vec")
        z_ready = space.sem("tk_z_ready")
        z_normed_ready = space.sem("tk_z_normed_ready")
        vec_step = space.sem("tk_vec_step")
        moments_ready = space.sem("tk_moments_ready")
        std_ready = space.sem("tk_std_ready")
        z_moments_ready = space.sem("tk_z_moments_ready")
        z_std_ready = space.sem("tk_z_std_ready")
        gained_ready = space.sem("tk_gained_ready")
        zeros_ready = space.sem("tk_zeros_ready")
        cleared = space.sem("tk_cleared")
        all_const = 16 * 4

        block = stack.enter_context(nc.Block())

        @block.sync
        def _(sp):
            with sp.Fori(0, PAIRS) as i:
                for half in range(2):
                    sp.wait_ge(normed_ready, 2 * i + half + 1)
                    sp.dma_start(patches[:, half, :], io["patches"][2 * i + half]).then_inc(patches_loaded[half], 16)

        @block.scalar
        def _(act):
            act.wait_ge(ident_ready, 3)
            act.dma_start(proj[:, :, :], io["proj"].rearrange("(k p) n -> p k n", p=128)).then_inc(const_loaded, 16)
            act.dma_start(ln1_g[:, :], io["ln1_g"]).then_inc(const_loaded, 16)
            act.dma_start(ln1_b[:, :], io["ln1_b"]).then_inc(const_loaded, 16)
            act.dma_start(proj_bias[:, :], io["proj_bias"]).then_inc(const_loaded, 16)
            act.wait_ge(const_loaded, all_const)

            def std_of(i, mv, std, count):
                act.wait_ge((moments_ready, z_moments_ready)[count], 2 * i + 2)
                act.activation(std[:, :], mv[:, :, 1], ACT.Sqrt, bias=eps[:, :]).then_inc((std_ready, z_std_ready)[count], 1)

            def turned_high(i):
                for half in range(2):
                    act.wait_ge(turned_ready, 2 * i + half + 1)
                    for k in range(KP // 2, KP):
                        ins = act.activation(normedT[:, half, k, :], turned[half][:, 1, (k - KP // 2) * R:(k - KP // 2 + 1) * R],
                                             ACT.Identity, bias=ln1_b[:, k:k + 1], scale=ln1_g[:, k:k + 1])
                    ins.then_inc(normedT_by_act, 1)

            std_of(0, mv, std, 0)
            turned_high(0)
            act.wait_ge(gain_cleared, 2)
            for s in range(SPT):
                first, rest = s * SEQ, (s + 1) * SEQ
                act.dma_start(gain[first + 2:rest, :], io["ln2_g"].partition_broadcast(PATCHES)).then_inc(rows_loaded, 16)
                act.dma_start(shift[first + 2:rest, :], io["ln2_b"].partition_broadcast(PATCHES)).then_inc(rows_loaded, 16)
                act.dma_start(shift[first + 1:first + 2, :], io["inner_cls"]).then_inc(rows_loaded, 16)
                act.dma_start(place[first + 1:rest, :], io["positions"]).then_inc(rows_loaded, 16)
                act.dma_start(place[first:first + 1, :], io["outer_cls"]).then_inc(rows_loaded, 16)
            act.wait_ge(zeros_ready, 1)

            def turn(i):
                std_of(i + 1, mv, std, 0)
                std_of(i, mv2, std2, 1)
                turned_high(i + 1)

            whole = pieces * 128 * (zeros.shape[1] // E)
            for rows in to_clear:
                rest = rows[whole:].rearrange("(p s) e -> p (s e)", p=128)
                act.dma_start(rest, zeros[:, 0:rest.shape[1]]).then_inc(cleared, 16)
            with act.Fori(0, pieces) as i:
                for rows in to_clear:
                    act.dma_start(rows[0:whole].rearrange("(c p s) e -> c p (s e)", p=128, c=pieces)[i], zeros[:, :]).then_inc(cleared, 16)
                turn(i)
            turn(PAIRS - 2)
            std_of(PAIRS - 1, mv2, std2, 1)
            act.wait_ge(cleared, 16 * (pieces + 1) * len(to_clear))

        @block.gpsimd
        def _(pool):
            pool.memset(eps[:, :], LN_EPS).then_inc(ident_ready, 1)
            pool.memset(ident[:, :], 0.0).then_inc(ident_zeroed, 1)
            pool.wait_ge(ident_zeroed, 1)
            pool.affine_select(out=ident[:, :], in_=ident[:, :], compare_op=ALU.not_equal, fill=1.0, base=0,
                               pattern=[[-1, 128]], channel_multiplier=1).then_inc(ident_ready, 1)
            pool.memset(ones_row[:, :], 1.0).then_inc(ident_ready, 1)
            pool.memset(gain[:, :], 0.0).then_inc(gain_cleared, 1)
            pool.memset(shift[:, :], 0.0).then_inc(gain_cleared, 1)
            pool.memset(zeros[:, :], 0.0).then_inc(zeros_ready, 1)
            pool.wait_ge(rows_loaded, 16 * 5 * SPT)
            pool.tensor_tensor(place[:, :], place[:, :], shift[:, :], ALU.add).then_inc(place_ready, 1)
            pool.wait_ge(place_ready, 1)
            pool.sem_inc(gained_ready, 2)
            with pool.Fori(0, PAIRS) as i:
                for half in range(2):
                    pool.wait_ge(z_normed_ready, 2 * i + half + 3)
                    pool.tensor_tensor(z_gained[:, half, :], z_normed[:, half, :], gain[:, :], ALU.mult).then_inc(gained_ready, 1)
                    pool.wait_ge(gained_ready, 2 * i + half + 3)
                    pool.tensor_tensor(hidden[:, 2 * i + half, :], z_gained[:, half, :], place[:, :], ALU.add)

        @block.vector
        def _(v):
            step = Chain(v, vec_step, spare)

            def front_normed(i):
                for half in range(2):
                    v.wait_ge(patches_loaded[half], 16 * i + 16)
                    moments(v, step, patches[:, half, :], stats[:, half], mv[:, half, :]).then_inc(moments_ready, 1)
                v.wait_ge(std_ready, i + 1)
                step(v.reciprocal(rstd[:, :], std[:, :]))
                for half in range(2):
                    normalize(v, normed[:, half, :], patches[:, half, :], mv[:, half, :], rstd[:, half:half + 1]).then_inc(normed_ready, 1)

            def turned_low(i, half):
                v.wait_ge(turned_ready, 2 * i + half + 1)
                for k in range(KP // 2):
                    ins = v.tensor_scalar(normedT[:, half, k, :], turned[half][:, 0, k * R:(k + 1) * R],
                                          ln1_g[:, k:k + 1], ln1_b[:, k:k + 1], ALU.mult, ALU.add)
                ins.then_inc(normedT_by_vec, 1)

            def z_moments(i, half):
                v.wait_ge(z_ready, 2 * i + half + 1)
                moments(v, step, z[half][0:R, 0:E], z_stats[:, half], mv2[:, half, :]).then_inc(z_moments_ready, 1)

            def z_normalized(i, half):
                v.wait_ge(gained_ready, 2 * i + half + 1)
                normalize(v, z_normed[:, half, :], z[half][0:R, 0:E], mv2[:, half, :], rstd2[:, half:half + 1]).then_inc(z_normed_ready, 1)

            def turn(i, last):
                if not last:
                    front_normed(i + 1)
                z_moments(i, 0)
                z_moments(i, 1)
                if not last:
                    turned_low(i + 1, 0)
                v.wait_ge(z_std_ready, i + 1)
                step(v.reciprocal(rstd2[:, :], std2[:, :]))
                z_normalized(i, 0)
                if not last:
                    turned_low(i + 1, 1)
                z_normalized(i, 1)

            v.sem_inc(normed_ready, 2)
            v.sem_inc(z_normed_ready, 2)
            front_normed(0)
            v.wait_ge(const_loaded, all_const)
            turned_low(0, 0)
            turned_low(0, 1)
            per_turn = 2 * 2 + 2
            with v.Fori(0, PAIRS - 1) as i:
                step.enter(i, per_turn)
                turn(i, False)
                step.leave(PAIRS - 1, per_turn)
            turn(PAIRS - 1, True)

        @block.tensor
        def _(pe):
            def front_turn(i):
                for half in range(2):
                    pe.wait_ge(normed_ready, 2 * i + half + 3)
                    for k in range(KP):
                        c, j = divmod(k, KP // 2)
                        ins = pe.transpose(turned[half][:, c, j * R:(j + 1) * R], normed[:, half, k * 128:(k + 1) * 128],
                                           ident[0:R, 0:R])
                    ins.then_inc(turned_ready, 1)

            def project(i):
                for half in range(2):
                    pe.wait_ge(normedT_by_act, 2 * i + half + 1)
                    pe.wait_ge(normedT_by_vec, 2 * i + half + 1)
                    pe.wait_ge(z_normed_ready, 2 * i + half + 1)
                    for k in range(KP):
                        pe.matmul(z[half][0:R, 0:E], normedT[:, half, k, :], proj[:, k, :], start=(k == 0), stop=False)
                    pe.matmul(z[half][0:R, 0:E], ones_row[:, 0:R], proj_bias[:, :], start=False, stop=True).then_inc(z_ready, 1)

            pe.wait_ge(ident_ready, 3)
            front_turn(0)
            pe.wait_ge(const_loaded, all_const)
            with pe.Fori(0, PAIRS - 1) as i:
                project(i)
                front_turn(i + 1)
            project(PAIRS - 1)


def attend(nc, space, io, hidden, ident, eps, spare):
    D = 64
    scale = (3.0 / D) ** 0.5
    with ExitStack() as stack:
        def sb(name, shape, dt=F32):
            return space.sb(stack, name, shape, dt)

        wq = sb("at_wq", [128, KE, D])
        wk = sb("at_wk", [128, KE, D])
        wv = sb("at_wv", [128, KE, D])
        wo = sb("at_wo", [D, E])
        same = sb("at_same", [R, R])
        stats = sb("at_stats", [R, 2, 1, 6])
        mv = sb("at_mv", [R, 2, 2])
        std = sb("at_std", [R, 2])
        rstd = sb("at_rstd", [R, 2])
        normed = sb("at_normed", [R, 2, E])
        normedT = sb("at_normedT", [128, 2, KE, R])
        qkT = sb("at_qkT", [D, 2, 2, R])
        vals = sb("at_vals", [R, 2, D])
        scoresT = sb("at_scoresT", [R, 2, R])
        contextT = sb("at_contextT", [D, 2, R])
        ps_turned = [space.ps(stack, f"at_ps_turned{i}", [128, 512]) for i in range(2)]
        ps_qkv = [space.ps(stack, f"at_ps_qkv{i}", [128, 512]) for i in range(2)]
        ps_mix = [space.ps(stack, f"at_ps_mix{i}", [128, 512]) for i in range(2)]
        ps_out = [space.ps(stack, f"at_ps_out{i}", [128, 512]) for i in range(2)]

        loaded = space.sem("at_loaded")
        same_step = space.sem("at_same_step")
        vec_step = space.sem("at_vec_step")
        moments_ready = space.sem("at_moments_ready")
        std_ready = space.sem("at_std_ready")
        normed_ready = space.sem("at_normed_ready")
        turned_ready = space.sem("at_turned_ready")
        normedT_ready = space.sem("at_normedT_ready")
        qkv_ready = space.sem("at_qkv_ready")
        qkv_copied = space.sem("at_qkv_copied")
        scores_ready = space.sem("at_scores_ready")
        scores_masked = space.sem("at_scores_masked")
        context_ready = space.sem("at_context_ready")
        context_copied = space.sem("at_context_copied")
        out_ready = space.sem("at_out_ready")
        added = space.sem("at_added")

        block = stack.enter_context(nc.Block())

        @block.sync
        def _(sp):
            for w, name in ((wq, "wqT"), (wk, "wkT"), (wv, "wvT")):
                sp.dma_start(w[:, :, :], io[name].rearrange("(k p) n -> p k n", p=128)).then_inc(loaded, 16)
            sp.dma_start(wo[:, :], io["woT"]).then_inc(loaded, 16)

        @block.gpsimd
        def _(pool):
            pool.memset(same[:, :], scale).then_inc(same_step, 1)
            pool.wait_ge(same_step, 1)
            cols = same[:, :].rearrange("p (s t) -> p s t", s=SPT)
            pool.affine_select(out=cols, in_=cols, compare_op=ALU.is_ge, fill=0.0, base=0,
                               pattern=[[-SEQ, SPT], [0, SEQ]], channel_multiplier=1).then_inc(same_step, 1)
            pool.wait_ge(same_step, 2)
            pool.affine_select(out=cols, in_=cols, compare_op=ALU.is_ge, fill=0.0, base=SEQ - 1,
                               pattern=[[SEQ, SPT], [0, SEQ]], channel_multiplier=-1).then_inc(same_step, 1)

        @block.vector
        def _(v):
            step = Chain(v, vec_step, spare)

            def front_moments(i):
                for half in range(2):
                    moments(v, step, hidden[:, 2 * i + half, :], stats[:, half], mv[:, half, :]).then_inc(moments_ready, 1)

            def front_normed(i):
                v.wait_ge(std_ready, i + 1)
                step(v.reciprocal(rstd[:, :], std[:, :]))
                for half in range(2):
                    normalize(v, normed[:, half, :], hidden[:, 2 * i + half, :], mv[:, half, :],
                              rstd[:, half:half + 1]).then_inc(normed_ready, 1)

            def turn(i, ahead):
                for half in range(2):
                    v.wait_ge(scores_ready, 2 * i + half + 1)
                    v.tensor_tensor(scoresT[:, half, :], ps_mix[half][0:R, 0:R], same[:, :], ALU.mult).then_inc(scores_masked, 1)
                if ahead >= 2:
                    front_moments(i + 2)
                    v.wait_ge(turned_ready, 2 * i + 4)
                    front_normed(i + 2)
                for half in range(2):
                    v.wait_ge(out_ready, 2 * i + half + 1)
                    v.tensor_tensor(hidden[:, 2 * i + half, :], hidden[:, 2 * i + half, :], ps_out[half][0:R, 0:E],
                                    ALU.add).then_inc(added, 1)

            v.wait_ge(same_step, 3)
            front_moments(0)
            front_normed(0)
            front_moments(1)
            v.wait_ge(turned_ready, 2)
            front_normed(1)
            per_turn = 2 + 1
            with v.Fori(0, PAIRS - 2) as i:
                step.enter(i, per_turn)
                turn(i, 2)
                step.leave(PAIRS - 2, per_turn)
            turn(PAIRS - 2, 1)
            turn(PAIRS - 1, 0)

        @block.scalar
        def _(act):
            def front_std(i):
                act.wait_ge(moments_ready, 2 * i + 2)
                act.activation(std[:, :], mv[:, :, 1], ACT.Sqrt, bias=eps[:, :]).then_inc(std_ready, 1)

            def front_turned(i):
                for half in range(2):
                    act.wait_ge(turned_ready, 2 * i + half + 1)
                    act.copy(normedT[:, half, :, :].rearrange("p k r -> p (k r)"), ps_turned[half][:, 0:G2]).then_inc(normedT_ready, 1)

            def front_qkv(i):
                for half in range(2):
                    act.wait_ge(qkv_ready, 2 * i + half + 1)
                    act.copy(qkT[:, half, :, :].rearrange("p k r -> p (k r)"), ps_qkv[half][0:D, 0:G2])
                    act.copy(vals[:, half, :], ps_qkv[half][0:R, G2:G2 + D]).then_inc(qkv_copied, 1)

            def turn(i, ahead):
                if ahead >= 1:
                    front_turned(i + 1)
                for half in range(2):
                    act.wait_ge(context_ready, 2 * i + half + 1)
                    act.copy(contextT[:, half, :], ps_mix[half][0:D, 128:128 + R]).then_inc(context_copied, 1)
                if ahead >= 2:
                    front_std(i + 2)
                if ahead >= 1:
                    front_qkv(i + 1)

            front_std(0)
            front_turned(0)
            front_std(1)
            front_qkv(0)
            with act.Fori(0, PAIRS - 2) as i:
                turn(i, 2)
            turn(PAIRS - 2, 1)
            turn(PAIRS - 1, 0)

        @block.tensor
        def _(pe):
            def front_turn(i):
                for half in range(2):
                    pe.wait_ge(normed_ready, 2 * i + half + 1)
                    for k in range(KE):
                        ins = pe.transpose(ps_turned[half][:, k * R:(k + 1) * R], normed[:, half, k * 128:(k + 1) * 128], ident[0:R, 0:R])
                    ins.then_inc(turned_ready, 1)

            def front_qkv(i):
                for half in range(2):
                    pe.wait_ge(normedT_ready, 2 * i + half + 1)
                    for c, w in enumerate((wq, wk)):
                        for k in range(KE):
                            pe.matmul(ps_qkv[half][0:D, c * R:(c + 1) * R], w[:, k, :], normedT[:, half, k, :],
                                      start=(k == 0), stop=(k == KE - 1))
                    for k in range(KE):
                        ins = pe.matmul(ps_qkv[half][0:R, G2:G2 + D], normedT[:, half, k, :], wv[:, k, :],
                                        start=(k == 0), stop=(k == KE - 1))
                    ins.then_inc(qkv_ready, 1)

            def turn(i, last):
                for half in range(2):
                    pe.wait_ge(qkv_copied, 2 * i + half + 1)
                    pe.matmul(ps_mix[half][0:R, 0:R], qkT[:, half, 1, :], qkT[:, half, 0, :], start=True, stop=True).then_inc(scores_ready, 1)
                if not last:
                    front_turn(i + 1)
                for half in range(2):
                    pe.wait_ge(scores_masked, 2 * i + half + 1)
                    pe.matmul(ps_mix[half][0:D, 128:128 + R], vals[:, half, :], scoresT[:, half, :], start=True, stop=True).then_inc(context_ready, 1)
                if not last:
                    front_qkv(i + 1)
                for half in range(2):
                    pe.wait_ge(context_copied, 2 * i + half + 1)
                    pe.matmul(ps_out[half][0:R, 0:E], contextT[:, half, :], wo[:, :], start=True, stop=True).then_inc(out_ready, 1)

            pe.wait_ge(loaded, 64)
            front_turn(0)
            front_qkv(0)
            with pe.Fori(0, PAIRS - 1) as i:
                turn(i, False)
            turn(PAIRS - 1, True)


EXPERTS = 8
JOB = 256
SUB = JOB // 128
MAX_JOBS = (2 * TOK + EXPERTS * 2 * JOB) // JOB
SLOTS = (MAX_JOBS + 2) * JOB
MOST = -(-TOK // JOB)
BIG = 1e38


def route(nc, space, name, gate_dram, scores_softmaxed, hidden, normed_all, slots, shares, jobs, stream,
          ident, eps, spare, shared=None, shared_dram=None, expert=None, expert_dram=None):
    with ExitStack() as stack:
        def sb(what, shape, dt=F32):
            return space.sb(stack, f"{name}_{what}", shape, dt)

        def sem(what):
            return space.sem(f"{name}_{what}")

        gate = sb("gate", [128, KE, EXPERTS])
        before = sb("before", [R, R])
        ones = sb("ones", [R, R])
        prefer = sb("prefer", [R, EXPERTS])
        steps_of = sb("steps_of", [R, MOST - 1])
        stats = sb("stats", [R, 2, 1, 6])
        mv = sb("mv", [R, 2, 2])
        std = sb("std", [R, 2])
        rstd = sb("rstd", [R, 2])
        normed_half = sb("normed_half", [R, 2, E])
        normedT = sb("normedT", [128, 2, KE, R])
        scores = sb("scores", [R, NT, EXPERTS])
        rest = sb("rest", [R, NT, EXPERTS])
        equal = sb("equal", [R, NT, EXPERTS])
        chosen = sb("chosen", [R, 2, NT, EXPERTS])
        both = sb("both", [R, NT, EXPERTS])
        top = sb("top", [R, 2, NT])
        pick = sb("pick", [R, 2, NT])
        expd = sb("expd", [R, NT, EXPERTS])
        total = sb("total", [R, NT])
        gap = sb("gap", [R, NT])
        run = sb("run", [R, 2, NT, EXPERTS])
        place = sb("place", [R, NT, EXPERTS])
        over = sb("over", [R, EXPERTS, MOST - 1])
        count = sb("count", [R, EXPERTS])
        ends = sb("ends", [R, 2, EXPERTS])
        first = sb("first", [R, EXPERTS])
        base = sb("base", [R, EXPERTS])
        slot_f = sb("slot_f", [R, 2, NT])
        ps_turned = [space.ps(stack, f"{name}_ps_turned{i}", [128, 512]) for i in range(2)]
        ps_gate = [space.ps(stack, f"{name}_ps_gate{i}", [128, 512]) for i in range(2)]
        ps_before = space.ps(stack, f"{name}_ps_before", [128, 512])
        ps_total = space.ps(stack, f"{name}_ps_total", [128, 512])

        loaded = sem("loaded")
        hidden_in = sem("hidden_in")
        shared_loaded = sem("shared_loaded")
        expert_loaded = sem("expert_loaded")
        shared_high = sem("shared_high")
        consts = sem("consts")
        const_step = sem("const_step")
        vec_step = sem("vec_step")
        moments_ready = sem("moments_ready")
        std_ready = sem("std_ready")
        normed_ready = sem("normed_ready")
        turned_ready = sem("turned_ready")
        normedT_ready = sem("normedT_ready")
        gate_ready = sem("gate_ready")
        gate_read = sem("gate_read")
        kept = sem("kept")
        exp_in = sem("exp_in")
        exp_out = sem("exp_out")
        both_ready = sem("both_ready")
        counted = sem("counted")

        block = stack.enter_context(nc.Block())

        @block.sync
        def _(sp):
            sp.dma_start(gate[:, :, :], gate_dram.rearrange("(k p) n -> p k n", p=128)).then_inc(loaded, 16)
            if stream is not None:
                sp.sem_inc(hidden_in, 16)
                with sp.Fori(0, PAIRS) as i:
                    sp.wait_ge(hidden_in, 16 * i + 16)
                    sp.dma_start(hidden[:, bass.ds(2 * i, 2), :], stream.rearrange("(i t) r e -> i r t e", t=2)[i]).then_inc(hidden_in, 16)

        @block.gpsimd
        def _(pool):
            pool.memset(ones[:, :], 1.0).then_inc(consts, 1)
            pool.memset(before[:, :], 1.0).then_inc(const_step, 1)
            for e in range(EXPERTS):
                ins = pool.memset(prefer[:, e:e + 1], float(EXPERTS - e))
            ins.then_inc(consts, 1)
            for c in range(MOST - 1):
                ins = pool.memset(steps_of[:, c:c + 1], float(JOB * (c + 1)))
            ins.then_inc(consts, 1)
            pool.wait_ge(const_step, 1)
            pool.affine_select(out=before[:, :], in_=before[:, :], compare_op=ALU.is_ge, fill=0.0, base=-1,
                               pattern=[[1, R]], channel_multiplier=-1).then_inc(consts, 1)
            with pool.Fori(0, PAIRS) as i:
                for half in range(2):
                    pool.wait_ge(normed_ready, 2 * i + half + 1)
                    pool.tensor_copy(normed_all[:, 2 * i + half, :], normed_half[:, half, :]).then_inc(kept, 1)
            if shared:
                pool.wait_ge(shared_high, 1)
                shared.split_low(pool)

        @block.tensor
        def _(pe):
            pe.wait_ge(loaded, 16)

            def front_turn(i):
                for half in range(2):
                    pe.wait_ge(normed_ready, 2 * i + half + 1)
                    for k in range(KE):
                        ins = pe.transpose(ps_turned[half][:, k * R:(k + 1) * R], normed_half[:, half, k * 128:(k + 1) * 128],
                                           ident[0:R, 0:R])
                    ins.then_inc(turned_ready, 1)

            def gate_of(i):
                for half in range(2):
                    pe.wait_ge(normedT_ready, 2 * i + half + 1)
                    for k in range(KE):
                        ins = pe.matmul(ps_gate[half][0:R, 0:EXPERTS], normedT[:, half, k, :], gate[:, k, :],
                                        start=(k == 0), stop=(k == KE - 1))
                    ins.then_inc(gate_ready, 1)

            front_turn(0)
            with pe.Fori(0, PAIRS - 1) as i:
                gate_of(i)
                front_turn(i + 1)
            gate_of(PAIRS - 1)
            pe.wait_ge(both_ready, 1)
            pe.wait_ge(consts, 4)
            flat = both[:, :, :].rearrange("p t e -> p (t e)")
            pe.matmul(ps_before[0:R, 0:NT * EXPERTS], before[:, :], flat, start=True, stop=True)
            pe.matmul(ps_total[0:R, 0:NT * EXPERTS], ones[:, :], flat, start=True, stop=True).then_inc(counted, 1)

        @block.scalar
        def _(act):
            def turn(i):
                act.wait_ge(moments_ready, 2 * i + 2)
                act.activation(std[:, :], mv[:, :, 1], ACT.Sqrt, bias=eps[:, :]).then_inc(std_ready, 1)
                for half in range(2):
                    act.wait_ge(turned_ready, 2 * i + half + 1)
                    act.copy(normedT[:, half, :, :].rearrange("p k r -> p (k r)"), ps_turned[half][:, 0:G2]).then_inc(normedT_ready, 1)

            SPLITS = 6 if shared else 0
            first_turns = 4 if shared else PAIRS
            with act.Fori(0, first_turns) as i:
                turn(i)
            if shared:
                n = shared.load(act, shared_loaded, *shared_dram)
                with act.Fori(first_turns, PAIRS - SPLITS) as i:
                    turn(i)
                m = expert.load(act, expert_loaded, *expert_dram, 0)
            for part in range(SPLITS):
                turn(PAIRS - SPLITS + part)
                act.wait_ge(shared_loaded, 16 * n)
                ins = shared.split_high(act, part, SPLITS)
                if part == SPLITS - 1:
                    ins.then_inc(shared_high, 1)
            if shared:
                act.wait_ge(expert_loaded, 16 * m)
            act.wait_ge(exp_in, 1)
            if scores_softmaxed:
                act.activation(expd[:, :, :], rest[:, :, :], ACT.Exp).then_inc(exp_out, 1)
            else:
                act.activation(total[:, :], gap[:, :], ACT.Exp).then_inc(exp_out, 1)

        @block.vector
        def _(v):
            step = Chain(v, vec_step, spare)

            def front_moments(i):
                if stream is not None:
                    v.wait_ge(hidden_in, 16 * i + 32)
                for half in range(2):
                    moments(v, step, hidden[:, 2 * i + half, :], stats[:, half], mv[:, half, :]).then_inc(moments_ready, 1)

            def front_normed(i):
                v.wait_ge(std_ready, i + 1)
                step(v.reciprocal(rstd[:, :], std[:, :]))
                v.wait_ge(kept, 2 * i + 2)
                for half in range(2):
                    normalize(v, normed_half[:, half, :], hidden[:, 2 * i + half, :], mv[:, half, :],
                              rstd[:, half:half + 1]).then_inc(normed_ready, 1)

            def read_scores(i):
                for half in range(2):
                    v.wait_ge(gate_ready, 2 * i + half + 1)
                    v.tensor_copy(scores[:, 2 * i + half, :], ps_gate[half][0:R, 0:EXPERTS]).then_inc(gate_read, 1)

            v.sem_inc(kept, 2)
            front_moments(0)
            front_normed(0)
            per_turn = 2 + 1
            with v.Fori(0, PAIRS - 1) as i:
                step.enter(i, per_turn)
                front_moments(i + 1)
                read_scores(i)
                front_normed(i + 1)
                step.leave(PAIRS - 1, per_turn)
            read_scores(PAIRS - 1)
            v.wait_ge(gate_read, NT)
            v.wait_ge(consts, 4)

            def per_token(x):
                return x.unsqueeze(2).broadcast_to([R, NT, EXPERTS])

            def per_expert(x):
                return x.unsqueeze(1).broadcast_to([R, NT, EXPERTS])

            if scores_softmaxed:
                step(v.tensor_reduce(top[:, 0, :], scores[:, :, :], AX.X, ALU.max))
                v.tensor_tensor(rest[:, :, :], scores[:, :, :], per_token(top[:, 0, :]), ALU.subtract).then_inc(exp_in, 1)
                v.wait_ge(exp_out, 1)
                step(v.tensor_reduce(total[:, :], expd[:, :, :], AX.X, ALU.add))
                step(v.reciprocal(gap[:, :], total[:, :]))
                step(v.tensor_tensor(scores[:, :, :], expd[:, :, :], per_token(gap[:, :]), ALU.mult))
            for c, values in enumerate((scores, rest)):
                step(v.tensor_reduce(top[:, c, :], values[:, :, :], AX.X, ALU.max))
                step(v.tensor_tensor(equal[:, :, :], values[:, :, :], per_token(top[:, c, :]), ALU.is_equal))
                step(v.tensor_tensor(place[:, :, :], equal[:, :, :], per_expert(prefer[:, :]), ALU.mult))
                step(v.tensor_reduce(pick[:, c, :], place[:, :, :], AX.X, ALU.max))
                step(v.tensor_tensor(chosen[:, c], per_expert(prefer[:, :]), per_token(pick[:, c, :]), ALU.is_equal))
                if c == 0:
                    step(v.scalar_tensor_tensor(rest[:, :, :].rearrange("p t e -> p (t e)"),
                                                chosen[:, 0].rearrange("p t e -> p (t e)"), -BIG,
                                                scores[:, :, :].rearrange("p t e -> p (t e)"), ALU.mult, ALU.add))
            v.tensor_tensor(both[:, :, :], chosen[:, 0], chosen[:, 1], ALU.add).then_inc(both_ready, 1)
            if scores_softmaxed:
                step(v.scalar_tensor_tensor(total[:, :], top[:, 0, :], 1e-20, top[:, 1, :], ALU.add, ALU.add))
                step(v.reciprocal(gap[:, :], total[:, :]))
                step(v.tensor_tensor(shares[:, 0, :], top[:, 0, :], gap[:, :], ALU.mult))
                step(v.tensor_tensor(shares[:, 1, :], top[:, 1, :], gap[:, :], ALU.mult))
            else:
                v.tensor_tensor(gap[:, :], top[:, 1, :], top[:, 0, :], ALU.subtract).then_inc(exp_in, 1)
                v.wait_ge(exp_out, 1)
                step(v.tensor_scalar(pick[:, 0, :], total[:, :], 1.0, None, ALU.add))
                step(v.reciprocal(shares[:, 0, :], pick[:, 0, :]))
                step(v.tensor_tensor(shares[:, 1, :], total[:, :], shares[:, 0, :], ALU.mult))
            v.wait_ge(counted, 1)
            step(v.tensor_copy(run[:, 0].rearrange("p t e -> p (t e)"), ps_total[0:R, 0:NT * EXPERTS]))
            now, reach = 0, 1
            while reach < NT:
                a, b = run[:, now], run[:, 1 - now]
                step(v.tensor_copy(b[:, 0:reach, :], a[:, 0:reach, :]))
                step(v.tensor_tensor(b[:, reach:NT, :], a[:, reach:NT, :], a[:, 0:NT - reach, :], ALU.add))
                now, reach = 1 - now, 2 * reach
            runs = run[:, now]
            step(v.tensor_tensor(over[:, :, :], runs[:, NT - 1, :].unsqueeze(2).broadcast_to([R, EXPERTS, MOST - 1]),
                                 steps_of[:, :].unsqueeze(1).broadcast_to([R, EXPERTS, MOST - 1]), ALU.is_gt))
            step(v.tensor_reduce(count[:, :], over[:, :, :], AX.X, ALU.add))
            step(v.tensor_scalar(count[:, :], count[:, :], 1.0, 2.0, ALU.add, ALU.max))
            step(v.tensor_copy(ends[:, 0, :], count[:, :]))
            now2, reach = 0, 1
            while reach < EXPERTS:
                a, b = ends[:, now2], ends[:, 1 - now2]
                step(v.tensor_copy(b[:, 0:reach], a[:, 0:reach]))
                step(v.tensor_tensor(b[:, reach:EXPERTS], a[:, reach:EXPERTS], a[:, 0:EXPERTS - reach], ALU.add))
                now2, reach = 1 - now2, 2 * reach
            step(v.tensor_tensor(first[:, :], ends[:, now2], count[:, :], ALU.subtract))
            step(v.tensor_copy(jobs[:, 0:EXPERTS], first[0:1, :]))
            step(v.tensor_copy(jobs[:, EXPERTS:EXPERTS + 1], ends[0:1, now2, EXPERTS - 1:EXPERTS]))
            step(v.tensor_scalar(base[:, :], first[:, :], float(JOB), None, ALU.mult))
            step(v.tensor_tensor(place[:, :, :].rearrange("p t e -> p (t e)"), ps_before[0:R, 0:NT * EXPERTS],
                                 runs.rearrange("p t e -> p (t e)"), ALU.add))
            step(v.tensor_tensor(place[:, :, :].rearrange("p t e -> p (t e)"), place[:, :, :].rearrange("p t e -> p (t e)"),
                                 ps_total[0:R, 0:NT * EXPERTS], ALU.subtract))
            step(v.tensor_tensor(place[:, :, :], place[:, :, :], per_expert(base[:, :]), ALU.add))
            for c in range(2):
                step(v.tensor_tensor(equal[:, :, :], chosen[:, c], place[:, :, :], ALU.mult))
                step(v.tensor_reduce(slot_f[:, c, :], equal[:, :, :], AX.X, ALU.add))
                v.tensor_copy(slots[:, c, :], slot_f[:, c, :])


def load_rows(eng, sem, tile, dram):
    rows = dram.shape[0]
    whole = rows // 128
    n = 1
    eng.dma_start(tile[:, 0:whole, :], dram[0:whole * 128].rearrange("(k p) n -> p k n", p=128)).then_inc(sem, 16)
    if rows % 128:
        eng.dma_start(tile[0:rows % 128, whole, :], dram[whole * 128:rows]).then_inc(sem, 16)
        n += 1
    return n


class ExpertWeights:

    def __init__(self, space, stack, name, ups, inner):
        self.inner = inner
        self.KD = -(-inner // 128)
        self.width = [min(128, inner - m * 128) for m in range(self.KD)]
        self.ups = ups
        self.up_raw = space.sb(stack, f"{name}_up_raw", [128, ups, KE, inner])
        self.down_raw = space.sb(stack, f"{name}_down_raw", [128, self.KD, E])
        self.up_hi, self.up_lo = ([space.sb(stack, f"{name}_up_{part}{p}", [128, ups, KE, inner], F32R) for p in range(2)] for part in ("hi", "lo"))
        self.down_hi, self.down_lo = ([space.sb(stack, f"{name}_down_{part}{p}", [128, self.KD, E], F32R) for p in range(2)] for part in ("hi", "lo"))

    def load(self, eng, sem, ups_dram, down_dram, e):
        return sum(load_rows(eng, sem, self.up_raw[:, u], dram[e]) for u, dram in enumerate(ups_dram)) + load_rows(eng, sem, self.down_raw, down_dram[e])

    def split_high(self, act, e, part=0, parts=1):
        p = e % 2
        for u in range(self.ups):
            for k in range(KE):
                a, b = self.inner * part // parts, self.inner * (part + 1) // parts
                ins = act.copy(self.up_hi[p][:, u, k, a:b], self.up_raw[:, u, k, a:b])
        for k in range(self.KD * part // parts, self.KD * (part + 1) // parts):
            ins = act.copy(self.down_hi[p][0:self.width[k], k, :], self.down_raw[0:self.width[k], k, :])
        return ins

    def split_low(self, eng, e, part=0, parts=1):
        self.split_up_low(eng, e, part, parts)
        return self.split_down_low(eng, e, part, parts)

    def split_up_low(self, eng, e, part=0, parts=1):
        p = e % 2
        a, b = self.inner * part // parts, self.inner * (part + 1) // parts
        for u in range(self.ups):
            ins = eng.tensor_tensor(self.up_lo[p][:, u, :, a:b], self.up_raw[:, u, :, a:b], self.up_hi[p][:, u, :, a:b].bitcast(F32), ALU.subtract)
        return ins

    def split_down_low(self, eng, e, part=0, parts=1):
        p = e % 2
        for k in range(self.KD * part // parts, self.KD * (part + 1) // parts):
            w = self.width[k]
            ins = eng.tensor_tensor(self.down_lo[p][0:w, k, :], self.down_raw[0:w, k, :], self.down_hi[p][0:w, k, :].bitcast(F32), ALU.subtract)
        return ins


def run_experts(nc, space, name, ups_dram, up_bias_dram, down_dram, down_bias_dram, inner, jobs, slot_rows, out_rows, ident, weights=None):
    gated = len(ups_dram) == 2
    KD = -(-inner // 128)
    width = [min(128, inner - m * 128) for m in range(KD)]
    U = len(ups_dram)
    with ExitStack() as stack:
        def sb(what, shape, dt=F32):
            return space.sb(stack, f"{name}_{what}", shape, dt)

        def sem(what):
            return space.sem(f"{name}_{what}")

        ahead = int(weights is not None)
        weights = weights or ExpertWeights(space, stack, name, U, inner)
        up_hi, up_lo, down_hi, down_lo = weights.up_hi, weights.up_lo, weights.down_hi, weights.down_lo
        if not gated:
            up_bias = sb("up_bias", [128, EXPERTS, KD])
            down_bias = [sb(f"down_bias{p}", [128, E]) for p in range(2)]
        rows = sb("rows", [128, SUB, E])
        rowsT_hi = sb("rowsT_hi", [128, KE, JOB], F32R)
        rowsT_lo = sb("rowsT_lo", [128, KE, JOB], F32R)
        RING = 4 if not gated else KD
        act_out = sb("act_out", [128, RING, JOB])
        inner_f = sb("inner_f", [128, KD, JOB]) if gated else act_out
        inner_hi = sb("inner_hi", [128, KD, JOB], F32R)
        inner_lo = sb("inner_lo", [128, KD, JOB], F32R)
        result = sb("result", [128, SUB, E])
        ps_rowsT = space.ps(stack, f"{name}_ps_rowsT", [128, KE, JOB])
        AHEAD_TILES = 4
        BANKS = 4 if not gated else KD
        ps_up = [space.ps(stack, f"{name}_ps_up{b}", [128, 512]) for b in range(BANKS)]
        ps_down = [space.ps(stack, f"{name}_ps_down{s}", [128, 512]) for s in range(SUB)]

        raw_loaded = sem("raw_loaded")
        bias_loaded = [sem(f"bias_loaded{p}") for p in range(2)]
        up_bias_loaded = sem("up_bias_loaded")
        weights_high = sem("weights_high")
        up_low = sem("up_low")
        down_low = sem("down_low")
        first_low = sem("first_low")
        rows_loaded = sem("rows_loaded")
        rowsT_ready = sem("rowsT_ready")
        rowsT_hi_ready = sem("rowsT_hi_ready")
        rowsT_split = sem("rowsT_split")
        up_ready = sem("up_ready")
        act_done = sem("act_done")
        inner_done = sem("inner_done")
        inner_hi_done = sem("inner_hi_done")
        inner_split = sem("inner_split")
        down_ready = sem("down_ready")
        result_ready = sem("result_ready")
        result_stored = sem("result_stored")
        raw_dmas = U + (2 if inner % 128 else 1)

        def expert_jobs(eng, e):
            first, end = (eng.value_load(jobs[0:1, n:n + 1], min_val=2 * n, max_val=MAX_JOBS - 2 * (EXPERTS - n))
                          for n in (e, e + 1))
            return first, end

        block = stack.enter_context(nc.Block())

        @block.sync
        def _(sp):
            def load_bias(e):
                if not gated:
                    sp.dma_start(down_bias[e % 2][:, :], down_bias_dram[e].partition_broadcast(128)).then_inc(bias_loaded[e % 2], 16)

            def load_rows_of(job):
                sp.dma_start(rows[:, :, :], slot_rows.rearrange("(j s p) e -> j p s e", s=SUB, p=128)[job]).then_inc(rows_loaded, 16)

            def one_job(j):
                sp.wait_ge(rowsT_ready, j + 2)
                load_rows_of(j + 2)

            def store(j):
                sp.wait_ge(result_ready, j + 2)
                sp.dma_start(out_rows.rearrange("(j s p) e -> j p s e", s=SUB, p=128)[j], result[:, :, :]).then_inc(result_stored, 16)

            if not gated:
                sp.dma_start(up_bias[:, :, :], up_bias_dram).then_inc(up_bias_loaded, 16)
            load_bias(0)
            load_rows_of(0)
            sp.wait_ge(rowsT_ready, 1)
            load_rows_of(1)
            for e in range(EXPERTS):
                first, end = expert_jobs(sp, e)
                one_job(first)
                store(first)
                if e + 1 < EXPERTS:
                    load_bias(e + 1)
                with sp.Fori(first + 1, end) as j:
                    one_job(j)
                    store(j)

        @block.gpsimd
        def _(pool):
            def load_weights(e):
                n = weights.load(pool, raw_loaded, ups_dram, down_dram, e)
                assert n == raw_dmas

            if not ahead:
                load_weights(0)
                pool.wait_ge(first_low, KD)
            load_weights(1)
            for e in range(1, EXPERTS):
                pool.wait_ge(weights_high, KD * (e + 1))
                weights.split_up_low(pool, e).then_inc(up_low, 1)
                if e + 1 < EXPERTS:
                    pool.wait_ge(up_low, e)
                    pool.wait_ge(down_low, KD * e)
                    load_weights(e + 1)
            _, end = expert_jobs(pool, EXPERTS - 1)
            pool.wait_ge(result_stored, 16 * (end + 1))

        @block.scalar
        def _(act):
            def turn_rows(j):
                act.wait_ge(rowsT_ready, j + 1)
                act.copy(rowsT_hi[:, :, :], ps_rowsT[:, :, :]).then_inc(rowsT_hi_ready, 1)

            def split(e, m):
                weights.split_high(act, e, m, KD).then_inc(weights_high, 1)

            def one_job(e, j, split_next, begin=False):
                for m in range(KD):
                    act.wait_ge(up_ready, KD * j + m + 1)
                    r = m % RING
                    if gated:
                        act.activation(act_out[0:width[m], r, :], ps_up[m][0:width[m], 0:JOB], ACT.Silu).then_inc(act_done, 1)
                    else:
                        act.activation(act_out[:, r, :], ps_up[m % BANKS][:, 0:JOB], ACT.Gelu, bias=up_bias[:, e, m:m + 1]).then_inc(act_done, 1)
                    if begin and m + AHEAD_TILES < KD:
                        split(0, m + AHEAD_TILES)
                    if split_next and not begin:
                        if m == 0:
                            act.wait_ge(raw_loaded, 16 * raw_dmas * (e + 2 - ahead))
                        split(e + 1, m)
                turn_rows(j + 1)

            turn_rows(0)
            if ahead:
                act.sem_inc(weights_high, KD)
            else:
                act.wait_ge(raw_loaded, 16 * raw_dmas)
                for m in range(AHEAD_TILES):
                    split(0, m)
            if not gated:
                act.wait_ge(up_bias_loaded, 16)
            for e in range(EXPERTS):
                first, end = expert_jobs(act, e)
                one_job(e, first, e + 1 < EXPERTS, e == 0 and not ahead)
                if e == 0 and not ahead:
                    act.wait_ge(raw_loaded, 16 * raw_dmas * 2)
                    for m in range(KD):
                        split(1, m)
                with act.Fori(first + 1, end) as j:
                    one_job(e, j, False)

        @block.vector
        def _(v):
            def turn_rows(j):
                v.wait_ge(rowsT_hi_ready, j + 1)
                v.tensor_tensor(rowsT_lo[:, :, :], ps_rowsT[:, :, :], rowsT_hi[:, :, :].bitcast(F32), ALU.subtract).then_inc(rowsT_split, 1)

            def split_first(m):
                v.wait_ge(weights_high, m + 1)
                weights.split_low(v, 0, m, KD).then_inc(first_low, 1)

            def split_next(e, m):
                v.wait_ge(weights_high, KD * (e + 1) + m + 1)
                weights.split_down_low(v, e + 1, m, KD).then_inc(down_low, 1)

            def one_job(e, j, begin=False, with_next=False):
                for m in range(KD):
                    w, n = width[m], KD * j + m + 1
                    if begin and m + AHEAD_TILES < KD:
                        split_first(m + AHEAD_TILES)
                    if with_next and m >= 1:
                        split_next(e, m - 1)
                    v.wait_ge(act_done, n)
                    if gated:
                        v.tensor_tensor(inner_f[0:w, m, :], act_out[0:w, m, :], ps_up[m][0:w, JOB:2 * JOB], ALU.mult).then_inc(inner_done, 1)
                        v.wait_ge(inner_done, n)
                    source = inner_f[0:w, m % RING, :]
                    v.tensor_copy(inner_hi[0:w, m, :], source).then_inc(inner_hi_done, 1)
                    v.wait_ge(inner_hi_done, n)
                    v.tensor_tensor(inner_lo[0:w, m, :], source, inner_hi[0:w, m, :].bitcast(F32), ALU.subtract).then_inc(inner_split, 1)
                if with_next:
                    split_next(e, KD - 1)
                turn_rows(j + 1)
                v.wait_ge(down_ready, j + 1)
                v.wait_ge(result_stored, 16 * (j + 1))
                for s in range(SUB):
                    if gated:
                        ins = v.tensor_copy(result[:, s, :], ps_down[s][:, 0:E])
                    else:
                        if s == 0:
                            v.wait_ge(bias_loaded[e % 2], 16 * (e // 2 + 1))
                        ins = v.tensor_tensor(result[:, s, :], ps_down[s][:, 0:E], down_bias[e % 2][:, :], ALU.add)
                ins.then_inc(result_ready, 1)

            v.sem_inc(inner_split, RING)
            v.sem_inc(result_ready, 1)
            v.sem_inc(result_stored, 16)
            turn_rows(0)
            if not ahead:
                for m in range(AHEAD_TILES):
                    split_first(m)
            for e in range(EXPERTS):
                first, end = expert_jobs(v, e)
                begin = e == 0 and not ahead
                one_job(e, first, begin, e + 1 < EXPERTS and not begin)
                if begin:
                    for m in range(KD):
                        split_next(0, m)
                with v.Fori(first + 1, end) as j:
                    one_job(e, j)

        @block.tensor
        def _(pe):
            def turn_rows(j):
                pe.wait_ge(rows_loaded, 16 * (j + 1))
                for k in range(KE):
                    for s in range(SUB):
                        ins = pe.transpose(ps_rowsT[:, k, s * 128:(s + 1) * 128], rows[:, s, k * 128:(k + 1) * 128], ident[:, :])
                ins.then_inc(rowsT_ready, 1)

            def one_job(e, j, begin=False):
                p = e % 2
                pe.wait_ge(rowsT_split, j + 1)
                for m in range(KD):
                    w = width[m]
                    if begin:
                        pe.wait_ge(first_low, m + 1)
                    pe.wait_ge(inner_split, KD * j + m + 1)
                    for u in range(U):
                        out = ps_up[m % BANKS][0:w, u * JOB:(u + 1) * JOB]
                        for k in range(KE):
                            for c, (wt, xt) in enumerate(((up_hi, rowsT_hi), (up_hi, rowsT_lo), (up_lo, rowsT_hi))):
                                ins = pe.matmul(out, wt[p][:, u, k, m * 128:m * 128 + w], xt[:, k, :],
                                                start=(k == 0 and c == 0), stop=(k == KE - 1 and c == 2))
                    ins.then_inc(up_ready, 1)
                turn_rows(j + 1)
                pe.wait_ge(result_ready, j + 1)
                for m in range(KD):
                    w = width[m]
                    pe.wait_ge(inner_split, KD * j + m + 1 + RING)
                    for s in range(SUB):
                        for c, (xt, wt) in enumerate(((inner_hi, down_hi), (inner_lo, down_hi), (inner_hi, down_lo))):
                            ins = pe.matmul(ps_down[s][:, 0:E], xt[0:w, m, s * 128:(s + 1) * 128], wt[p][0:w, m, :],
                                            start=(m == 0 and c == 0), stop=(m == KD - 1 and c == 2))
                ins.then_inc(down_ready, 1)

            turn_rows(0)
            for e in range(EXPERTS):
                first, end = expert_jobs(pe, e)
                begin = e == 0 and not ahead
                if e > 0:
                    pe.wait_ge(weights_high, KD * (e + 1))
                    pe.wait_ge(up_low, e)
                    pe.wait_ge(down_low, KD * e)
                one_job(e, first, begin)
                with pe.Fori(first + 1, end) as j:
                    one_job(e, j)


HEADS = 32
HD = 64
DIM = HEADS * HD
STATE = 128
LEVELS = 7
TAPS = 4
CONV_TILES = (2 * STATE + DIM) // 128
Z_TILES = DIM // 128
FM_TILES = CONV_TILES + Z_TILES
DTL = HEADS * (1 + LEVELS)
GROUP = 4
GROUPS = HEADS // GROUP
LROWS = 2 * LEVELS * SPT
CHUNK = 16
CHUNKS = [(a, min(a + CHUNK, SEQ)) for a in range(0, SEQ, CHUNK)]
assert 1 + (SEQ - 1).bit_length() == LEVELS and DTL == 256 and SEQ % 2 == 0
RMS_EPS = 1e-5


def split_and_scatter(nc, space, in_dram, w_hi, w_lo, out_dram, norm_dram, w_out, slots, normed_all, slot_rows, hidden, stream):
    with ExitStack() as stack:
        N = FM_TILES * 128 + DTL
        COLS = 512
        CH = N // COLS
        assert CH * COLS == N
        raw = [space.sb(stack, f"sp_raw{p}", [128, KE, COLS]) for p in range(2)]
        norm = space.sb(stack, "sp_norm", [128, Z_TILES])
        raw_out = space.sb(stack, "sp_raw_out", [128, Z_TILES, E])
        loaded = [space.sem(f"sp_loaded{p}") for p in range(2)]
        out_loaded = space.sem("sp_out_loaded")
        high_done = space.sem("sp_high_done")
        low_done = space.sem("sp_low_done")
        scattered = space.sem("sp_scattered")
        stream_stored = space.sem("sp_stream_stored")
        block = stack.enter_context(nc.Block())
        view = in_dram.rearrange("(k p) n -> p k n", p=128)

        @block.gpsimd
        def _(pool):
            scatter_rows(pool, scattered, slots, normed_all, slot_rows)

        @block.sync
        def _(sp):
            sp.dma_start(stream.rearrange("t r e -> r t e"), hidden[:, :, :]).then_inc(stream_stored, 16)
            for c in range(CH):
                if c >= 2:
                    sp.wait_ge(low_done, c - 1)
                sp.dma_start(raw[c % 2][:, :, :], view[:, :, c * COLS:(c + 1) * COLS]).then_inc(loaded[c % 2], 16)
                if c == 1:
                    sp.dma_start(norm[:, :], norm_dram).then_inc(out_loaded, 16)
                    sp.dma_start(raw_out[:, :, :], out_dram.rearrange("(m p) n -> p m n", p=128)).then_inc(out_loaded, 16)
            sp.wait_ge(stream_stored, 16)

        @block.scalar
        def _(act):
            for c in range(CH):
                act.wait_ge(loaded[c % 2], 16 * (c // 2 + 1))
                act.copy(w_hi[:, :, c * COLS:(c + 1) * COLS], raw[c % 2][:, :, :]).then_inc(high_done, 1)
            act.wait_ge(out_loaded, 32)
            for m in range(Z_TILES):
                act.activation(w_out[:, m, :], raw_out[:, m, :], ACT.Copy, scale=norm[:, m:m + 1])

        @block.vector
        def _(v):
            for c in range(CH):
                v.wait_ge(high_done, c + 1)
                part = slice(c * COLS, (c + 1) * COLS)
                v.tensor_tensor(w_lo[:, :, part], raw[c % 2][:, :, :], w_hi[:, :, part].bitcast(F32), ALU.subtract).then_inc(low_done, 1)


def mix_sequences(nc, space, io, stream, expert_rows, slots, shares, w_hi, w_lo, w_out, lam_rows, ident, eps, spare):
    with ExitStack() as stack:
        def sb(what, shape, dt=F32):
            return space.sb(stack, f"mx_{what}", shape, dt)

        def sem(what):
            return space.sem(f"mx_{what}")

        RING = 4
        STEPS = 3

        fm_bias = sb("fm_bias", [128, FM_TILES])
        taps = sb("taps", [128, CONV_TILES, TAPS])
        skip = sb("skip", [128, Z_TILES])
        dtl_bias = sb("dtl_bias", [R, DTL])
        dt_bias = sb("dt_bias", [R, HEADS])
        factor = sb("factor", [R, DTL])
        a_log = sb("a_log", [R, HEADS])
        a_exp = sb("a_exp", [R, HEADS])
        out_bias = sb("out_bias", [R, E])
        later = sb("later", [R, R], F32R)
        upto = sb("upto", [R, SEQ])
        causal = sb("causal", [R, R])
        block_of = sb("block_of", [R, R])
        odd = sb("odd", [R, 2])
        level_of = sb("level_of", [LROWS, SEQ // 2, R], F32R)
        ones = sb("ones", [128, 1])
        one = sb("one", [R, 1])
        table = sb("table", [1, 1])
        index = sb("index", [R, 2, 2], U32)
        gathered = sb("gathered", [R, 2, 2, E])
        raw_in = sb("raw_in", [R, 2, E])
        ahead = sb("ahead", [R, 2, E])
        residual = sb("residual", [R, 2, E])
        stats = sb("stats", [R, 2, 1, 6])
        mv = sb("mv", [R, 2, 2])
        std = sb("std", [R, 2])
        rstd = sb("rstd", [R, 2])
        normed = gathered[:, :, 0, :]
        normedT_hi = sb("normedT_hi", [128, KE, G2], F32R)
        normedT_lo = sb("normedT_lo", [128, KE, G2], F32R)
        soft = sb("soft", [R, 2, DTL])
        decay_in = sb("decay_in", [R, 2, HEADS])
        even_part = decay_in
        dt_now = sb("dt_now", [R, 2, HEADS])
        decay_parts = sb("decay_parts", [R, 2, 2, HEADS], F32R)
        level_parts = sb("level_parts", [R, 2, 2, LEVELS * HEADS], F32R)
        level_rows = sb("level_rows", [LROWS, 2, SEQ * HEADS], F32R)
        first_bias = sb("first_bias", [128, CONV_TILES])
        padded = sb("padded", [128, RING, 2 * SPT, SEQ + TAPS - 1])
        conv = sb("conv", [128, RING, 2 * SPT, SEQ])
        xs = sb("xs", [128, CONV_TILES, G2])
        zs = sb("zs", [128, Z_TILES, G2])
        steps, att_block = space.sb_twice(stack, "mx_steps", [R, STEPS, 2, CHUNK * HEADS], F32R, "mx_att_block", [R, 2, GROUP * 2, R])
        decay = sb("decay", [R, 2, CHUNK * HEADS])
        qk_all = sb("qk_all", [R, 2, R])
        qk = sb("qk", [R, 2, SEQ])
        att = sb("att", [R, HEADS, 2, SEQ])
        vals = sb("vals", [R, 2, 2, GROUP, HD])
        logd, miss = (decay[:, b].rearrange("p (t c) -> p t c", t=2) for b in range(2))
        dtl, grown = (gathered[:, b].rearrange("p c e -> p (c e)").rearrange("p (t c) -> p t c", t=2) for b in range(2))
        shared = sb("shared", [128, 2, CHUNK * HEADS])
        weighed = shared[0:R]
        y = shared[:, :, 0:2 * G2].rearrange("p b (m r) -> p b m r", m=2)
        small = sb("small", [R, 3, 2])
        sumsq, rms, inv_rms = (small[:, c, :] for c in range(3))
        sums_result = sb("sums_result", [128, 2, E])
        squares_sum = sums_result.rearrange("p h e -> p (h e)")[:, 0:2 * G2].rearrange("p (m r) -> p m r", m=2)
        result = sums_result[0:R]

        ps_turned = space.ps(stack, "mx_ps_turned", [128, 512])
        ps_fm = [space.ps(stack, f"mx_ps_fm{b}", [128, 512]) for b in range(2)]
        ps_decay = space.ps(stack, "mx_ps_decay", [128, 512])
        ps_level = space.ps(stack, "mx_ps_level", [128, 512])
        ps_decays = [ps_decay, ps_fm[0]]
        ps_levels = [ps_level, ps_fm[1]]
        ps_chan = ps_fm + [ps_decay, ps_level]
        ps_dtl = space.ps(stack, "mx_ps_dtl", [128, 512])
        ps_out = [space.ps(stack, f"mx_ps_out{h}", [128, 512]) for h in range(2)]
        SS = KE * G2

        consts = sem("consts")
        masks_cast = sem("masks_cast")
        padded_zero = sem("padded_zero")
        ones_ready = sem("ones_ready")
        a_ready = sem("a_ready")
        bias_ready = sem("bias_ready")
        index_ready = sem("index_ready")
        gather_done = [[sem(f"gather_done{h}{c}") for c in range(2)] for h in range(2)]
        stream_in = sem("stream_in")
        ahead_ready = sem("ahead_ready")
        residual_ready = sem("residual_ready")
        moments_ready = sem("moments_ready")
        normed_ready = sem("normed_ready")
        turned_ready = sem("turned_ready")
        normedT_ready = sem("normedT_ready")
        dtl_ready = sem("dtl_ready")
        dtl_read = sem("dtl_read")
        tail_ready = sem("tail_ready")
        grown_ready = sem("grown_ready")
        logd_ready = sem("logd_ready")
        act_step = sem("act_step")
        soft_ready = sem("soft_ready")
        lam_stored = sem("lam_stored")
        levels_loaded = sem("levels_loaded")
        decay_in_ready = sem("decay_in_ready")
        fm_ready = sem("fm_ready")
        fm_read = sem("fm_read")
        conv_done = sem("conv_done")
        xs_ready = sem("xs_ready")
        zs_ready = sem("zs_ready")
        steps_ready = sem("steps_ready")
        decay_ps_ready = sem("decay_ps_ready")
        decay_ready = sem("decay_ready")
        qk_ps_ready = sem("qk_ps_ready")
        qk_ready = sem("qk_ready")
        weighed_ready = sem("weighed_ready")
        level_ps_ready = sem("level_ps_ready")
        att_ready = sem("att_ready")
        xT_ready = sem("xT_ready")
        vals_ready = sem("vals_ready")
        block_ready = sem("block_ready")
        y_ps_ready = sem("y_ps_ready")
        y_read = sem("y_read")
        yz_ready = sem("yz_ready")
        squares_ready = sem("squares_ready")
        squares_added = sem("squares_added")
        conv_step = sem("conv_step")
        first_bias_ready = sem("first_bias_ready")
        dt_copied = sem("dt_copied")
        out_ready = sem("out_ready")
        sumsq_ready = sem("sumsq_ready")
        rms_ready = sem("rms_ready")
        out_read = sem("out_read")
        result_stored = sem("result_stored")
        root_step = sem("root_step")
        vec_step = sem("vec_step")
        NC = len(CHUNKS)
        DC = 2 * NC

        const_loads = [(fm_bias[:, :], io["fm_bias"]), (taps[:, :, :], io["taps"]), (skip[:, :], io["skip"]),
                       (dtl_bias[:, :], io["dtl_bias"].partition_broadcast(R)), (dt_bias[:, :], io["dt_bias"].partition_broadcast(R)),
                       (factor[:, HEADS:DTL], io["factor"].partition_broadcast(R)), (a_log[:, :], io["a_log"].partition_broadcast(R)),
                       (out_bias[:, :], io["out_bias"].partition_broadcast(R)), (upto[:, :], io["upto"]),
                       (causal[:, :], io["causal"]), (block_of[:, :], io["block_of"]), (odd[:, :], io["odd"])]
        const_casts = [(later[:, :], io["later"]), (level_of[:, :, :], io["level_of"])]
        all_consts = 16 * len(const_loads)

        POOL_ADDS = (2, 4, 6)

        def add_squares(eng, i, k):
            eng.wait_ge(squares_ready, GROUPS * i + k + 1)
            if k >= 2:
                eng.wait_ge(squares_added, (GROUPS - 1) * i + k - 1)
            else:
                eng.wait_ge(result_stored, 16 * (i + 1))
            before = y[:, 0] if k == 1 else squares_sum[:, :, :]
            eng.tensor_tensor(squares_sum[:, :, :], y[:, k % 2], before, ALU.add).then_inc(squares_added, 1)

        block = stack.enter_context(nc.Block())

        @block.sync
        def _(sp):

            def front_load(i):
                sp.dma_start(raw_in[:, :, :], stream.rearrange("(i t) r e -> i r t e", t=2)[i]).then_inc(stream_in, 16)

            def store_levels(i):
                sp.wait_ge(soft_ready, i + 1)
                for h in range(2):
                    sp.dma_start(lam_rows[h].rearrange("p l r h -> r (p l) h"), level_parts[:, h].bitcast(F32).rearrange("r p (l h) -> r (p l) h", l=LEVELS)).then_inc(lam_stored, 16)

            def turn(i, last):
                if not last:
                    sp.wait_ge(ahead_ready, 2 * i + 2)
                    front_load(i + 1)
                    store_levels(i + 1)
                sp.wait_ge(out_read, i + 2)
                sp.dma_start(stream.rearrange("(i t) r e -> i r t e", t=2)[i], result[:, :, :]).then_inc(result_stored, 16)

            front_load(0)
            for dst, src in const_loads:
                sp.dma_start(dst, src).then_inc(consts, 16)
            store_levels(0)
            with sp.Fori(0, PAIRS - 1) as i:
                turn(i, False)
            turn(PAIRS - 1, True)
            sp.wait_ge(result_stored, 16 * (PAIRS + 1))

        @block.gpsimd
        def _(pool):
            def front_gather(i):
                for h in range(2):
                    for c in range(2):
                        pool.indirect_dma_start(gathered[:, h, c, :], None, expert_rows,
                                                bass.IndirectOffsetOnAxis(ap=index[:, h, c:c + 1], axis=0)).then_inc(gather_done[h][c], 16)

            def turn(i, last):
                pool.wait_ge(ahead_ready, 2 * i + 2)
                if not last:
                    pool.wait_ge(index_ready, i + 2)
                pool.wait_ge(lam_stored, 32 * i + 32)
                pool.wait_ge(out_read, i + 1)
                pool.tensor_tensor(residual[:, :, :], ahead[:, :, :], out_bias[:, :].unsqueeze(1).broadcast_to([R, 2, E]),
                                   ALU.add).then_inc(residual_ready, 1)
                if not last:
                    front_gather(i + 1)
                for h in range(2):
                    pool.dma_start(level_rows[:, h, :], lam_rows[h].rearrange("p l (b t) h -> (p l b) (t h)", b=SPT)).then_inc(levels_loaded, 16)
                pool.wait_ge(decay_in_ready, i + 1)
                for n in range(DC):
                    h, (a, b) = n // NC, CHUNKS[n % NC]
                    cols = (b - a) * HEADS
                    if n >= STEPS:
                        pool.wait_ge(decay_ready, DC * i + n - STEPS + 3)
                    pool.tensor_tensor(steps[:, n % STEPS, :, 0:cols].rearrange("p c (t h) -> p c t h", h=HEADS),
                                       decay_parts[:, h].bitcast(F32).unsqueeze(2).broadcast_to([R, 2, b - a, HEADS]),
                                       upto[:, a:b].unsqueeze(1).unsqueeze(3).broadcast_to([R, 2, b - a, HEADS]), ALU.mult).then_inc(steps_ready, 1)
                pool.wait_ge(att_ready, DC * (i + 1) + 2)
                for g in range(GROUPS):
                    if g >= 2:
                        pool.wait_ge(y_ps_ready, GROUPS * i + g - 1)
                    pool.tensor_tensor(att_block[:, g % 2].rearrange("p n (b t) -> p n b t", b=SPT),
                                           att[:, g * GROUP:(g + 1) * GROUP].rearrange("p h c t -> p (h c) t").unsqueeze(2).broadcast_to([R, 2 * GROUP, SPT, SEQ]),
                                           block_of[:, :].rearrange("p (b t) -> p b t", b=SPT).unsqueeze(1).broadcast_to([R, 2 * GROUP, SPT, SEQ]),
                                           ALU.mult).then_inc(block_ready, 1)
                    if g - 1 in POOL_ADDS:
                        add_squares(pool, i, g - 1)

            pool.wait_ge(index_ready, 1)
            front_gather(0)
            pool.memset(padded[:, :, :, :], 0.0).then_inc(padded_zero, 1)
            pool.memset(factor[:, 0:HEADS], 1.0).then_inc(ones_ready, 1)
            pool.memset(one[:, :], 1.0).then_inc(ones_ready, 1)
            pool.memset(ones[:, :], 1.0).then_inc(ones_ready, 1)
            for dst, src in const_casts:
                pool.dma_start(dst, src).then_inc(masks_cast, 16)
            pool.wait_ge(consts, all_consts)
            pool.tensor_tensor(dtl_bias[:, 0:HEADS], dtl_bias[:, 0:HEADS], dt_bias[:, :], ALU.add).then_inc(bias_ready, 1)
            pool.tensor_tensor(first_bias[:, :], fm_bias[:, 0:CONV_TILES], taps[:, :, TAPS - 1], ALU.mult).then_inc(first_bias_ready, 1)
            with pool.Fori(0, PAIRS - 1) as i:
                turn(i, False)
            turn(PAIRS - 1, True)

        @block.scalar
        def _(act):
            act.sem_inc(fm_read, 4)
            act.sem_inc(decay_ready, 2)
            def grow(i):
                act.wait_ge(tail_ready, i + 1)
                act.activation(grown[:, :, :], dtl[:, :, :], ACT.Abs).then_inc(act_step, 1)
                act.wait_ge(act_step, i + 1)
                act.activation(grown[:, :, :], grown[:, :, :], ACT.Exp, scale=-1.0).then_inc(grown_ready, 1)

            def log_grown(i):
                act.wait_ge(grown_ready, i + 1)
                act.activation(logd[:, :, :], grown[:, :, :], ACT.Ln, bias=one[:, :]).then_inc(logd_ready, 1)

            def turn(i, last):
                act.activation(table[:, :], one[0:1, :], ACT.Silu)
                for n in range(CONV_TILES + RING):
                    if n >= RING:
                        act.wait_ge(conv_done, CONV_TILES * i + n - RING + 1)
                        act.activation(xs[:, n - RING, :], conv[:, n % RING].rearrange("p s t -> p (s t)"), ACT.Silu).then_inc(xs_ready, 1)
                    if n < CONV_TILES:
                        q = n if n < 2 else 2 * n - 2
                        act.wait_ge(fm_ready, FM_TILES * i + q + 1)
                        src = ps_chan[q % 4][:, 0:G2].rearrange("p (s t) -> p s t", t=SEQ)
                        act.activation(padded[:, n % RING, :, TAPS - 1:], src, ACT.Identity, bias=fm_bias[:, n:n + 1])
                        if n >= RING:
                            act.wait_ge(xs_ready, CONV_TILES * i + n - RING + 1)
                        act.activation(conv[:, n % RING], src, ACT.Identity, bias=first_bias[:, n:n + 1], scale=taps[:, n, TAPS - 1:TAPS]).then_inc(fm_read, 1)
                        if n >= 2:
                            q, m = q + 1, n - 2
                            act.wait_ge(fm_ready, FM_TILES * i + q + 1)
                            act.activation(zs[:, m, :], ps_chan[q % 4][:, 0:G2], ACT.Silu,
                                           bias=fm_bias[:, CONV_TILES + m:CONV_TILES + m + 1]).then_inc(fm_read, 1)
                for n in range(DC):
                    cols = (CHUNKS[n % NC][1] - CHUNKS[n % NC][0]) * HEADS
                    act.wait_ge(decay_ps_ready, DC * i + n + 1)
                    if n >= 2:
                        act.wait_ge(weighed_ready, DC * i + n - 1)
                    act.activation(decay[:, n % 2, 0:cols], ps_decays[n % 2][0:R, 0:cols], ACT.Exp).then_inc(decay_ready, 1)
                if not last:
                    grow(i + 1)
                    log_grown(i + 1)
                for g in range(GROUPS):
                    act.wait_ge(yz_ready, GROUPS * i + g + 1)
                    act.activation(y[:, g % 2], zs[:, 2 * g:2 * g + 2, :], ACT.Square).then_inc(squares_ready, 1)
                act.wait_ge(sumsq_ready, i + 1)
                act.activation(rms[:, :], sumsq[:, :], ACT.Sqrt, bias=eps[:, :], scale=1.0 / DIM).then_inc(rms_ready, 1)

            act.wait_ge(consts, all_consts)
            act.activation(a_exp[:, :], a_log[:, :], ACT.Exp).then_inc(a_ready, 1)
            act.wait_ge(padded_zero, 1)
            act.wait_ge(ones_ready, 3)
            act.wait_ge(first_bias_ready, 1)
            grow(0)
            log_grown(0)
            with act.Fori(0, PAIRS - 1) as i:
                turn(i, False)
            turn(PAIRS - 1, True)

        @block.vector
        def _(v):
            step = Chain(v, vec_step, spare)

            def front(i):
                v.tensor_copy(index[:, :, :], slots[:, :, bass.ds(2 * i, 2)].rearrange("p c h -> p h c")).then_inc(index_ready, 1)

            def front_shares(i, tiles):
                v.wait_ge(stream_in, 16 * i + 16)
                for h in tiles:
                    v.wait_ge(gather_done[h][0], 16 * i + 16)
                    step(v.scalar_tensor_tensor(ahead[:, h, :], gathered[:, h, 0, :], shares[:, 0, bass.ds(2 * i + h, 1)],
                                                raw_in[:, h, :], ALU.mult, ALU.add))
                    v.wait_ge(gather_done[h][1], 16 * i + 16)
                    v.scalar_tensor_tensor(ahead[:, h, :], gathered[:, h, 1, :], shares[:, 1, bass.ds(2 * i + h, 1)],
                                           ahead[:, h, :], ALU.mult, ALU.add).then_inc(ahead_ready, 1)
                    v.wait_ge(ahead_ready, 2 * i + h + 1)
                    moments(v, step, ahead[:, h, :], stats[:, h], mv[:, h, :]).then_inc(moments_ready, 1)

            def front_root(i):
                return inverse_root(v, root_step, ROOT_STEPS * i, rstd[:, :], sumsq[:, :], std[:, :], mv[:, :, 1])

            def front_normed(i):
                v.wait_ge(root_step, ROOT_STEPS * (i + 1))
                for h in range(2):
                    normalize(v, normed[:, h, :], ahead[:, h, :], mv[:, h, :], rstd[:, h:h + 1]).then_inc(normed_ready, 1)

            def front_turned(i):
                v.wait_ge(turned_ready, i + 1)
                src = ps_turned[:, 0:SS].rearrange("p (k r) -> p k r", k=KE)
                step(v.tensor_copy(normedT_hi[:, :, :], src))
                v.tensor_tensor(normedT_lo[:, :, :], src, normedT_hi[:, :, :].bitcast(F32), ALU.subtract).then_inc(normedT_ready, 1)

            def dtl_begin(i):
                v.wait_ge(dtl_ready, i + 1)
                v.tensor_tensor(miss[:, :, :], ps_dtl[0:R, :].rearrange("p (h c) -> p h c", h=2),
                                dtl_bias[:, :].unsqueeze(1).broadcast_to([R, 2, DTL]), ALU.add).then_inc(dtl_read, 1)
                v.wait_ge(dtl_read, i + 1)
                v.tensor_tensor(dtl[:, :, :], miss[:, :, :], factor[:, :].unsqueeze(1).broadcast_to([R, 2, DTL]), ALU.mult).then_inc(tail_ready, 1)

            def dtl_grown(i):
                v.wait_ge(grown_ready, i + 1)
                step(v.tensor_scalar(soft[:, :, :], grown[:, :, :], 1.0, None, ALU.add))
                step(v.scalar_tensor_tensor(miss[:, :, :], soft[:, :, :], -1.0, grown[:, :, :], ALU.add, ALU.subtract))

            def dtl_soft(i):
                v.wait_ge(logd_ready, i + 1)
                step(v.tensor_tensor(miss[:, :, :], logd[:, :, :], miss[:, :, :], ALU.subtract))
                step(v.scalar_tensor_tensor(soft[:, :, :], dtl[:, :, :], 0.0, miss[:, :, :], ALU.max, ALU.add))

            def dtl_levels(i):
                v.wait_ge(decay_in_ready, i + 1)
                step(v.tensor_scalar(even_part[:, :, :], soft[:, :, 2 * HEADS:3 * HEADS], odd[:, 1:2], None, ALU.mult))
                step(v.scalar_tensor_tensor(soft[:, :, HEADS:2 * HEADS], soft[:, :, HEADS:2 * HEADS], odd[:, 0:1], even_part[:, :, :],
                                            ALU.mult, ALU.add))
                step(v.tensor_copy(level_parts[:, :, 0, :], soft[:, :, HEADS:DTL]))
                v.tensor_tensor(level_parts[:, :, 1, :], soft[:, :, HEADS:DTL], level_parts[:, :, 0, :].bitcast(F32), ALU.subtract).then_inc(soft_ready, 1)

            def dtl_decay(i):
                step(v.scalar_tensor_tensor(decay_in[:, :, :], soft[:, :, 0:HEADS], -1.0, a_exp[:, :].unsqueeze(1).broadcast_to([R, 2, HEADS]),
                                            ALU.mult, ALU.mult))
                step(v.tensor_copy(decay_parts[:, :, 0, :], decay_in[:, :, :]))
                v.tensor_tensor(decay_parts[:, :, 1, :], decay_in[:, :, :], decay_parts[:, :, 0, :].bitcast(F32), ALU.subtract).then_inc(decay_in_ready, 1)

            per_turn = 1 + (2 * 2 + 1) + (2 + 2 + 3 + 2) + 1

            SHARES_AFTER = 8

            def turn(i, last):
                v.tensor_copy(dt_now[:, :, :], soft[:, :, 0:HEADS]).then_inc(dt_copied, 1)
                if not last:
                    front(i + 1)

                def taps_of(n, c):
                    if c == 0:
                        v.wait_ge(fm_read, FM_TILES * i + (n if n < 2 else 2 * n - 2) + 1 + 4)
                    else:
                        v.wait_ge(conv_step, 2 * CONV_TILES * i + 4 * (n // 2) + 2 * (c - 1) + n % 2 + 1)
                    dst = conv[:, n % RING]
                    v.scalar_tensor_tensor(dst, padded[:, n % RING, :, c:c + SEQ], taps[:, n, c:c + 1], dst,
                                           ALU.mult, ALU.add).then_inc(conv_step if c < TAPS - 2 else conv_done, 1)

                root = iter(())
                for n in range(0, CONV_TILES, 2):
                    for c in range(TAPS - 1):
                        taps_of(n, c)
                        next(root, None)
                        taps_of(n + 1, c)
                        next(root, None)
                    if n in (SHARES_AFTER - 2, SHARES_AFTER) and not last:
                        v.wait_ge(residual_ready, i + 1)
                        front_shares(i + 1, [int(n == SHARES_AFTER)])
                    if n == SHARES_AFTER and not last:
                        v.wait_ge(moments_ready, 2 * i + 4)
                        root = front_root(i + 1)
                    if n == SHARES_AFTER + 6 and not last:
                        assert next(root, True)
                        front_normed(i + 1)
                if not last:
                    front_turned(i + 1)
                v.wait_ge(qk_ps_ready, i + 1)
                for h in range(2):
                    ins = v.tensor_tensor(qk_all[:, h, :], ps_out[h][0:R, E:E + R], causal[:, :], ALU.mult)
                step(ins)
                for h in range(2):
                    ins = v.tensor_reduce(qk[:, h, :], qk_all[:, h, :].rearrange("p (b t) -> p t b", b=SPT), AX.X, ALU.add)
                ins.then_inc(qk_ready, 1)
                def weigh(n):
                    h, (a, b) = n // NC, CHUNKS[n % NC]
                    cols = (b - a) * HEADS
                    v.wait_ge(decay_ready, DC * i + n + 3)
                    if n >= 2:
                        v.wait_ge(att_ready, DC * i + n + 1)
                    v.tensor_tensor(weighed[:, n % 2, 0:cols].rearrange("p (t h) -> p t h", h=HEADS),
                                    decay[:, n % 2, 0:cols].rearrange("p (t h) -> p t h", h=HEADS),
                                    qk[:, h, a:b].unsqueeze(2).broadcast_to([R, b - a, HEADS]), ALU.mult).then_inc(weighed_ready, 1)

                v.wait_ge(qk_ready, i + 1)
                weigh(0)
                for n in range(DC):
                    h, (a, b) = n // NC, CHUNKS[n % NC]
                    cols = (b - a) * HEADS
                    if n + 1 < DC:
                        weigh(n + 1)
                    v.wait_ge(weighed_ready, DC * i + n + 1)
                    v.wait_ge(level_ps_ready, DC * i + n + 1)
                    v.tensor_tensor(att[:, :, h, a:b].rearrange("p h t -> p t h"),
                                    weighed[:, n % 2, 0:cols].rearrange("p (t h) -> p t h", h=HEADS),
                                    ps_levels[n % 2][0:R, 0:cols].rearrange("p (t h) -> p t h", h=HEADS), ALU.mult).then_inc(att_ready, 1)
                if not last:
                    dtl_begin(i + 1)
                v.wait_ge(dt_copied, i + 1)

                for g in range(GROUPS + 1):
                    if g < GROUPS:
                        if g >= 2:
                            v.wait_ge(y_ps_ready, GROUPS * i + g - 1)
                        v.wait_ge(xT_ready, GROUPS * i + g + 1)
                        v.tensor_tensor(vals[:, g % 2], [ps_decay, ps_level][g % 2][0:R, :].rearrange("p (c h d) -> p c h d", c=2, h=GROUP),
                                        dt_now[:, :, g * GROUP:(g + 1) * GROUP].unsqueeze(3).broadcast_to([R, 2, GROUP, HD]),
                                        ALU.mult).then_inc(vals_ready, 1)
                    if g >= 1:
                        k = g - 1
                        v.wait_ge(y_ps_ready, GROUPS * i + k + 1)
                        if k >= 2 and k - 1 not in POOL_ADDS:
                            add_squares(v, i, k - 1)
                        if k >= 3:
                            v.wait_ge(squares_added, (GROUPS - 1) * i + k - 2)
                        elif k == 2:
                            v.wait_ge(squares_added, (GROUPS - 1) * i + 1)
                        for m in range(2):
                            ins = v.scalar_tensor_tensor(y[:, k % 2, m, :], xs[:, 2 + 2 * k + m, :], skip[:, 2 * k + m:2 * k + m + 1],
                                                         ps_fm[k % 2][:, m * G2:(m + 1) * G2], ALU.mult, ALU.add)
                        ins.then_inc(y_read, 1)
                        v.wait_ge(y_read, GROUPS * i + k + 2)
                        v.tensor_tensor(zs[:, 2 * k:2 * k + 2, :], zs[:, 2 * k:2 * k + 2, :], y[:, k % 2], ALU.mult).then_inc(yz_ready, 1)
                    if not last:
                        if g == 2:
                            dtl_grown(i + 1)
                        if g == 3:
                            dtl_soft(i + 1)
                        if g == 4:
                            dtl_decay(i + 1)
                        if g == 5:
                            dtl_levels(i + 1)
                add_squares(v, i, GROUPS - 1)
                v.wait_ge(residual_ready, i + 1)
                v.wait_ge(out_ready, i + 1)
                v.tensor_reduce(sumsq[:, :], ps_turned[0:R, SS:SS + 4].rearrange("p (h m) -> p h m", h=2), AX.X, ALU.add).then_inc(sumsq_ready, 1)
                v.wait_ge(rms_ready, i + 1)
                step(v.reciprocal(inv_rms[:, :], rms[:, :]))
                for h in range(2):
                    ins = v.scalar_tensor_tensor(result[:, h, :], ps_out[h][0:R, 0:E], inv_rms[:, h:h + 1], residual[:, h, :], ALU.mult, ALU.add)
                ins.then_inc(out_read, 1)

            v.sem_inc(att_ready, 2)
            v.sem_inc(y_read, 1)
            v.sem_inc(out_read, 1)
            v.sem_inc(result_stored, 16)
            front(0)
            front_shares(0, range(2))
            v.wait_ge(moments_ready, 2)
            for _ in front_root(0):
                pass
            front_normed(0)
            front_turned(0)
            v.wait_ge(consts, all_consts)
            v.wait_ge(ones_ready, 3)
            v.wait_ge(bias_ready, 1)
            v.wait_ge(a_ready, 1)
            dtl_begin(0)
            dtl_grown(0)
            dtl_soft(0)
            dtl_decay(0)
            dtl_levels(0)
            with v.Fori(0, PAIRS - 1) as i:
                step.enter(i, per_turn)
                turn(i, False)
                step.leave(PAIRS - 1, per_turn)
            turn(PAIRS - 1, True)

        @block.tensor
        def _(pe):
            three = lambda hi_a, lo_a, hi_b, lo_b: ((hi_a, hi_b), (hi_a, lo_b), (lo_a, hi_b))

            def front(i):
                pe.wait_ge(normed_ready, 2 * i + 2)
                for k in range(KE):
                    for h in range(2):
                        ins = pe.transpose(ps_turned[:, k * G2 + h * R:k * G2 + (h + 1) * R], normed[:, h, k * 128:(k + 1) * 128], ident[0:R, 0:R])
                ins.then_inc(turned_ready, 1)

            def project(i, q, tile):
                pe.wait_ge(fm_read, FM_TILES * i + q + 1)
                out = ps_chan[q % 4][:, 0:G2]
                for k in range(KE):
                    for c, (w, x) in enumerate(three(w_hi, w_lo, normedT_hi, normedT_lo)):
                        ins = pe.matmul(out, w[:, k, tile * 128:(tile + 1) * 128], x[:, k, :], start=(k == 0 and c == 0), stop=(k == KE - 1 and c == 2))
                ins.then_inc(fm_ready, 1)

            def turn_x(i, g):
                if g == 0:
                    pe.wait_ge(decay_ready, DC * (i + 1) + 2)
                    pe.wait_ge(xs_ready, CONV_TILES * (i + 1))
                if g == 1:
                    pe.wait_ge(att_ready, DC * (i + 1) + 2)
                if g >= 2:
                    pe.wait_ge(vals_ready, GROUPS * i + g - 1)
                out = (ps_decay, ps_level)[g % 2]
                for h in range(2):
                    for m in range(2):
                        ins = pe.transpose(out[0:R, h * 256 + m * 128:h * 256 + (m + 1) * 128], xs[:, 2 + 2 * g + m, h * R:(h + 1) * R], ident[:, :])
                ins.then_inc(xT_ready, 1)

            def heads(i, g):
                pe.wait_ge(vals_ready, GROUPS * i + g + 1)
                pe.wait_ge(block_ready, GROUPS * i + g + 1)
                if g >= 2:
                    pe.wait_ge(y_read, GROUPS * i + g)
                for n in range(GROUP):
                    m, low = divmod(n, 2)
                    for h in range(2):
                        ins = pe.matmul(ps_fm[g % 2][low * HD:(low + 1) * HD, m * G2 + h * R:m * G2 + (h + 1) * R],
                                        vals[:, g % 2, h, n, :], att_block[:, g % 2, 2 * n + h, :], start=True, stop=True)
                ins.then_inc(y_ps_ready, 1)

            def project_out(i, g):
                pe.wait_ge(yz_ready, GROUPS * i + g + 1)
                for m in range(2 * g, 2 * g + 2):
                    for h in range(2):
                        ins = pe.matmul(ps_out[h][0:R, 0:E], zs[:, m, h * R:(h + 1) * R], w_out[:, m, :], start=(m == 0), stop=(m == Z_TILES - 1))
                if g == GROUPS - 1:
                    pe.wait_ge(squares_added, (GROUPS - 1) * (i + 1))
                    for h in range(2):
                        for m in range(2):
                            ins = pe.matmul(ps_turned[0:R, SS + 2 * h + m:SS + 2 * h + m + 1], squares_sum[:, m, h * R:(h + 1) * R],
                                            ones[:, :], start=True, stop=True)
                    ins.then_inc(out_ready, 1)

            def project_dtl(i):
                pe.wait_ge(normedT_ready, i + 1)
                for h in range(2):
                    for k in range(KE):
                        for c, (x, w) in enumerate(three(normedT_hi, normedT_lo, w_hi, w_lo)):
                            ins = pe.matmul(ps_dtl[0:R, h * DTL:(h + 1) * DTL], x[:, k, h * R:(h + 1) * R], w[:, k, FM_TILES * 128:FM_TILES * 128 + DTL],
                                            start=(k == 0 and c == 0), stop=(k == KE - 1 and c == 2))
                ins.then_inc(dtl_ready, 1)

            def turn(i, last):
                pe.wait_ge(y_read, GROUPS * i + 1)
                project(i, 0, 0)
                project(i, 1, 1)
                for m in range(Z_TILES):
                    project(i, 2 + 2 * m, 2 + m)
                    project(i, 3 + 2 * m, CONV_TILES + m)
                if not last:
                    front(i + 1)
                pe.wait_ge(xs_ready, CONV_TILES * i + 2)
                pe.wait_ge(out_read, i + 1)
                for h in range(2):
                    ins = pe.matmul(ps_out[h][0:R, E:E + R], xs[:, 0, h * R:(h + 1) * R], xs[:, 1, h * R:(h + 1) * R], start=True, stop=True)
                ins.then_inc(qk_ps_ready, 1)
                pe.wait_ge(fm_read, FM_TILES * (i + 1) + 4)
                pe.wait_ge(levels_loaded, 32 * i + 32)
                for n in range(DC):
                    h, (a, b) = n // NC, CHUNKS[n % NC]
                    cols = (b - a) * HEADS
                    pe.wait_ge(steps_ready, DC * i + n + 1)
                    pe.wait_ge(decay_ready, DC * i + n + 1)
                    for c in range(2):
                        ins = pe.matmul(ps_decays[n % 2][0:R, 0:cols], later[:, :], steps[:, n % STEPS, c, 0:cols], start=(c == 0), stop=(c == 1))
                    ins.then_inc(decay_ps_ready, 1)
                    pe.wait_ge(att_ready, DC * i + n + 1)
                    for m in range(a // 2, b // 2):
                        ins = pe.matmul(ps_levels[n % 2][0:R, (2 * m - a) * HEADS:(2 * m - a + 2) * HEADS], level_of[:, m, :],
                                        level_rows[:, h, 2 * m * HEADS:(2 * m + 2) * HEADS], start=True, stop=True)
                    ins.then_inc(level_ps_ready, 1)
                    if n == 1 and not last:
                        project_dtl(i + 1)
                for g in range(GROUPS + 2):
                    if g < GROUPS:
                        turn_x(i, g)
                    if 1 <= g <= GROUPS:
                        heads(i, g - 1)
                    if g >= 2:
                        project_out(i, g - 2)

            front(0)
            project_dtl(0)
            pe.wait_ge(masks_cast, 16 * len(const_casts))
            pe.wait_ge(ones_ready, 3)
            with pe.Fori(0, PAIRS - 1) as i:
                turn(i, False)
            turn(PAIRS - 1, True)


INNER_SHARED = 704
KD_SHARED = -(-INNER_SHARED // 128)
EARLY = 4


def scatter_rows(pool, scattered, slots, normed_all, slot_rows):
    for c in range(2):
        for t in range(NT):
            pool.indirect_dma_start(slot_rows, bass.IndirectOffsetOnAxis(ap=slots[:, c, t:t + 1], axis=0),
                                    normed_all[:, t, :], None).then_inc(scattered, 16)
    pool.wait_ge(scattered, 16 * 2 * NT)


class SharedWeights:

    def __init__(self, space, stack):
        self.up_raw = space.sb(stack, "sw_up_raw", [128, 2, KE, INNER_SHARED])
        self.down_raw = space.sb(stack, "sw_down_raw", [128, KD_SHARED, E])
        self.up_hi = space.sb(stack, "sw_up_hi", [128, 2, KE, INNER_SHARED], F32R)
        self.up_lo = space.sb(stack, "sw_up_lo", [128, 2, KE, INNER_SHARED], F32R)
        self.down_hi = space.sb(stack, "sw_down_hi", [128, KD_SHARED, E], F32R)
        self.down_lo = space.sb(stack, "sw_down_lo", [128, KD_SHARED, E], F32R)

    def load(self, eng, sem, gate_dram, up_dram, down_dram):
        return load_rows(eng, sem, self.up_raw[:, 0], gate_dram) + load_rows(eng, sem, self.up_raw[:, 1], up_dram) + load_rows(eng, sem, self.down_raw, down_dram)

    def split_high(self, act, part, parts):
        a, b = INNER_SHARED * part // parts, INNER_SHARED * (part + 1) // parts
        ins = act.copy(self.up_hi[:, :, :, a:b], self.up_raw[:, :, :, a:b])
        for k in range(KD_SHARED * part // parts, KD_SHARED * (part + 1) // parts):
            w = min(128, INNER_SHARED - k * 128)
            ins = act.copy(self.down_hi[0:w, k, :], self.down_raw[0:w, k, :])
        return ins

    def split_low(self, eng):
        eng.tensor_tensor(self.up_lo[:, :, :, :].rearrange("p u k n -> p (u k n)"), self.up_raw[:, :, :, :].rearrange("p u k n -> p (u k n)"),
                          self.up_hi[:, :, :, :].bitcast(F32).rearrange("p u k n -> p (u k n)"), ALU.subtract)
        for k in range(KD_SHARED):
            w = min(128, INNER_SHARED - k * 128)
            ins = eng.tensor_tensor(self.down_lo[0:w, k, :], self.down_raw[0:w, k, :], self.down_hi[0:w, k, :].bitcast(F32), ALU.subtract)
        return ins


def share_experts(nc, space, name, finish, weights, expert_weights, hidden, normed_all, slot_rows, expert_rows, slots, shares, out, ident):
    KD = KD_SHARED
    width = [min(128, INNER_SHARED - m * 128) for m in range(KD)]
    start = EARLY if finish else 0
    turns = PAIRS - EARLY if finish else EARLY
    up_hi, up_lo, down_hi, down_lo = weights.up_hi, weights.up_lo, weights.down_hi, weights.down_lo
    assert PAIRS - EARLY > EARLY
    with ExitStack() as stack:
        def sb(what, shape, dt=F32):
            return space.sb(stack, f"{name}_{what}", shape, dt)

        def sem(what):
            return space.sem(f"{name}_{what}")

        normed = sb("normed", [R, 2, E])
        normedT_hi = sb("normedT_hi", [128, KE, G2], F32R)
        normedT_lo = sb("normedT_lo", [128, KE, G2], F32R)
        silu = sb("silu", [128, KD, G2])
        inner_f = sb("inner_f", [128, KD, G2])
        inner_hi = sb("inner_hi", [128, KD, G2], F32R)
        inner_lo = sb("inner_lo", [128, KD, G2], F32R)
        index = [sb(f"index{z}", [R, 2, 2], U32) for z in range(2)]
        gathered = [sb(f"gathered{z}", [R, 2, 2, E]) for z in range(2)]
        sums = [sb(f"sums{z}", [R, 2, 2, E]) for z in range(2)]
        result = [sb(f"result{z}", [R, 2, E]) for z in range(2)]
        mark = sb("mark", [1, 3])
        ps_turned = space.ps(stack, f"{name}_ps_turned", [128, 512])
        RING = 3
        ps_up = [space.ps(stack, f"{name}_ps_up{b}", [128, 512]) for b in range(RING)]
        ps_down = [space.ps(stack, f"{name}_ps_down{h}", [128, 512]) for h in range(2)]

        scattered = sem("scattered")
        high_done = sem("high_done")
        normed_ready = sem("normed_ready")
        turned_ready = sem("turned_ready")
        normedT_ready = sem("normedT_ready")
        up_ready = sem("up_ready")
        silu_done = sem("silu_done")
        inner_done = sem("inner_done")
        inner_split = sem("inner_split")
        down_ready = sem("down_ready")
        down_read = sem("down_read")
        index_ready = [sem(f"index_ready{z}") for z in range(2)]
        gather_done = [[[sem(f"gather_done{z}{h}{c}") for c in range(2)] for h in range(2)] for z in range(2)]
        early_ready = sem("early_ready")
        stored = [sem(f"stored{z}") for z in range(2)]
        marked = [sem(f"marked{z}") for z in range(2)]
        vec_step = sem("vec_step")

        block = stack.enter_context(nc.Block())

        @block.sync
        def _(sp):
            if not finish:
                return
            late_rows, early_rows = (out[a * G2:b * G2].rearrange("(i t r) e -> i r t e", r=R, t=2)
                                     for a, b in ((start, PAIRS - 1), (0, EARLY)))

            for i in range(turns - 1):
                sp.wait_ge(down_read, 2 * i + 3)
                sp.dma_start(late_rows[i], result[0][:, :, :]).then_inc(stored[0], 16)
                if i < EARLY:
                    sp.wait_ge(early_ready, i + 1)
                    sp.dma_start(early_rows[i], result[1][:, :, :]).then_inc(stored[1], 16)
            done, end = (NT - 2) * R, BATCH * SEQ
            sp.wait_ge(down_read, 2 * turns + 1)
            sp.dma_start(out[done:done + R], result[0][:, 0, :]).then_inc(stored[0], 16)
            sp.dma_start(out[done + R:end], result[0][0:end - done - R, 1, :]).then_inc(stored[0], 16)
            sp.wait_ge(stored[0], 16 * (turns + 2))
            sp.wait_ge(stored[1], 16 * (EARLY + 1))

        @block.gpsimd
        def _(pool):
            if not finish:
                scatter_rows(pool, scattered, slots, normed_all, slot_rows)
                return

            def gather(i, z):
                pool.wait_ge(index_ready[z], i + 1)
                pool.tensor_tensor(mark[:, z + 1:z + 2], mark[:, 0:1], mark[:, 0:1], ALU.add).then_inc(marked[z], 1)
                for h in range(2):
                    for c in range(2):
                        pool.indirect_dma_start(gathered[z][:, h, c, :], None, expert_rows,
                                                bass.IndirectOffsetOnAxis(ap=index[z][:, h, c:c + 1], axis=0)).then_inc(gather_done[z][h][c], 16)

            pool.memset(mark[:, 0:1], 0.0).then_inc(marked[0], 1)
            pool.wait_ge(marked[0], 1)
            pool.sem_inc(marked[1], 1)
            with pool.Fori(0, EARLY) as i:
                gather(i, 0)
                gather(i, 1)
            for i in range(EARLY, turns):
                gather(i, 0)

        @block.scalar
        def _(act):
            if not finish:
                expert_weights.split_high(act, 0).then_inc(high_done, 1)
            with act.Fori(0, turns) as i:
                for m in range(KD):
                    act.wait_ge(up_ready, KD * i + m + 1)
                    act.activation(silu[0:width[m], m, :], ps_up[m % RING][0:width[m], 0:G2], ACT.Silu).then_inc(silu_done, 1)

        @block.vector
        def _(v):
            step = Chain(v, vec_step)

            def front(i):
                v.tensor_copy(normed[:, :, :], normed_all[:, bass.ds(2 * (i + start), 2), :]).then_inc(normed_ready, 1)

            def turn_rows(i):
                v.wait_ge(turned_ready, i + 1)
                src = ps_turned[:, 0:KE * G2].rearrange("p (k r) -> p k r", k=KE)
                step(v.tensor_copy(normedT_hi[:, :, :], src))
                v.tensor_tensor(normedT_lo[:, :, :], src, normedT_hi[:, :, :].bitcast(F32), ALU.subtract).then_inc(normedT_ready, 1)

            def ask(i, z, first):
                v.wait_ge(marked[z], i + 1)
                v.tensor_copy(index[z][:, :, :], slots[:, :, bass.ds(2 * (i + first), 2)].rearrange("p c h -> p h c")).then_inc(index_ready[z], 1)

            def add_shares(i, z, first, last_out):
                for c in range(2):
                    for h in range(2):
                        v.wait_ge(gather_done[z][h][c], 16 * i + 16)
                        before = hidden[:, 2 * (i + first) + h, :] if c == 0 else sums[z][:, 0, h, :]
                        after = last_out[:, h, :] if c == 1 and last_out is not None else sums[z][:, c, h, :]
                        ins = v.scalar_tensor_tensor(after, gathered[z][:, h, c, :], shares[:, c, bass.ds(2 * (i + first) + h, 1)], before, ALU.mult, ALU.add)
                    if c == 0 or last_out is None:
                        step(ins)
                return ins

            def turn(i, early, last):
                if finish:
                    ask(i, 0, start)
                    if early:
                        ask(i, 1, 0)
                if not last:
                    front(i + 1)
                for m in range(KD):
                    w = width[m]
                    v.wait_ge(silu_done, KD * i + m + 1)
                    v.tensor_tensor(inner_f[0:w, m, :], silu[0:w, m, :], ps_up[m % RING][0:w, G2:2 * G2], ALU.mult).then_inc(inner_done, 1)
                    v.wait_ge(inner_done, KD * i + m + 1 + RING)
                    step(v.tensor_copy(inner_hi[0:w, m, :], inner_f[0:w, m, :]))
                    v.tensor_tensor(inner_lo[0:w, m, :], inner_f[0:w, m, :], inner_hi[0:w, m, :].bitcast(F32), ALU.subtract).then_inc(inner_split, 1)
                if not last:
                    turn_rows(i + 1)
                if finish:
                    add_shares(i, 0, start, None)
                    v.wait_ge(stored[0], 16 * i + 16)
                v.wait_ge(down_ready, i + 1)
                for h in range(2):
                    if finish:
                        v.tensor_tensor(result[0][:, h, :], ps_down[h][0:R, 0:E], sums[0][:, 1, h, :], ALU.add).then_inc(down_read, 1)
                    else:
                        rows = hidden[:, 2 * (i + start) + h, :]
                        v.tensor_tensor(rows, ps_down[h][0:R, 0:E], rows, ALU.add).then_inc(down_read, 1)
                if early:
                    v.wait_ge(stored[1], 16 * i + 16)
                    add_shares(i, 1, 0, result[1]).then_inc(early_ready, 1)

            v.sem_inc(inner_done, RING)
            v.sem_inc(down_read, 1)
            for z in range(2):
                v.sem_inc(stored[z], 16)
            front(0)
            turn_rows(0)
            if not finish:
                v.wait_ge(high_done, 1)
                expert_weights.split_low(v, 0)
            if finish:
                per_turn = KD + 1 + 2 + 1
                with v.Fori(0, EARLY) as i:
                    step.enter(i, per_turn)
                    turn(i, True, False)
                    step.leave(EARLY, per_turn)
                for i in range(EARLY, turns):
                    turn(i, False, i == turns - 1)
            else:
                per_turn = KD + 1
                with v.Fori(0, turns - 1) as i:
                    step.enter(i, per_turn)
                    turn(i, False, False)
                    step.leave(turns - 1, per_turn)
                turn(turns - 1, False, True)

        @block.tensor
        def _(pe):
            def front(i):
                pe.wait_ge(normed_ready, i + 1)
                for k in range(KE):
                    for h in range(2):
                        ins = pe.transpose(ps_turned[:, k * G2 + h * R:k * G2 + (h + 1) * R], normed[:, h, k * 128:(k + 1) * 128], ident[0:R, 0:R])
                ins.then_inc(turned_ready, 1)

            def turn(i, last):
                pe.wait_ge(normedT_ready, i + 1)
                for m in range(KD):
                    w = width[m]
                    pe.wait_ge(inner_done, KD * i + m + 1)
                    for u in range(2):
                        for k in range(KE):
                            for c, (wt, xt) in enumerate(((up_hi, normedT_hi), (up_hi, normedT_lo), (up_lo, normedT_hi))):
                                ins = pe.matmul(ps_up[m % RING][0:w, u * G2:(u + 1) * G2], wt[:, u, k, m * 128:m * 128 + w], xt[:, k, :],
                                                start=(k == 0 and c == 0), stop=(k == KE - 1 and c == 2))
                    ins.then_inc(up_ready, 1)
                if not last:
                    front(i + 1)
                pe.wait_ge(down_read, 2 * i + 1)
                for m in range(KD):
                    w = width[m]
                    pe.wait_ge(inner_split, KD * i + m + 1)
                    for h in range(2):
                        for c, (xt, wt) in enumerate(((inner_hi, down_hi), (inner_lo, down_hi), (inner_hi, down_lo))):
                            ins = pe.matmul(ps_down[h][0:R, 0:E], xt[0:w, m, h * R:(h + 1) * R], wt[0:w, m, :],
                                            start=(m == 0 and c == 0), stop=(m == KD - 1 and c == 2))
                ins.then_inc(down_ready, 1)

            front(0)
            with pe.Fori(0, turns - 1) as i:
                turn(i, False)
            turn(turns - 1, True)


def tower(nc, io, out, upto=9):
    with ExitStack() as outer:
        space = Space(nc)
        ident = space.sb(outer, "ident", [128, 128])
        ones_row = space.sb(outer, "ones_row", [1, 128])
        eps = space.sb(outer, "eps", [R, 1])
        spare = space.sb(outer, "spare", [1, 1])
        slots = space.sb(outer, "slots", [R, 2, NT], U32)
        shares = space.sb(outer, "shares", [R, 2, NT])
        jobs = space.sb(outer, "jobs", [1, EXPERTS + 1], I32)
        slot_rows = nc.dram_tensor("slot_rows", (SLOTS, E), F32, kind="Internal").ap()
        expert_rows = nc.dram_tensor("expert_rows", (SLOTS, E), F32, kind="Internal").ap()
        stream = nc.dram_tensor("stream", (NT, R, E), F32, kind="Internal").ap()
        lam_rows = nc.dram_tensor("lam_rows", (2, 2, LEVELS, R, HEADS), F32, kind="Internal").ap()

        with ExitStack() as mixer:
            w_hi = space.sb(mixer, "w_hi", [128, KE, FM_TILES * 128 + DTL], F32R)
            w_lo = space.sb(mixer, "w_lo", [128, KE, FM_TILES * 128 + DTL], F32R)
            w_out = space.sb(mixer, "w_out", [128, Z_TILES, E])
            with space.part(), ExitStack() as first:
                hidden = space.sb(first, "hidden0", [R, NT, E])
                tokenize(nc, space, io, hidden, [slot_rows, expert_rows], ident, ones_row, eps, spare)
                attend(nc, space, io, hidden, ident, eps, spare)
                normed_all = space.sb(first, "normed_all0", [R, NT, E])
                route(nc, space, "r0", io["gate0"], False, hidden, normed_all, slots, shares, jobs, None, ident, eps, spare)
                split_and_scatter(nc, space, io["in_proj"], w_hi, w_lo, io["out_proj"], io["norm_w"], w_out, slots, normed_all, slot_rows, hidden, stream)
            with space.part():
                run_experts(nc, space, "x0", [io["w_in"]], io["b_in"], io["w_out"], io["b_out"], 1024, jobs, slot_rows, expert_rows, ident)
            with space.part():
                mix_sequences(nc, space, io, stream, expert_rows, slots, shares, w_hi, w_lo, w_out, lam_rows, ident, eps, spare)
        with ExitStack() as last:
            hidden = space.sb(last, "hidden1", [R, NT, E])
            normed_all = space.sb(last, "normed_all1", [R, NT, E])
            shared = SharedWeights(space, last)
            expert = ExpertWeights(space, last, "x1", 2, 352)
            rest = (shared, expert, hidden, normed_all, slot_rows, expert_rows, slots, shares, out, ident)
            with space.part():
                route(nc, space, "r1", io["gate1"], True, hidden, normed_all, slots, shares, jobs, stream, ident, eps, spare,
                      shared, (io["swg"], io["swu"], io["swd"]), expert, ([io["wg"], io["wu"]], io["wd"]))
                share_experts(nc, space, "s0", False, *rest)
            with space.part():
                run_experts(nc, space, "x1", [io["wg"], io["wu"]], None, io["wd"], None, 352, jobs, slot_rows, expert_rows, ident, expert)
                share_experts(nc, space, "s1", True, *rest)


def lay_out(a):
    import numpy as np

    x = np.asarray(a["x"])
    side, size = 6, 16
    patches = x.reshape(BATCH, 3, side, size, side, size).transpose(0, 2, 4, 3, 5, 1).reshape(BATCH, PATCHES, PD)
    tokens = np.zeros((NT * SPT, SEQ, PD), x.dtype)
    tokens[:BATCH, 2:] = patches
    w = {k: np.asarray(v) for k, v in a.items() if k != "x"}

    chan = np.arange(4 * DIM)
    z, xc, bc = chan[0:DIM], chan[DIM:2 * DIM], chan[2 * DIM:2 * DIM + 2 * STATE]
    dt = 2 * DIM + 2 * STATE + np.arange(HEADS)
    all_levels = 15
    level_chan = (2 * DIM + 2 * STATE + HEADS + all_levels * np.arange(HEADS)[None, :]
                  + np.array([1, 0] + list(range(2, LEVELS)))[:, None]).reshape(-1)
    order = np.concatenate([bc, xc, z, dt, level_chan])
    bias = w["L1_attn_in_proj_b"][order]
    conv = np.concatenate([w["L1_attn_conv_w"][DIM:], w["L1_attn_conv_w"][:DIM]])

    seq, pos = np.divmod(np.arange(R), SEQ)
    same = seq[:, None] == seq[None, :]
    later = same & (pos[:, None] > pos[None, :])
    upto = pos[:, None] <= np.arange(SEQ)[None, :]
    causal = same & (pos[:, None] <= pos[None, :])
    odd = np.stack([pos % 2 == 1, pos % 2 == 0], axis=1)
    level_of = np.zeros((LEVELS, SPT, SEQ // 2, SPT, SEQ), bool)
    for m in range(SEQ // 2):
        for key in range(2 * m + 2):
            row = key - 2 * m if key >= 2 * m else (key ^ (2 * m)).bit_length()
            for b in range(SPT):
                level_of[row, b, m, b, key] = True
    flat = {
        "later": later, "upto": upto, "causal": causal, "block_of": same, "odd": odd,
        "level_of": np.stack([level_of, level_of]).reshape(LROWS, SEQ // 2, R),
    }
    laid = {
        "patches": tokens.reshape(NT, R, PD),
        "proj": w["L0_tok_W_proj"],
        "proj_bias": w["L0_tok_b_proj"].reshape(1, E),
        "ln1_g": w["L0_tok_ln1_g"].reshape(KP, 128).T,
        "ln1_b": w["L0_tok_ln1_b"].reshape(KP, 128).T,
        "ln2_g": w["L0_tok_ln2_g"],
        "ln2_b": w["L0_tok_ln2_b"],
        "inner_cls": w["L0_tok_cls_token"].reshape(1, E),
        "positions": w["L0_tok_pos_emb"].reshape(PATCHES + 1, E),
        "outer_cls": w["cls_tok"].reshape(1, E),
        "wqT": w["L0_attn_wq"].T,
        "wkT": w["L0_attn_wk"].T,
        "wvT": w["L0_attn_wv"].T,
        "woT": w["L0_attn_wo"].T,
        "gate0": w["L0_ffn_W_gate"],
        "w_in": w["L0_ffn_W_in"],
        "b_in": w["L0_ffn_b_in"].reshape(EXPERTS, -1, 128).transpose(2, 0, 1),
        "w_out": w["L0_ffn_W_out"],
        "b_out": w["L0_ffn_b_out"],
        "in_proj": w["L1_attn_in_proj_w"][order].T,
        "fm_bias": bias[:FM_TILES * 128].reshape(FM_TILES, 128).T,
        "dtl_bias": bias[FM_TILES * 128:],
        "taps": conv.reshape(CONV_TILES, 128, TAPS).transpose(1, 0, 2),
        "dt_bias": w["L1_attn_dt_bias"],
        "factor": w["L1_attn_L"][:, [1, 0] + list(range(2, LEVELS))].T.reshape(-1),
        "a_log": w["L1_attn_A_log"],
        "skip": np.repeat(w["L1_attn_D"], HD).reshape(Z_TILES, 128).T,
        "norm_w": w["L1_attn_norm_w"].reshape(Z_TILES, 128).T,
        "out_proj": w["L1_attn_out_proj_w"].T,
        "out_bias": w["L1_attn_out_proj_b"],
        "gate1": w["L1_ffn_gate_w"].T,
        "wg": w["L1_ffn_wg"],
        "wu": w["L1_ffn_wu"],
        "wd": w["L1_ffn_wd"],
        "swg": w["L1_ffn_swg"],
        "swu": w["L1_ffn_swu"],
        "swd": w["L1_ffn_swd"],
    }
    laid |= {k: np.where(v, np.float32(1), np.float32(0)) for k, v in flat.items()}
    return {k: np.ascontiguousarray(v) for k, v in laid.items()}


def kernel(**inputs):
    import concourse.bacc as bacc
    from concourse.bass_utils import run_bass_kernel_spmd

    nc = bacc.Bacc("TRN2", target_bir_lowering=False, num_devices=1)
    laid = lay_out(inputs)
    io = {k: nc.dram_tensor(f"in_{k}", v.shape, mybir.dt.from_np(v.dtype), kind="ExternalInput").ap() for k, v in laid.items()}
    out = nc.dram_tensor("out", (BATCH * SEQ, E), F32, kind="ExternalOutput").ap()
    tower(nc, io, out)
    r = run_bass_kernel_spmd(nc, [{f"in_{k}": v for k, v in laid.items()}], core_ids=[0])
    return r.results[0]["out"].reshape(BATCH, SEQ, E)
```
